# Optimizing a Trainium2 kernel written in Bass

```python
import numpy as np
import jax
import jax.numpy as jnp

def _softmax(x, axis=-1):
    return jax.nn.softmax(x, axis=axis)

def _gelu(x):
    return jax.nn.gelu(x, approximate=True)

def _silu(x):
    return jax.nn.silu(x)

def _sigmoid(x):
    return jax.nn.sigmoid(x)

def _layernorm(x, axis=-1, eps=1e-05):
    m = jnp.mean(x, axis=axis, keepdims=True)
    v = jnp.var(x, axis=axis, keepdims=True)
    return (x - m) / jnp.sqrt(v + eps)

def _scatter_add(tgt, idx, src, axis=0):
    return tgt.at[idx].add(src)

def _segment_sum(src, seg, n):
    return jax.ops.segment_sum(src, seg, n)
kernel_name = 'mk_adaln_d1_jaxref_r4_a7815e'

def setup_inputs(seed: int=0):
    np.random.seed(seed)
    _w = jnp.asarray

    def _L0_attn_setup():
        import jax, jax.numpy as jnp
        import numpy as np
        D_MODEL = 256
        EXPAND = 2
        D_INNER = EXPAND * D_MODEL
        HEADDIM = 64
        NHEADS = D_INNER // HEADDIM
        D_STATE = 128
        D_CONV = 4
        NGROUPS = 1
        D_IN_PROJ = 2 * D_INNER + 2 * NGROUPS * D_STATE + NHEADS
        CONV_DIM = D_INNER + 2 * NGROUPS * D_STATE
        BATCH, SEQLEN = (4, 512)
        EPS = 1e-05

        def _mamba2(x, W_in, conv_w, conv_b, dt_bias, A_log, D_skip, rms_w, W_out):
            b, l, _ = x.shape
            zxbcdt = x @ W_in
            z = zxbcdt[..., :D_INNER]
            xBC = zxbcdt[..., D_INNER:D_INNER + CONV_DIM]
            dt = zxbcdt[..., D_INNER + CONV_DIM:]
            dt = jax.nn.softplus(dt + dt_bias)
            xBC_cl = jnp.transpose(xBC, (0, 2, 1))
            conv = jax.lax.conv_general_dilated(xBC_cl, conv_w[:, None, :], window_strides=(1,), padding=[(D_CONV - 1, 0)], feature_group_count=CONV_DIM, dimension_numbers=('NCL', 'OIL', 'NCL'))
            xBC = jax.nn.silu(jnp.transpose(conv, (0, 2, 1)) + conv_b)
            xs = xBC[..., :D_INNER]
            Bm = xBC[..., D_INNER:D_INNER + D_STATE]
            Cm = xBC[..., D_INNER + D_STATE:]
            A = -jnp.exp(A_log)
            xh = xs.reshape(b, l, NHEADS, HEADDIM)
            dt_t = jnp.transpose(dt, (1, 0, 2))
            x_t = jnp.transpose(xh, (1, 0, 2, 3))
            B_t = jnp.transpose(Bm, (1, 0, 2))
            C_t = jnp.transpose(Cm, (1, 0, 2))

            def step(h, inp):
                dti, xi, Bi, Ci = inp
                dA = jnp.exp(dti * A)
                h = h * dA[:, :, None, None] + dti[:, :, None, None] * xi[..., None] * Bi[:, None, None, :]
                y = jnp.einsum('bhpn,bn->bhp', h, Ci)
                return (h, y)
            h0 = jnp.zeros((b, NHEADS, HEADDIM, D_STATE), x.dtype)
            _, ys = jax.lax.scan(step, h0, (dt_t, x_t, B_t, C_t))
            y = jnp.transpose(ys, (1, 0, 2, 3)) + D_skip[None, None, :, None] * xh
            y = y.reshape(b, l, D_INNER)
            y = y * jax.nn.silu(z)
            y = y * jax.lax.rsqrt(jnp.mean(y * y, axis=-1, keepdims=True) + EPS) * rms_w
            return y @ W_out
        key = jax.random.key(seed)
        ks = jax.random.split(key, 8)
        sc = lambda k, shape, s=0.02: jax.random.normal(k, shape, jnp.float32) * s
        x = jax.random.normal(ks[0], (BATCH, SEQLEN, D_MODEL), jnp.float32)
        W_in = sc(ks[1], (D_MODEL, D_IN_PROJ))
        conv_w = sc(ks[2], (CONV_DIM, D_CONV), 0.1)
        conv_b = jnp.zeros((CONV_DIM,), jnp.float32)
        dt = jax.random.uniform(ks[3], (NHEADS,), jnp.float32, 0.001, 0.1)
        dt_bias = jnp.log(jnp.expm1(dt))
        A_log = jnp.log(jax.random.uniform(ks[4], (NHEADS,), jnp.float32, 1.0, 16.0))
        D_skip = jnp.ones((NHEADS,), jnp.float32)
        rms_w = jnp.ones((D_INNER,), jnp.float32)
        W_out = sc(ks[5], (D_INNER, D_MODEL))
        glu_w = sc(ks[6], (D_MODEL, 2 * D_MODEL))
        glu_b = jnp.zeros((2 * D_MODEL,), jnp.float32)
        ln_w = jnp.ones((D_MODEL,), jnp.float32)
        ln_b = jnp.zeros((D_MODEL,), jnp.float32)
        return dict(x=x, W_in=W_in, conv_w=conv_w, conv_b=conv_b, dt_bias=dt_bias, A_log=A_log, D_skip=D_skip, rms_w=rms_w, W_out=W_out, glu_w=glu_w, glu_b=glu_b, ln_w=ln_w, ln_b=ln_b)
    _L0_attn_in = _L0_attn_setup()

    def _L0_ffn_setup():
        import jax, jax.numpy as jnp
        import numpy as np
        from jax import lax
        DIM = 256
        INTER = 128
        N_EXPERTS = 16
        TOPK = 4
        ROUTE_SCALE = 2.5
        VOCAB = 8000

        def _silu_and_mul(gu):
            gate, up = jnp.split(gu, 2, axis=-1)
            return jax.nn.silu(gate) * up
        key = jax.random.key(seed)
        ks = jax.random.split(key, 8)
        x = jax.random.normal(ks[0], (2, 128, DIM), dtype=jnp.float32)
        input_ids = jax.random.randint(ks[1], (2, 128), 0, VOCAB)
        s = 0.02
        gate_w = jax.random.normal(ks[2], (N_EXPERTS, DIM), dtype=jnp.float32) * s
        gate_b = jax.random.normal(ks[3], (N_EXPERTS,), dtype=jnp.float32) * s
        w13 = jax.random.normal(ks[4], (N_EXPERTS, 2 * INTER, DIM), dtype=jnp.float32) * s
        w2 = jax.random.normal(ks[5], (N_EXPERTS, DIM, INTER), dtype=jnp.float32) * s
        w13_s = jax.random.normal(ks[6], (2 * INTER, DIM), dtype=jnp.float32) * s
        w2_s = jax.random.normal(ks[7], (DIM, INTER), dtype=jnp.float32) * s
        return {'x': x, 'input_ids': input_ids, 'gate_w': gate_w, 'gate_b': gate_b, 'w13': w13, 'w2': w2, 'w13_s': w13_s, 'w2_s': w2_s}
    _L0_ffn_in = _L0_ffn_setup()
    _L0_c = _w((lambda *s: np.random.randn(*s).astype(np.float32) * 0.05)(2, 256))
    _L0_wmod = _w((lambda *s: np.random.randn(*s).astype(np.float32) * 0.05)(256, 6 * 256) * 256 ** (-0.5))
    _d = {'L0_attn_x': _L0_attn_in['x'], 'L0_attn_W_in': _L0_attn_in['W_in'], 'L0_attn_conv_w': _L0_attn_in['conv_w'], 'L0_attn_conv_b': _L0_attn_in['conv_b'], 'L0_attn_dt_bias': _L0_attn_in['dt_bias'], 'L0_attn_A_log': _L0_attn_in['A_log'], 'L0_attn_D_skip': _L0_attn_in['D_skip'], 'L0_attn_rms_w': _L0_attn_in['rms_w'], 'L0_attn_W_out': _L0_attn_in['W_out'], 'L0_attn_glu_w': _L0_attn_in['glu_w'], 'L0_attn_glu_b': _L0_attn_in['glu_b'], 'L0_attn_ln_w': _L0_attn_in['ln_w'], 'L0_attn_ln_b': _L0_attn_in['ln_b'], 'L0_ffn_input_ids': _L0_ffn_in['input_ids'], 'L0_ffn_gate_w': _L0_ffn_in['gate_w'], 'L0_ffn_gate_b': _L0_ffn_in['gate_b'], 'L0_ffn_w13': _L0_ffn_in['w13'], 'L0_ffn_w2': _L0_ffn_in['w2'], 'L0_ffn_w13_s': _L0_ffn_in['w13_s'], 'L0_ffn_w2_s': _L0_ffn_in['w2_s'], 'L0_c': _L0_c, 'L0_wmod': _L0_wmod}
    _x0 = _d['L0_attn_x']
    _d['L0_attn_x'] = jax.random.normal(jax.random.fold_in(jax.random.key(seed), 1), (2, 4096, 256), dtype=_x0.dtype)
    del _x0
    return _d

def reference(L0_attn_x, L0_attn_W_in, L0_attn_conv_w, L0_attn_conv_b, L0_attn_dt_bias, L0_attn_A_log, L0_attn_D_skip, L0_attn_rms_w, L0_attn_W_out, L0_attn_glu_w, L0_attn_glu_b, L0_attn_ln_w, L0_attn_ln_b, L0_ffn_input_ids, L0_ffn_gate_w, L0_ffn_gate_b, L0_ffn_w13, L0_ffn_w2, L0_ffn_w13_s, L0_ffn_w2_s, L0_c, L0_wmod):

    def _L0_attn_ref(x, W_in, conv_w, conv_b, dt_bias, A_log, D_skip, rms_w, W_out, glu_w, glu_b, ln_w, ln_b):
        import jax, jax.numpy as jnp
        import numpy as np
        D_MODEL = 256
        EXPAND = 2
        D_INNER = EXPAND * D_MODEL
        HEADDIM = 64
        NHEADS = D_INNER // HEADDIM
        D_STATE = 128
        D_CONV = 4
        NGROUPS = 1
        D_IN_PROJ = 2 * D_INNER + 2 * NGROUPS * D_STATE + NHEADS
        CONV_DIM = D_INNER + 2 * NGROUPS * D_STATE
        BATCH, SEQLEN = (4, 512)
        EPS = 1e-05

        def _mamba2(x, W_in, conv_w, conv_b, dt_bias, A_log, D_skip, rms_w, W_out):
            b, l, _ = x.shape
            zxbcdt = x @ W_in
            z = zxbcdt[..., :D_INNER]
            xBC = zxbcdt[..., D_INNER:D_INNER + CONV_DIM]
            dt = zxbcdt[..., D_INNER + CONV_DIM:]
            dt = jax.nn.softplus(dt + dt_bias)
            xBC_cl = jnp.transpose(xBC, (0, 2, 1))
            conv = jax.lax.conv_general_dilated(xBC_cl, conv_w[:, None, :], window_strides=(1,), padding=[(D_CONV - 1, 0)], feature_group_count=CONV_DIM, dimension_numbers=('NCL', 'OIL', 'NCL'))
            xBC = jax.nn.silu(jnp.transpose(conv, (0, 2, 1)) + conv_b)
            xs = xBC[..., :D_INNER]
            Bm = xBC[..., D_INNER:D_INNER + D_STATE]
            Cm = xBC[..., D_INNER + D_STATE:]
            A = -jnp.exp(A_log)
            xh = xs.reshape(b, l, NHEADS, HEADDIM)
            dt_t = jnp.transpose(dt, (1, 0, 2))
            x_t = jnp.transpose(xh, (1, 0, 2, 3))
            B_t = jnp.transpose(Bm, (1, 0, 2))
            C_t = jnp.transpose(Cm, (1, 0, 2))

            def step(h, inp):
                dti, xi, Bi, Ci = inp
                dA = jnp.exp(dti * A)
                h = h * dA[:, :, None, None] + dti[:, :, None, None] * xi[..., None] * Bi[:, None, None, :]
                y = jnp.einsum('bhpn,bn->bhp', h, Ci)
                return (h, y)
            h0 = jnp.zeros((b, NHEADS, HEADDIM, D_STATE), x.dtype)
            _, ys = jax.lax.scan(step, h0, (dt_t, x_t, B_t, C_t))
            y = jnp.transpose(ys, (1, 0, 2, 3)) + D_skip[None, None, :, None] * xh
            y = y.reshape(b, l, D_INNER)
            y = y * jax.nn.silu(z)
            y = y * jax.lax.rsqrt(jnp.mean(y * y, axis=-1, keepdims=True) + EPS) * rms_w
            return y @ W_out
        y = _mamba2(x, W_in, conv_w, conv_b, dt_bias, A_log, D_skip, rms_w, W_out)
        y = y + x
        g = y @ glu_w + glu_b
        a, gate = (g[..., :D_MODEL], g[..., D_MODEL:])
        y = y + a * jax.nn.sigmoid(gate)
        mu = jnp.mean(y, axis=-1, keepdims=True)
        var = jnp.mean((y - mu) ** 2, axis=-1, keepdims=True)
        y = (y - mu) * jax.lax.rsqrt(var + EPS) * ln_w + ln_b
        return y

    def _L0_ffn_ref(x, input_ids, gate_w, gate_b, w13, w2, w13_s, w2_s):
        import jax, jax.numpy as jnp
        import numpy as np
        from jax import lax
        DIM = 256
        INTER = 128
        N_EXPERTS = 16
        TOPK = 4
        ROUTE_SCALE = 2.5
        VOCAB = 8000

        def _silu_and_mul(gu):
            gate, up = jnp.split(gu, 2, axis=-1)
            return jax.nn.silu(gate) * up
        B, S, D = x.shape
        xt = x.reshape(-1, D)
        T = xt.shape[0]
        scores = jax.nn.sigmoid(xt.astype(jnp.float32) @ gate_w.T)
        biased = scores + gate_b
        _, idx = lax.top_k(biased, TOPK)
        w = jnp.take_along_axis(scores, idx, axis=-1)
        w = w / jnp.sum(w, axis=-1, keepdims=True)
        w = w * ROUTE_SCALE
        comb = jnp.zeros((T, N_EXPERTS), jnp.float32)
        comb = comb.at[jnp.arange(T)[:, None], idx].add(w)
        comb = comb.astype(x.dtype)

        def expert_body(y, args):
            w13_e, w2_e, c_e = args
            h = _silu_and_mul(xt @ w13_e.T)
            return (y + c_e[:, None] * (h @ w2_e.T), None)
        y, _ = lax.scan(expert_body, jnp.zeros_like(xt), (w13, w2, comb.T))
        y = y + _silu_and_mul(xt @ w13_s.T) @ w2_s.T
        return y.astype(x.dtype).reshape(B, S, D)
    x = L0_attn_x
    mod = (_silu(L0_c) @ L0_wmod).reshape(L0_c.shape[0], 6, 1, -1)
    sa, ca, ga, sb, cb, gb = (mod[:, 0], mod[:, 1], mod[:, 2], mod[:, 3], mod[:, 4], mod[:, 5])
    ga = (2 * (ga >= 0) - 1) * jnp.maximum(jnp.abs(ga), 0.25)
    gb = (2 * (gb >= 0) - 1) * jnp.maximum(jnp.abs(gb), 0.25)
    h = _layernorm(x, axis=-1) * (1 + ca) + sa
    x = x + ga * _L0_attn_ref(h, L0_attn_W_in, L0_attn_conv_w, L0_attn_conv_b, L0_attn_dt_bias, L0_attn_A_log, L0_attn_D_skip, L0_attn_rms_w, L0_attn_W_out, L0_attn_glu_w, L0_attn_glu_b, L0_attn_ln_w, L0_attn_ln_b)
    h = _layernorm(x, axis=-1) * (1 + cb) + sb
    x = x + gb * _L0_ffn_ref(h, L0_ffn_input_ids, L0_ffn_gate_w, L0_ffn_gate_b, L0_ffn_w13, L0_ffn_w2, L0_ffn_w13_s, L0_ffn_w2_s)
    return x

_drawn_inputs = setup_inputs


def setup_inputs(seed=0):
    import zlib

    import numpy as np

    out = dict(_drawn_inputs(seed))
    spreads = {'L0_attn_conv_b': (0.0, 0.1),
     'L0_attn_D_skip': (1.0, 0.6),
     'L0_attn_rms_w': (1.0, 0.6),
     'L0_attn_glu_b': (0.0, 0.694),
     'L0_attn_ln_w': (1.0, 0.2),
     'L0_attn_ln_b': (0.0, 0.318)}
    factors = {'L0_attn_dt_bias': 8.0,
     'L0_attn_A_log': 8.0,
     'L0_ffn_gate_w': 8.0,
     'L0_ffn_gate_b': 8.0,
     'L0_ffn_w13': 8.0,
     'L0_ffn_w2': 8.0,
     'L0_ffn_w13_s': 8.0,
     'L0_ffn_w2_s': 8.0}
    for name, (base, spread) in spreads.items():
        noise = np.random.default_rng([zlib.crc32(name.encode()), seed]).standard_normal(out[name].shape)
        drawn = base * np.exp(spread * noise) if base else spread * noise
        out[name] = jnp.asarray(drawn.astype(out[name].dtype))
    for name, factor in factors.items():
        out[name] = (out[name] * factor).astype(out[name].dtype)
    return out
```

```python
from contextlib import ExitStack

import numpy as np
import concourse.bass as bass
from concourse import mybir

ALU = mybir.AluOpType
ACT = mybir.ActivationFunctionType
F32 = mybir.dt.float32
F32R = mybir.dt.float32r

P = 128
NB = 2
SEQ = 4096
D = 256
DI = 512
H = 8
HD = DI // H
NS = 128
CONV = DI + 2 * NS
TAPS = 4
KD = D // P
KI = DI // P
MC = CONV // P
IN_COLS = 2 * DI + 2 * NS + H
EPS = 1e-5
NE = 16
INTER = 128
TOPK = 4
ROUTE_SCALE = 2.5

GROUP = 256
CH = GROUP // P
STEPS = SEQ // GROUP
MGROUP = 512
MT = MGROUP // P
MSTEPS = SEQ // MGROUP
DT_LINKS = 16
SERIES = [1.0 / (2 * n + 1) for n in range(8, -1, -1)]


def build(nc, t, x2_dram, out):
    ctx = ExitStack()

    def sb(name, shape, dt=F32):
        return ctx.enter_context(nc.sbuf_tensor(name, shape, dt))

    taken = []

    def sem(name):
        taken.append(nc.alloc_semaphore(name=name))
        return taken[-1]

    def prime(counts):
        with nc.Block() as block:
            @block.sync
            def _(sp):
                for semaphore, per_step in counts:
                    sp.sem_inc(semaphore, per_step)

    def clear_semaphores():
        nc.all_engine_barrier()
        nc.clear_and_free_semaphores(taken)
        nc.all_engine_barrier()
        taken.clear()

    with ctx:
        bank = [ctx.enter_context(nc.psum_tensor(f"bank{n}", [P, 512], F32)) for n in range(8)]
        mod = [sb(f"mod{b}", [P, 4, KD]) for b in range(NB)]
        gate_b_row = [sb(f"gb_row{b}", [P, D]) for b in range(NB)]
        ident = sb("ident", [P, P])
        minus_half = sb("minus_half", [P, MT])
        gate_ln = sb("gate_ln", [P, NB, 2, D])
        setup(nc, sem, t, mod, gate_b_row, gate_ln, ident, minus_half, bank)
        mixer(nc, sem, prime, t, mod, gate_ln, ident, minus_half, bank, x2_dram)
        clear_semaphores()
        experts(nc, sem, prime, t, mod, gate_b_row, ident, minus_half, bank, x2_dram, out)


def split3(pe, out, a_hi, a_lo, b_hi, b_lo, start, stop):
    pe.matmul(out, a_hi, b_hi, start=start, stop=False, skip_group_check=True)
    pe.matmul(out, a_hi, b_lo, start=False, stop=False, skip_group_check=True)
    return pe.matmul(out, a_lo, b_hi, start=False, stop=stop, skip_group_check=True)


def stand_alone(eng, counter):
    eng.sem_inc(counter, 1)


def setup(nc, sem, t, mod, gate_b_row, gate_ln, ident, minus_half, bank):
    with ExitStack() as ctx:
        c_col = ctx.enter_context(nc.sbuf_tensor("c_col", [P, KD, NB], F32))
        c_silu = ctx.enter_context(nc.sbuf_tensor("c_silu", [P, KD, NB], F32))
        c_wide = ctx.enter_context(nc.sbuf_tensor("c_wide", [P, KD, NB, P], F32))
        wmod = ctx.enter_context(nc.sbuf_tensor("wmod", [P, KD, 6 * D], F32))
        pos = ctx.enter_context(nc.sbuf_tensor("pos", [P, 2, D], F32))
        mag = ctx.enter_context(nc.sbuf_tensor("mag", [P, 2, D], F32))
        lnw = ctx.enter_context(nc.sbuf_tensor("lnw", [P, 2, D], F32))
        loaded = sem("mod_loaded")
        silu_done = sem("c_silu_done")
        wide_done = sem("c_wide_done")
        cols_done = sem("mod_cols_done")
        rows_done = sem("mod_rows_done")
        link = sem("mod_link")
        with nc.Block() as block:
            @block.sync
            def _(sp):
                sp.dma_start(c_col[:, :, :], t["c_col"]).then_inc(loaded, 16)
                sp.dma_start(wmod[:, :, :], t["wmod"]).then_inc(loaded, 16)
                sp.dma_start(ident[:, :], t["ident"]).then_inc(loaded, 16)
                sp.dma_start(lnw[:, :, :], t["ln_wb"]).then_inc(loaded, 16)

            @block.gpsimd
            def _(pool):
                pool.memset(minus_half[:, :], -0.5)

            @block.scalar
            def _(act):
                act.wait_ge(loaded, 64)
                act.activation(c_silu[:, :, :], c_col[:, :, :], ACT.Silu).then_inc(silu_done, 1)
                act.wait_ge(silu_done, 1)
                act.activation(c_wide[:, :, :, :], c_silu[:, :, :].unsqueeze(3).to_broadcast([P, KD, NB, P]),
                               ACT.Copy).then_inc(wide_done, 1)

            @block.tensor
            def _(pe):
                pe.wait_ge(wide_done, 1)
                for b in range(NB):
                    for n, chunk in enumerate((1, 0, 4, 3)):
                        for m in range(KD):
                            for k in range(KD):
                                last = pe.matmul(bank[b][:, (n * KD + m) * 2:(n * KD + m) * 2 + 2],
                                                 wmod[:, k, chunk * D + m * P:chunk * D + (m + 1) * P],
                                                 c_silu[:, k, :], start=(k == 0), stop=(k == KD - 1))
                    last.then_inc(cols_done, 1)
                    for n, chunk in enumerate((2, 5)):
                        for k in range(KD):
                            last = pe.matmul(bank[2 + b][:, n * D:(n + 1) * D], c_wide[:, k, b, :],
                                             wmod[:, k, chunk * D:(chunk + 1) * D],
                                             start=(k == 0), stop=(k == KD - 1))
                    last.then_inc(rows_done, 1)

            @block.vector
            def _(dve):
                n = [0]

                def then_wait(ins):
                    n[0] += 1
                    ins.then_inc(link, 1)
                    dve.wait_ge(link, n[0])

                for b in range(NB):
                    dve.wait_ge(cols_done, b + 1)
                    col = bank[b][:, 0:8 * KD].rearrange("p (n m b) -> p n m b", n=4, b=NB)[:, :, :, b]
                    for j in range(2):
                        then_wait(dve.tensor_scalar(mod[b][:, 2 * j, :], col[:, 2 * j, :], 1.0, None, ALU.add))
                        then_wait(dve.tensor_copy(mod[b][:, 2 * j + 1, :], col[:, 2 * j + 1, :]))
                dve.wait_ge(loaded, 64)
                for b in range(NB):
                    dve.wait_ge(rows_done, b + 1)
                    g = bank[2 + b][:, :].rearrange("p (n d) -> p n d", n=2)
                    dve.tensor_scalar(pos[:, :, :], g, 0.0, 2.0, ALU.is_ge, ALU.mult)
                    then_wait(dve.tensor_scalar(mag[:, :, :], g, -1.0, None, ALU.mult))
                    then_wait(dve.tensor_tensor(mag[:, :, :], mag[:, :, :], g, ALU.max))
                    then_wait(dve.tensor_scalar(mag[:, :, :], mag[:, :, :], 0.25, None, ALU.max))
                    then_wait(dve.scalar_tensor_tensor(pos[:, :, :], pos[:, :, :], -1.0, mag[:, :, :],
                                                       ALU.add, ALU.mult))
                    dve.tensor_copy(gate_b_row[b][:, :], pos[:, 1, :])
                    for n2 in range(2):
                        last = dve.tensor_tensor(gate_ln[:, b, n2, :], pos[:, 0, :], lnw[:, n2, :], ALU.mult)
                    then_wait(last)


def mixer(nc, sem, prime, t, mod, gate_ln, ident, minus_half, bank, x2_dram):
    with ExitStack() as ctx:
        def sb(name, shape, dt=F32):
            return ctx.enter_context(nc.sbuf_tensor(name, shape, dt))

        def both(name, shape, dt=F32):
            return [sb(f"{name}{b}", shape, dt) for b in range(NB)]

        counts = []

        def sems(name, per_step=None):
            pair = [sem(f"{name}{b}") for b in range(NB)]
            if per_step:
                counts.extend((s, per_step) for s in pair)
            return pair

        win = [sb(f"win_{h}", [P, KD, IN_COLS], F32R) for h in ("hi", "lo")]
        wout = [sb(f"wout_{h}", [P, KI, D], F32R) for h in ("hi", "lo")]
        wglu = [sb(f"wglu_{h}", [P, KD, 2 * D], F32R) for h in ("hi", "lo")]
        upto = sb("upto", [P, P])
        after = sb("after", [P, P])
        ones = sb("ones", [P, P])
        convw = sb("convw", [P, MC, TAPS])
        convb = sb("convb", [P, MC])
        dtb = sb("dtb", [P, CH, H])
        negA = sb("negA", [P, CH, H])
        dskip = sb("dskip", [P, DI])
        glub = sb("glub", [P, 2 * KD])
        xt = both("xt", [P, CH, D])
        xr = both("xr", [P, CH, D])
        st = both("st", [P, CH, 6])
        mv = both("mv", [P, CH, 2])
        rs = both("rs", [P, CH])
        xn = both("xn", [P, CH, D])
        hT = both("hT", [P, KD, GROUP])
        hTh = both("hTh", [P, KD, GROUP], F32R)
        hTl = both("hTl", [P, KD, GROUP], F32R)
        zs = both("zs", [P, CH, DI])
        xc = both("xc", [P, MC, TAPS - 1 + GROUP])
        cv = both("cv", [P, MC, GROUP])
        dts = both("dts", [P, 8, CH, H])
        ex = both("ex", [P, 3, CH, H])
        xtok = both("xtok", [P, CH, DI])
        xdt = both("xdt", [P, CH, DI])
        xend = both("xend", [P, DI])
        btok = both("btok", [P, CH, NS])
        au = both("au", [P, H, P])
        dec = both("dec", [P, H, P])
        gm = both("gm", [P, CH, P])
        state = both("state", [P, DI])
        yy = both("yy", [P, CH, DI])
        ss = both("ss", [P, CH])
        rr = both("rr", [P, CH])
        yTh = both("yTh", [P, KI, GROUP], F32R)
        yTl = both("yTl", [P, KI, GROUP], F32R)
        y1 = both("y1", [P, KD, GROUP])
        y1h = both("y1h", [P, KD, GROUP], F32R)
        y1l = both("y1l", [P, KD, GROUP], F32R)
        sg = both("sg", [P, KD, GROUP])
        xo = both("xo", [P, CH, D])

        w_in, w_ready, w_hi, link = sems("w_in"), sem("w_ready"), sem("w_hi"), sem("w_link")
        with nc.Block() as block:
            raws = [cv[b][:, :, :].rearrange("p a b -> p (a b)") for b in range(NB)]
            pieces = []
            for k in range(KD):
                pieces.append((t["W_in"][:, k, :], IN_COLS, win[0][:, k, :], win[1][:, k, :]))
            pieces.append((t["W_out"], KI * D, wout[0][:, :, :].rearrange("p a b -> p (a b)"),
                           wout[1][:, :, :].rearrange("p a b -> p (a b)")))
            pieces.append((t["glu_w"], KD * 2 * D, wglu[0][:, :, :].rearrange("p a b -> p (a b)"),
                           wglu[1][:, :, :].rearrange("p a b -> p (a b)")))
            OUT_PIECE = 2
            consts = [(upto, "upto"), (after, "after"), (ones, "ones"), (convw, "conv_w"), (convb, "conv_b"),
                      (dtb, "dt_bias"), (negA, "A_log"), (dskip, "D_skip"), (glub, "glu_b"),
                      ]
            c_in = sem("c_in")
            rms = sg[0][:, 0, 0:KI]
            CONSTS = len(consts) + 1

            @block.sync
            def _(sp):
                for n, (src, cols, _, _) in enumerate(pieces):
                    if n >= 2:
                        sp.wait_ge(w_ready, n - 1)
                    sp.dma_start(raws[n % 2][:, 0:cols], src).then_inc(w_in[n % 2], 16)
                    if n == 1:
                        for dst, name in consts:
                            sp.dma_start(dst[tuple(slice(None) for _ in dst.shape)], t[name]).then_inc(c_in, 16)
                        sp.dma_start(rms, t["rms_w"]).then_inc(c_in, 16)
                        sp.wait_ge(c_in, 16 * CONSTS)

            @block.vector
            def _(dve):
                for n, (_, cols, hi, lo) in enumerate(pieces):
                    dve.wait_ge(w_in[n % 2], 16 * (n // 2 + 1))
                    raw = raws[n % 2][:, 0:cols]
                    if n == OUT_PIECE:
                        dve.wait_ge(c_in, 16 * CONSTS)
                        for k in range(KI):
                            last = dve.tensor_scalar(raw[:, k * D:(k + 1) * D], raw[:, k * D:(k + 1) * D],
                                                     rms[:, k:k + 1], None, ALU.mult)
                        last.then_inc(link, 1)
                        dve.wait_ge(link, 1)
                    dve.tensor_copy(hi, raw).then_inc(w_hi, 1)
                    dve.wait_ge(w_hi, n + 1)
                    dve.tensor_tensor(lo, raw, hi.bitcast(F32), ALU.subtract).then_inc(w_ready, 1)
                dve.tensor_scalar(glub[:, KD:], glub[:, KD:], 0.5, None, ALU.mult)

            @block.scalar
            def _(act):
                act.wait_ge(c_in, 16 * CONSTS)
                act.activation(negA[:, :, :], negA[:, :, :], ACT.Exp)

            @block.gpsimd
            def _(pool):
                for b in range(NB):
                    pool.memset(state[b][:, :], 0.0)
                    pool.memset(xc[b][:, :, GROUP:GROUP + TAPS - 1], 0.0)

        x_in = sems("x_in", 16)
        xr_in = sems("xr_in", 16)
        ln1 = sems("ln1", 3)
        root1 = sems("root1", 1)
        xn_done = sems("xn_done", 1)
        xnT_ps = sems("xnT_ps", 1)
        hT_done = sems("hT_done", 1)
        hTh_done = sems("hTh_done", 1)
        hTl_done = sems("hTl_done", 1)
        z_ps = sems("z_ps", CH)
        dt_ps = sems("dt_ps", 1)
        xbc_ps = sems("xbc_ps", 3)
        zs_done = sems("zs_done", CH)
        halo_done = sems("halo_done", 1)
        xc_done = sems("xc_done", 3)
        tap_done = sems("tap_done", MC * TAPS)
        xs_done = sems("xs_done", 3)
        dt_abs = sems("dt_abs", 1)
        dt_exp = sems("dt_exp", 1)
        dt_link = sems("dt_link", DT_LINKS)
        a_done = sems("a_done", 1)
        sums_ps = sems("sums_ps", 1)
        ex_done = sems("ex_done", 1)
        wend_done = sems("wend_done", 1)
        xT_ps = sems("xT_ps", CH)
        btg_ps = sems("btg_ps", 1)
        xtok_done = sems("xtok_done", CH)
        xdt_done = sems("xdt_done", CH)
        btok_done = sems("btok_done", 1)
        gm_done = sems("gm_done", 1)
        au_done = sems("au_done", CH)
        dec_ps = sems("dec_ps", CH)
        dec_done = sems("dec_done", CH)
        w_done = sems("w_done", CH)
        xend_done = sems("xend_done", CH)
        yin_ps = sems("yin_ps", CH)
        yst_ps = sems("yst_ps", CH)
        add_ps = sems("add_ps", CH)
        sdec_done = sems("sdec_done", CH)
        st_done = sems("st_done", CH)
        y1s_done = sems("y1s_done", CH)
        y2s_done = sems("y2s_done", CH)
        xd_done = sems("xd_done", CH)
        y3_done = sems("y3_done", CH)
        y4_done = sems("y4_done", CH)
        sq_done = sems("sq_done", CH)
        ms_done = sems("ms_done", CH)
        rr_done = sems("rr_done", CH)
        yn_done = sems("yn_done", CH)
        yT_ps = sems("yT_ps", CH)
        yTh_done = sems("yTh_done", CH)
        yTl_done = sems("yTl_done", CH)
        o_ps = sems("o_ps", 1)
        y1_done = sems("y1_done", 1)
        y1h_done = sems("y1h_done", 1)
        y1l_done = sems("y1l_done", 1)
        glu_ps = sems("glu_ps", 1)
        tg_done = sems("tg_done", 1)
        sg_done = sems("sg_done", 1)
        ag_done = sems("ag_done", 1)
        y2_done = sems("y2_done", 1)
        y2T_ps = sems("y2T_ps", 1)
        ln2 = sems("ln2", 3)
        root2 = sems("root2", 1)
        yo_done = sems("yo_done", 1)
        xo_link = sems("xo_link", 2)
        xo_done = sems("xo_done", 1)
        stored = sems("x2_stored", 16)

        prime(counts)
        held_dve, held_pool = sem("held_dve"), sem("held_pool")

        def Q(b, n):
            return bank[4 * b + n]

        def wide(ap, shape):
            return ap.to_broadcast(shape)

        def rows(b, i):
            return bass.ds(b * SEQ + i * GROUP, GROUP)

        with nc.Block() as block:
            @block.sync
            def _(sp):
                def step(dram, b, i):
                    return dram[b, bass.ds(i - 1, 1)].rearrange("o p c d -> p (o c) d")

                def load_x(b, i):
                    sp.dma_start(xt[b][:, :, :], step(t["x"], b, i)).then_inc(x_in[b], 16)

                def load_again(b, i):
                    sp.wait_ge(xo_done[b], i)
                    sp.dma_start(xr[b][:, :, :], step(t["x"], b, i)).then_inc(xr_in[b], 16)

                def store(b, i):
                    sp.wait_ge(xo_done[b], i + 1)
                    sp.dma_start(step(x2_dram, b, i), xo[b][:, :, :]).then_inc(stored[b], 16)

                for b in range(NB):
                    load_x(b, 1)
                with sp.Fori(1, STEPS) as i:
                    for b in range(NB):
                        load_again(b, i)
                    for b in range(NB):
                        sp.wait_ge(xn_done[b], i + 1)
                        load_x(b, i + 1)
                    for b in range(NB):
                        store(b, i)
                for b in range(NB):
                    load_again(b, STEPS)
                for b in range(NB):
                    store(b, STEPS)
                for b in range(NB):
                    sp.wait_ge(stored[b], 16 * (STEPS + 1))

            @block.tensor
            def _(pe):
                def transpose_xn(b, i):
                    pe.wait_ge(xn_done[b], i + 1)
                    pe.wait_ge(ag_done[b], i)
                    for k in range(KD):
                        for c in range(CH):
                            last = pe.transpose(Q(b, 0)[:, k * GROUP + c * P:k * GROUP + (c + 1) * P],
                                                xn[b][:, c, k * P:(k + 1) * P], ident[:, :])
                    last.then_inc(xnT_ps[b], 1)

                def project_in(b, i):
                    pe.wait_ge(hTh_done[b], i + 1)
                    pe.wait_ge(hTl_done[b], i + 1)
                    pe.wait_ge(yo_done[b], i)
                    pe.wait_ge(yTl_done[b], CH * i)
                    for c in range(CH):
                        for k in range(KD):
                            tok = slice(c * P, (c + 1) * P)
                            last = split3(pe, Q(b, 1 + c)[:, :], hTh[b][:, k, tok], hTl[b][:, k, tok],
                                          win[0][:, k, 0:DI], win[1][:, k, 0:DI], k == 0, k == KD - 1)
                        last.then_inc(z_ps[b], 1)
                    pe.wait_ge(tg_done[b], i)
                    for c in range(CH):
                        for k in range(KD):
                            tok = slice(c * P, (c + 1) * P)
                            last = split3(pe, Q(b, 3)[:, c * H:(c + 1) * H], hTh[b][:, k, tok], hTl[b][:, k, tok],
                                          win[0][:, k, IN_COLS - H:IN_COLS], win[1][:, k, IN_COLS - H:IN_COLS],
                                          k == 0, k == KD - 1)
                    last.then_inc(dt_ps[b], 1)
                    for pair in range(MC // 2):
                        if pair > 0:
                            pe.wait_ge(zs_done[b], CH * i + pair)
                        for m in range(2):
                            col = DI + (2 * pair + m) * P
                            for k in range(KD):
                                last = split3(pe, Q(b, pair)[:, m * GROUP:(m + 1) * GROUP],
                                              win[0][:, k, col:col + P], win[1][:, k, col:col + P],
                                              hTh[b][:, k, :], hTl[b][:, k, :], k == 0, k == KD - 1)
                        last.then_inc(xbc_ps[b], 1)

                def sums(b, i):
                    pe.wait_ge(a_done[b], i + 1)
                    a = dts[b][:, 7, :, :]
                    for n, m in enumerate((upto, after, ones)):
                        last = pe.matmul(Q(b, 3)[:, 64 + n * CH * H:64 + (n + 1) * CH * H], m[:, :],
                                         a.rearrange("p c h -> p (c h)"), start=True, stop=True)
                    last.then_inc(sums_ps[b], 1)

                def by_token(b, i):
                    pe.wait_ge(xs_done[b], 3 * i + 2)
                    for c in range(CH):
                        pe.wait_ge(xc_done[b], 3 * i + 1 + c)
                        for m in range(KI):
                            last = pe.transpose(Q(b, c)[:, m * P:(m + 1) * P], cv[b][:, m, c * P:(c + 1) * P],
                                                ident[:, :])
                        last.then_inc(xT_ps[b], 1)
                    pe.wait_ge(xs_done[b], 3 * i + 3)
                    for c in range(CH):
                        tok = slice(c * P, (c + 1) * P)
                        pe.transpose(Q(b, 2)[:, tok], cv[b][:, KI, tok], ident[:, :])
                    for c in range(CH):
                        tok = slice(c * P, (c + 1) * P)
                        last = pe.matmul(Q(b, 2)[:, GROUP + c * P:GROUP + (c + 1) * P], cv[b][:, KI, tok],
                                         cv[b][:, KI + 1, tok], start=True, stop=True)
                    last.then_inc(btg_ps[b], 1)

                def exponents(b, i, c):
                    pe.wait_ge(au_done[b], CH * i + c + 1)
                    if c == 0:
                        pe.wait_ge(xtok_done[b], CH * i + CH)
                    else:
                        pe.wait_ge(y2s_done[b], CH * i + c)
                        pe.wait_ge(y1s_done[b], CH * i + c)
                    for half in range(2):
                        last = pe.matmul(Q(b, half)[:, :], after[:, :],
                                         au[b][:, half * 4:half * 4 + 4, :].rearrange("p h i -> p (h i)"),
                                         start=True, stop=True)
                    last.then_inc(dec_ps[b], 1)

                def within(b, i, c):
                    pe.wait_ge(w_done[b], CH * i + c + 1)
                    if c == 0:
                        pe.wait_ge(dec_done[b], CH * i + 1)
                    else:
                        pe.wait_ge(btok_done[b], i + 1)
                        pe.wait_ge(gm_done[b], i + 1)
                    for h in range(H):
                        last = pe.matmul(Q(b, 2 * c)[:, h * HD:(h + 1) * HD], dec[b][:, h, :],
                                         xdt[b][:, c, h * HD:(h + 1) * HD], start=True, stop=True)
                    last.then_inc(yin_ps[b], 1)

                def from_state(b, i, c):
                    pe.wait_ge(st_done[b], CH * i + c)
                    if c == 0:
                        pe.wait_ge(dec_done[b], CH * i + 1)
                    else:
                        pe.wait_ge(dec_done[b], CH * i + c + 1)
                    pe.matmul(Q(b, 1)[:, :], cv[b][:, KI + 1, c * P:(c + 1) * P], state[b][:, :],
                              start=True, stop=True).then_inc(yst_ps[b], 1)

                def state_add(b, i, c):
                    pe.wait_ge(xend_done[b], CH * i + c + 1)
                    pe.wait_ge(btok_done[b], i + 1)
                    pe.wait_ge(ex_done[b], i + 1)
                    pe.matmul(Q(b, 3)[:, :], btok[b][:, c, :], xend[b][:, :],
                              start=True, stop=True).then_inc(add_ps[b], 1)

                def transpose_y(b, i):
                    for c in range(CH):
                        pe.wait_ge(yn_done[b], CH * i + c + 1)
                        pe.wait_ge(y2s_done[b], CH * i + c + 1)
                        for m in range(KI):
                            last = pe.transpose(Q(b, 2 * c)[:, m * P:(m + 1) * P], yy[b][:, c, m * P:(m + 1) * P],
                                                ident[:, :])
                        last.then_inc(yT_ps[b], 1)

                def project_out(b, i):
                    pe.wait_ge(yTh_done[b], CH * i + CH)
                    pe.wait_ge(yTl_done[b], CH * i + CH)
                    pe.wait_ge(y1s_done[b], CH * i + CH)
                    for m in range(KD):
                        for k in range(KI):
                            last = split3(pe, Q(b, 1)[:, m * GROUP:(m + 1) * GROUP],
                                          wout[0][:, k, m * P:(m + 1) * P], wout[1][:, k, m * P:(m + 1) * P],
                                          yTh[b][:, k, :], yTl[b][:, k, :], k == 0, k == KI - 1)
                    last.then_inc(o_ps[b], 1)

                def glu(b, i):
                    pe.wait_ge(y1h_done[b], i + 1)
                    pe.wait_ge(y1l_done[b], i + 1)
                    pe.wait_ge(st_done[b], CH * i + CH)
                    for m in range(2 * KD):
                        for k in range(KD):
                            last = split3(pe, Q(b, 0 if m < KD else 3)[:, m % KD * GROUP:(m % KD + 1) * GROUP],
                                          wglu[0][:, k, m * P:(m + 1) * P], wglu[1][:, k, m * P:(m + 1) * P],
                                          y1h[b][:, k, :], y1l[b][:, k, :], k == 0, k == KD - 1)
                    last.then_inc(glu_ps[b], 1)

                def transpose_y2(b, i):
                    pe.wait_ge(y2_done[b], i + 1)
                    pe.wait_ge(y1_done[b], i + 1)
                    for c in range(CH):
                        for k in range(KD):
                            last = pe.transpose(Q(b, 1)[:, c * D + k * P:c * D + (k + 1) * P],
                                                y1[b][:, k, c * P:(c + 1) * P], ident[:, :])
                    last.then_inc(y2T_ps[b], 1)

                with pe.Fori(1, STEPS + 1) as i:
                    for b in range(NB):
                        transpose_xn(b, i)
                    for b in range(NB):
                        project_in(b, i)
                    for b in range(NB):
                        sums(b, i)
                    for b in range(NB):
                        by_token(b, i)
                    for c in range(CH):
                        for b in range(NB):
                            exponents(b, i, c)
                        for b in range(NB):
                            within(b, i, c)
                            from_state(b, i, c)
                            state_add(b, i, c)
                    for b in range(NB):
                        transpose_y(b, i)
                    for b in range(NB):
                        project_out(b, i)
                    for b in range(NB):
                        glu(b, i)
                    for b in range(NB):
                        transpose_y2(b, i)

            @block.scalar
            def _(act):
                def modulate(b, i):
                    act.wait_ge(xnT_ps[b], i + 1)
                    act.wait_ge(y1_done[b], i)
                    act.wait_ge(xbc_ps[b], 3 * i)
                    for k in range(KD):
                        last = act.activation(hT[b][:, k, :], Q(b, 0)[:, k * GROUP:(k + 1) * GROUP], ACT.Identity,
                                              bias=mod[b][:, 1, k:k + 1], scale=mod[b][:, 0, k:k + 1])
                    last.then_inc(hT_done[b], 1)
                    for k in range(KD):
                        last = act.activation(hTh[b][:, k, :], Q(b, 0)[:, k * GROUP:(k + 1) * GROUP], ACT.Identity,
                                              bias=mod[b][:, 1, k:k + 1], scale=mod[b][:, 0, k:k + 1])
                    last.then_inc(hTh_done[b], 1)

                def silu_z(b, i):
                    for c in range(CH):
                        act.wait_ge(z_ps[b], CH * i + c + 1)
                        act.wait_ge(y4_done[b], CH * i)
                        act.activation(zs[b][:, c, :], Q(b, 1 + c)[:, :], ACT.Silu).then_inc(zs_done[b], 1)

                def copy_xbc(b, i):
                    act.wait_ge(tap_done[b], MC * TAPS * i)
                    act.activation(xc[b][:, :, 0:TAPS - 1], xc[b][:, :, GROUP:GROUP + TAPS - 1],
                                   ACT.Copy).then_inc(halo_done[b], 1)
                    act.wait_ge(halo_done[b], i + 1)
                    for pair in range(MC // 2):
                        act.wait_ge(xbc_ps[b], 3 * i + pair + 1)
                        act.activation(xc[b][:, 2 * pair:2 * pair + 2, TAPS - 1:],
                                       Q(b, pair)[:, :].rearrange("p (m t) -> p m t", m=2),
                                       ACT.Copy).then_inc(xc_done[b], 1)

                def silu_xbc(b, i):
                    for pair in range(MC // 2):
                        act.wait_ge(tap_done[b], MC * TAPS * i + 2 * TAPS * (pair + 1))
                        v = cv[b][:, 2 * pair:2 * pair + 2, :]
                        act.activation(v, v, ACT.Silu).then_inc(xs_done[b], 1)

                def exp_dt(b, i):
                    act.wait_ge(dt_abs[b], i + 1)
                    act.activation(dts[b][:, 2, :, :], dts[b][:, 1, :, :], ACT.Exp, scale=-1.0).then_inc(dt_exp[b], 1)

                def exp_sums(b, i):
                    act.wait_ge(sums_ps[b], i + 1)
                    act.wait_ge(sdec_done[b], CH * i)
                    act.wait_ge(wend_done[b], i)
                    act.wait_ge(y1s_done[b], CH * i)
                    act.activation(ex[b][:, :, :, :].rearrange("p n c h -> p (n c h)"),
                                   Q(b, 3)[:, 64:64 + 3 * CH * H], ACT.Exp).then_inc(ex_done[b], 1)

                def copy_tokens(b, i):
                    for c in range(CH):
                        act.wait_ge(xT_ps[b], CH * i + c + 1)
                        act.wait_ge(xd_done[b], CH * i)
                        act.wait_ge(y3_done[b], CH * i)
                        act.activation(xtok[b][:, c, :], Q(b, c)[:, :], ACT.Copy).then_inc(xtok_done[b], 1)
                    act.wait_ge(btg_ps[b], i + 1)
                    act.wait_ge(add_ps[b], CH * i)
                    act.activation(btok[b][:, :, :].rearrange("p c n -> p (c n)"), Q(b, 2)[:, 0:GROUP],
                                   ACT.Copy).then_inc(btok_done[b], 1)

                def decays(b, i, c):
                    act.wait_ge(dec_ps[b], CH * i + c + 1)
                    act.wait_ge(yin_ps[b], CH * i + c)
                    for half in range(2):
                        last = act.activation(dec[b][:, 4 * half:4 * half + 4, :].rearrange("p h i -> p (h i)"),
                                              Q(b, half)[:, :], ACT.Exp)
                    last.then_inc(dec_done[b], 1)

                def squares(b, i, c):
                    act.wait_ge(y4_done[b], CH * i + c + 1)
                    act.wait_ge(yT_ps[b], CH * i)
                    act.activation(xdt[b][:, c, :], yy[b][:, c, :], ACT.Square,
                                   accum_out=ss[b][:, c:c + 1]).then_inc(sq_done[b], 1)

                def split_yT(b, i):
                    for c in range(CH):
                        act.wait_ge(yT_ps[b], CH * i + c + 1)
                        act.wait_ge(o_ps[b], i)
                        act.activation(yTh[b][:, :, c * P:(c + 1) * P],
                                       Q(b, 2 * c)[:, :].rearrange("p (k t) -> p k t", k=KI),
                                       ACT.Copy).then_inc(yTh_done[b], 1)

                def split_y1(b, i):
                    act.wait_ge(y1_done[b], i + 1)
                    act.wait_ge(glu_ps[b], i)
                    act.activation(y1h[b][:, :, :], y1[b][:, :, :], ACT.Copy).then_inc(y1h_done[b], 1)

                def tanh_gate(b, i):
                    act.wait_ge(glu_ps[b], i + 1)
                    act.wait_ge(ag_done[b], i)
                    for m in range(KD):
                        last = act.activation(sg[b][:, m, :], Q(b, 3)[:, m * GROUP:(m + 1) * GROUP], ACT.Tanh,
                                              bias=glub[:, KD + m:KD + m + 1], scale=0.5)
                    last.then_inc(tg_done[b], 1)

                with act.Fori(1, STEPS + 1) as i:
                    for b in range(NB):
                        modulate(b, i)
                    for b in range(NB):
                        silu_z(b, i)
                        copy_xbc(b, i)
                    for b in range(NB):
                        silu_xbc(b, i)
                    for b in range(NB):
                        exp_dt(b, i)
                    for b in range(NB):
                        exp_sums(b, i)
                    for b in range(NB):
                        copy_tokens(b, i)
                    for c in range(CH):
                        for b in range(NB):
                            decays(b, i, c)
                    for c in range(CH):
                        for b in range(NB):
                            squares(b, i, c)
                    for b in range(NB):
                        split_yT(b, i)
                    for b in range(NB):
                        split_y1(b, i)
                    for b in range(NB):
                        tanh_gate(b, i)

            @block.vector
            def _(dve):
                def norm1(b, i):
                    dve.wait_ge(x_in[b], 16 * (i + 1))
                    dve.wait_ge(xnT_ps[b], i)
                    for c in range(CH):
                        last = dve.bn_stats(st[b][:, c, :], xt[b][:, c, :])
                    last.then_inc(ln1[b], 1)
                    dve.wait_ge(ln1[b], 3 * i + 1)
                    stand_alone(dve, held_dve)
                    for c in range(CH):
                        last = dve.bn_aggr(mv[b][:, c, :], st[b][:, c, :])
                    last.then_inc(ln1[b], 1)
                    dve.wait_ge(ln1[b], 3 * i + 2)
                    dve.tensor_scalar(rs[b][:, :], mv[b][:, :, 1], EPS, None, ALU.add).then_inc(ln1[b], 1)

                def apply1(b, i):
                    dve.wait_ge(root1[b], i + 1)
                    for c in range(CH):
                        last = dve.tensor_scalar(xn[b][:, c, :], xt[b][:, c, :], mv[b][:, c, 0:1],
                                                 rs[b][:, c:c + 1], ALU.subtract, ALU.mult)
                    last.then_inc(xn_done[b], 1)

                def conv(b, i):
                    n = MC * TAPS * i
                    dve.wait_ge(halo_done[b], i + 1)
                    dve.wait_ge(yst_ps[b], CH * i)
                    for pair in range(MC // 2):
                        dve.wait_ge(xc_done[b], 3 * i + pair + 1)
                        for tap in range(TAPS):
                            for m in (2 * pair, 2 * pair + 1):
                                src = xc[b][:, m, tap:tap + GROUP]
                                w = convw[:, m, tap:tap + 1]
                                if tap == 0:
                                    last = dve.tensor_scalar(cv[b][:, m, :], src, w, convb[:, m:m + 1],
                                                             ALU.mult, ALU.add)
                                else:
                                    dve.wait_ge(tap_done[b], n + (pair * TAPS + tap - 1) * 2 + m % 2 + 1)
                                    last = dve.scalar_tensor_tensor(cv[b][:, m, :], src, w, cv[b][:, m, :],
                                                                    ALU.mult, ALU.add)
                                last.then_inc(tap_done[b], 1)

                def dt_link_step(b, i, n, ins):
                    ins.then_inc(dt_link[b], 1)
                    dve.wait_ge(dt_link[b], DT_LINKS * i + n)

                def softplus_head(b, i):
                    v, size = dts[b][:, 0, :, :], dts[b][:, 1, :, :]
                    dve.wait_ge(dt_ps[b], i + 1)
                    dve.wait_ge(xdt_done[b], CH * i)
                    dve.wait_ge(au_done[b], CH * i)
                    dve.wait_ge(xend_done[b], CH * i)
                    dve.wait_ge(sums_ps[b], i)
                    dt_link_step(b, i, 1, dve.tensor_tensor(
                        v, Q(b, 3)[:, 0:CH * H].rearrange("p (c h) -> p c h", c=CH), dtb[:, :, :], ALU.add))
                    dve.scalar_tensor_tensor(size, v, -1.0, v, ALU.mult, ALU.max).then_inc(dt_abs[b], 1)

                def softplus_tail(b, i):
                    v, _, u, s, s2, acc, dt, a = (dts[b][:, n, :, :] for n in range(8))
                    n = [1]

                    def link(ins):
                        n[0] += 1
                        dt_link_step(b, i, n[0], ins)

                    dve.wait_ge(dt_exp[b], i + 1)
                    link(dve.tensor_scalar(s, u, 2.0, None, ALU.add))
                    link(dve.reciprocal(s, s))
                    link(dve.tensor_tensor(s, s, u, ALU.mult))
                    link(dve.tensor_tensor(s2, s, s, ALU.mult))
                    link(dve.tensor_scalar(acc, s2, SERIES[0], None, ALU.mult))
                    for coef in SERIES[1:-1]:
                        link(dve.scalar_tensor_tensor(acc, acc, coef, s2, ALU.add, ALU.mult))
                    link(dve.scalar_tensor_tensor(acc, acc, 1.0, s, ALU.add, ALU.mult))
                    link(dve.tensor_scalar(v, v, 0.0, None, ALU.max))
                    link(dve.scalar_tensor_tensor(dt, acc, 2.0, v, ALU.mult, ALU.add))
                    assert n[0] == DT_LINKS
                    dve.scalar_tensor_tensor(a, dt, -1.0, negA[:, :, :], ALU.mult, ALU.mult
                                             ).then_inc(a_done[b], 1)

                def times_dt(b, i):
                    for c in range(CH):
                        dve.wait_ge(xtok_done[b], CH * i + c + 1)
                        dve.wait_ge(yn_done[b], CH * i)
                        dve.tensor_tensor(xdt[b][:, c, :].rearrange("p (h e) -> p h e", h=H),
                                          xtok[b][:, c, :].rearrange("p (h e) -> p h e", h=H),
                                          dts[b][:, 6, c, :].unsqueeze(2).to_broadcast([P, H, HD]),
                                          ALU.mult).then_inc(xdt_done[b], 1)

                def mask_bc(b, i):
                    dve.wait_ge(btok_done[b], i + 1)
                    dve.wait_ge(w_done[b], CH * i)
                    dve.tensor_tensor(gm[b][:, :, :], Q(b, 2)[:, GROUP:2 * GROUP].rearrange("p (c t) -> p c t", c=CH),
                                      upto[:, :].unsqueeze(1).to_broadcast([P, CH, P]),
                                      ALU.mult).then_inc(gm_done[b], 1)

                def times_decay(b, i, c):
                    dve.wait_ge(dec_done[b], CH * i + c + 1)
                    dve.wait_ge(gm_done[b], i + 1)
                    dve.tensor_tensor(dec[b][:, :, :], dec[b][:, :, :],
                                      gm[b][:, c, :].unsqueeze(1).to_broadcast([P, H, P]),
                                      ALU.mult).then_inc(w_done[b], 1)

                def output(b, i, c):
                    dve.wait_ge(yst_ps[b], CH * i + c + 1)
                    dve.wait_ge(ex_done[b], i + 1)
                    dve.wait_ge(yT_ps[b], CH * i)
                    y = yy[b][:, c, :]
                    dve.tensor_tensor(y.rearrange("p (h e) -> p h e", h=H),
                                      Q(b, 1)[:, :].rearrange("p (h e) -> p h e", h=H),
                                      ex[b][:, 0, c, :].unsqueeze(2).to_broadcast([P, H, HD]),
                                      ALU.mult).then_inc(y1s_done[b], 1)
                    dve.wait_ge(y1s_done[b], CH * i + c + 1)
                    dve.wait_ge(yin_ps[b], CH * i + c + 1)
                    dve.tensor_tensor(y, y, Q(b, 2 * c)[:, :], ALU.add).then_inc(y2s_done[b], 1)

                def new_state(b, i, c):
                    dve.wait_ge(add_ps[b], CH * i + c + 1)
                    dve.wait_ge(sdec_done[b], CH * i + c + 1)
                    dve.tensor_tensor(state[b][:, :], state[b][:, :], Q(b, 3)[:, :], ALU.add).then_inc(st_done[b], 1)

                def mean_square(b, i, c):
                    dve.wait_ge(sq_done[b], CH * i + c + 1)
                    dve.tensor_scalar(rr[b][:, c:c + 1], ss[b][:, c:c + 1], 1.0 / DI, EPS, ALU.mult,
                                      ALU.add).then_inc(ms_done[b], 1)

                def norm_y(b, i, c):
                    dve.wait_ge(rr_done[b], CH * i + c + 1)
                    dve.tensor_scalar(yy[b][:, c, :], yy[b][:, c, :], rr[b][:, c:c + 1], None,
                                      ALU.mult).then_inc(yn_done[b], 1)

                def split_yT(b, i):
                    for c in range(CH):
                        dve.wait_ge(yTh_done[b], CH * i + c + 1)
                        tok = slice(c * P, (c + 1) * P)
                        dve.tensor_tensor(yTl[b][:, :, tok], Q(b, 2 * c)[:, :].rearrange("p (k t) -> p k t", k=KI),
                                          yTh[b][:, :, tok].bitcast(F32), ALU.subtract).then_inc(yTl_done[b], 1)

                def add_h(b, i):
                    dve.wait_ge(o_ps[b], i + 1)
                    dve.wait_ge(y2T_ps[b], i)
                    dve.wait_ge(hT_done[b], i + 1)
                    dve.tensor_tensor(y1[b][:, :, :], Q(b, 1)[:, :].rearrange("p (k t) -> p k t", k=KD),
                                      hT[b][:, :, :], ALU.add).then_inc(y1_done[b], 1)

                def gated(b, i):
                    dve.wait_ge(sg_done[b], i + 1)
                    for m in range(KD):
                        last = dve.scalar_tensor_tensor(sg[b][:, m, :], Q(b, 0)[:, m * GROUP:(m + 1) * GROUP],
                                                        glub[:, m:m + 1], sg[b][:, m, :], ALU.add, ALU.mult)
                    last.then_inc(ag_done[b], 1)

                def norm2(b, i):
                    dve.wait_ge(y2T_ps[b], i + 1)
                    y = Q(b, 1)[:, :].rearrange("p (c d) -> p c d", c=CH)
                    for c in range(CH):
                        last = dve.bn_stats(st[b][:, c, :], y[:, c, :])
                    last.then_inc(ln2[b], 1)
                    dve.wait_ge(ln2[b], 3 * i + 1)
                    stand_alone(dve, held_dve)
                    for c in range(CH):
                        last = dve.bn_aggr(mv[b][:, c, :], st[b][:, c, :])
                    last.then_inc(ln2[b], 1)
                    dve.wait_ge(ln2[b], 3 * i + 2)
                    dve.tensor_scalar(rs[b][:, :], mv[b][:, :, 1], EPS, None, ALU.add).then_inc(ln2[b], 1)

                def apply2(b, i):
                    y = Q(b, 1)[:, :].rearrange("p (c d) -> p c d", c=CH)
                    dve.wait_ge(root2[b], i + 1)
                    dve.wait_ge(stored[b], 16 * i)
                    for c in range(CH):
                        last = dve.tensor_scalar(xo[b][:, c, :], y[:, c, :], mv[b][:, c, 0:1],
                                                 rs[b][:, c:c + 1], ALU.subtract, ALU.mult)
                    last.then_inc(yo_done[b], 1)

                with dve.Fori(1, STEPS + 1) as i:
                    for b in range(NB):
                        norm1(b, i)
                    for b in range(NB):
                        apply1(b, i)
                    for b in range(NB):
                        softplus_head(b, i)
                    for b in range(NB):
                        conv(b, i)
                    for b in range(NB):
                        softplus_tail(b, i)
                    for b in range(NB):
                        times_dt(b, i)
                    for b in range(NB):
                        mask_bc(b, i)
                    for c in range(CH):
                        for b in range(NB):
                            times_decay(b, i, c)
                            output(b, i, c)
                            new_state(b, i, c)
                    for c in range(CH):
                        for b in range(NB):
                            mean_square(b, i, c)
                        for b in range(NB):
                            norm_y(b, i, c)
                    for b in range(NB):
                        split_yT(b, i)
                    for b in range(NB):
                        add_h(b, i)
                    for b in range(NB):
                        gated(b, i)
                    for b in range(NB):
                        norm2(b, i)
                    for b in range(NB):
                        apply2(b, i)

            @block.gpsimd
            def _(pool):
                def root(out, n):
                    return pool.tensor_tensor(out, out, minus_half[:, 0:n], ALU.pow)

                def root_norm1(b, i):
                    pool.wait_ge(ln1[b], 3 * i + 3)
                    root(rs[b][:, :], CH).then_inc(root1[b], 1)

                def root_norm2(b, i):
                    pool.wait_ge(ln2[b], 3 * i + 3)
                    root(rs[b][:, :], CH).then_inc(root2[b], 1)

                def root_y(b, i, c):
                    pool.wait_ge(ms_done[b], CH * i + c + 1)
                    root(rr[b][:, c:c + 1], 1).then_inc(rr_done[b], 1)

                def split_h(b, i):
                    pool.wait_ge(hT_done[b], i + 1)
                    pool.wait_ge(hTh_done[b], i + 1)
                    pool.tensor_tensor(hTl[b][:, :, :], hT[b][:, :, :], hTh[b][:, :, :].bitcast(F32),
                                       ALU.subtract).then_inc(hTl_done[b], 1)

                def mask_a(b, i, c):
                    if c == 0:
                        pool.wait_ge(a_done[b], i + 1)
                    pool.wait_ge(dec_ps[b], CH * i + c)
                    pool.tensor_tensor(au[b][:, :, :], upto[:, :].unsqueeze(1).to_broadcast([P, H, P]),
                                       dts[b][:, 7, c, :].unsqueeze(2).to_broadcast([P, H, P]),
                                       ALU.mult).then_inc(au_done[b], 1)

                def end_weights(b, i):
                    pool.wait_ge(ex_done[b], i + 1)
                    pool.tensor_tensor(dts[b][:, 1, :, :], dts[b][:, 6, :, :], ex[b][:, 1, :, :],
                                       ALU.mult).then_inc(wend_done[b], 1)

                def times_end(b, i, c):
                    pool.wait_ge(wend_done[b], i + 1)
                    pool.wait_ge(xtok_done[b], CH * i + c + 1)
                    pool.wait_ge(add_ps[b], CH * i + c)
                    pool.tensor_tensor(xend[b][:, :].rearrange("p (h e) -> p h e", h=H),
                                       xtok[b][:, c, :].rearrange("p (h e) -> p h e", h=H),
                                       dts[b][:, 1, c, :].unsqueeze(2).to_broadcast([P, H, HD]),
                                       ALU.mult).then_inc(xend_done[b], 1)

                def times_skip(b, i, c):
                    pool.wait_ge(xend_done[b], CH * i + c + 1)
                    pool.wait_ge(xdt_done[b], CH * i + c + 1)
                    pool.tensor_tensor(xtok[b][:, c, :], xtok[b][:, c, :], dskip[:, :], ALU.mult).then_inc(xd_done[b], 1)

                def decay_state(b, i, c):
                    pool.wait_ge(ex_done[b], i + 1)
                    pool.wait_ge(yst_ps[b], CH * i + c + 1)
                    pool.wait_ge(st_done[b], CH * i + c)
                    s = state[b][:, :].rearrange("p (h e) -> p h e", h=H)
                    pool.tensor_tensor(s, s, ex[b][:, 2, c, :].unsqueeze(2).to_broadcast([P, H, HD]),
                                       ALU.mult).then_inc(sdec_done[b], 1)

                def gate_y(b, i, c):
                    y = yy[b][:, c, :]
                    pool.wait_ge(xd_done[b], CH * i + c + 1)
                    pool.wait_ge(y2s_done[b], CH * i + c + 1)
                    pool.tensor_tensor(y, y, xtok[b][:, c, :], ALU.add).then_inc(y3_done[b], 1)
                    pool.wait_ge(y3_done[b], CH * i + c + 1)
                    pool.wait_ge(zs_done[b], CH * i + c + 1)
                    pool.tensor_tensor(y, y, zs[b][:, c, :], ALU.mult).then_inc(y4_done[b], 1)

                def split_y1(b, i):
                    pool.wait_ge(y1h_done[b], i + 1)
                    pool.wait_ge(y1_done[b], i + 1)
                    pool.tensor_tensor(y1l[b][:, :, :], y1[b][:, :, :], y1h[b][:, :, :].bitcast(F32),
                                       ALU.subtract).then_inc(y1l_done[b], 1)

                def sigmoid(b, i):
                    pool.wait_ge(tg_done[b], i + 1)
                    stand_alone(pool, held_pool)
                    pool.tensor_scalar(sg[b][:, :, :], sg[b][:, :, :], 0.5, 0.5, ALU.mult,
                                       ALU.add).then_inc(sg_done[b], 1)

                def add_gated(b, i):
                    pool.wait_ge(ag_done[b], i + 1)
                    pool.wait_ge(y1l_done[b], i + 1)
                    pool.tensor_tensor(y1[b][:, :, :], y1[b][:, :, :], sg[b][:, :, :], ALU.add).then_inc(y2_done[b], 1)

                def residual(b, i):
                    pool.wait_ge(yo_done[b], i + 1)
                    pool.tensor_tensor(xo[b][:, :, :], xo[b][:, :, :],
                                       gate_ln[:, b, 0, :].unsqueeze(1).to_broadcast([P, CH, D]),
                                       ALU.mult).then_inc(xo_link[b], 1)
                    pool.wait_ge(xo_link[b], 2 * i + 1)
                    pool.tensor_tensor(xo[b][:, :, :], xo[b][:, :, :],
                                       gate_ln[:, b, 1, :].unsqueeze(1).to_broadcast([P, CH, D]),
                                       ALU.add).then_inc(xo_link[b], 1)
                    pool.wait_ge(xo_link[b], 2 * i + 2)
                    pool.wait_ge(xr_in[b], 16 * (i + 1))
                    pool.tensor_tensor(xo[b][:, :, :], xo[b][:, :, :], xr[b][:, :, :], ALU.add).then_inc(xo_done[b], 1)

                with pool.Fori(1, STEPS + 1) as i:
                    for b in range(NB):
                        root_norm1(b, i)
                    for b in range(NB):
                        split_h(b, i)
                    for b in range(NB):
                        mask_a(b, i, 0)
                    for b in range(NB):
                        end_weights(b, i)
                    for c in range(CH):
                        for b in range(NB):
                            times_end(b, i, c)
                            if c == 0:
                                mask_a(b, i, 1)
                        for b in range(NB):
                            decay_state(b, i, c)
                            times_skip(b, i, c)
                        for b in range(NB):
                            gate_y(b, i, c)
                    for c in range(CH):
                        for b in range(NB):
                            root_y(b, i, c)
                    for b in range(NB):
                        split_y1(b, i)
                    for b in range(NB):
                        sigmoid(b, i)
                        add_gated(b, i)
                    for b in range(NB):
                        root_norm2(b, i)
                    for b in range(NB):
                        residual(b, i)


def experts(nc, sem, prime, t, mod, gate_b_row, ident, minus_half, bank, x2_dram, out):
    ALL = NE + 1
    GROUPS = NB * MSTEPS
    with ExitStack() as ctx:
        def sb(name, shape, dt=F32):
            return ctx.enter_context(nc.sbuf_tensor(name, shape, dt))

        def two(name, shape, dt=F32):
            return [sb(f"{name}{b}", shape, dt) for b in range(2)]

        EW = KD * 2 * INTER + D
        wh = sb("wh", [P, ALL, EW], F32R)
        wl = sb("wl", [P, ALL, EW], F32R)
        gatew = sb("gatew", [P, KD, NE])
        gateb = sb("gateb", [P, MT, NE])
        pick_raw = sb("pick_raw", [2 * NE, NE, P])
        pick = sb("pick", [2 * NE, NE, P], F32R)
        x2 = sb("x2", [P, MT, D])
        st = sb("mst", [P, MT, 6])
        mv = sb("mmv", [P, MT, 2])
        rs = sb("mrs", [P, MT])
        hT = sb("mhT", [P, KD, MGROUP])
        hh = two("mhh", [P, KD, MGROUP], F32R)
        hl = two("mhl", [P, KD, MGROUP], F32R)
        score = sb("score", [P, MT, NE])
        biased = sb("biased", [P, MT, NE])
        top = sb("top", [P, MT, 8])
        best = sb("best", [P, MT, 8])
        rest = sb("rest", [P, MT, NE])
        wsum = sb("wsum", [P, MT])
        comb = sb("comb", [P, MT, NE])
        comb_hi = sb("comb_hi", [P, MT, NE], F32R)
        comb2 = sb("comb2", [P, MT, 2 * NE])
        combT = two("combT", [2 * NE, MGROUP], F32R)
        gs = two("gs", [P, MGROUP])
        ff = two("ff", [P, MGROUP])
        fh = two("fh", [P, MGROUP], F32R)
        fl = two("fl", [P, MGROUP], F32R)
        xres = sb("xres", [P, MT, D])
        yo = sb("yo", [P, MT, D])

        if True:
            raw = [hT[:, :, :].rearrange("p k t -> p (k t)")[:, 0:EW],
                   x2[:, :, :].rearrange("p k t -> p (k t)")[:, 0:EW],
                   xres[:, :, :].rearrange("p k t -> p (k t)")[:, 0:EW],
                   yo[:, :, :].rearrange("p k t -> p (k t)")[:, 0:EW]]
            raw_in = [sem(f"ew_in{r}") for r in range(len(raw))]
            hi_done = sem("ew_hi")
            lo_done = sem("ew_lo")
            k_in = sem("k_in")
            with nc.Block() as block:
                @block.sync
                def _(sp):
                    sp.dma_start(gatew[:, :, :], t["gate_w"]).then_inc(k_in, 16)
                    sp.dma_start(gateb[:, :, :], t["gate_b"]).then_inc(k_in, 16)
                    sp.dma_start(pick_raw[:, :, :], t["pick"]).then_inc(k_in, 16)
                    for e in range(ALL):
                        if e >= len(raw):
                            sp.wait_ge(lo_done, e - len(raw) + 1)
                        sp.dma_start(raw[e % len(raw)], t["experts"][e]).then_inc(raw_in[e % len(raw)], 16)
                    sp.wait_ge(k_in, 48)

                @block.scalar
                def _(act):
                    for e in range(ALL):
                        act.wait_ge(raw_in[e % len(raw)], 16 * (e // len(raw) + 1))
                        act.activation(wh[:, e, :], raw[e % len(raw)], ACT.Copy).then_inc(hi_done, 1)

                @block.vector
                def _(dve):
                    dve.wait_ge(k_in, 48)
                    dve.tensor_copy(pick[:, :, :], pick_raw[:, :, :])
                    dve.memset(best[:, :, :], 3.0e38)
                    for e in range(ALL):
                        dve.wait_ge(hi_done, e + 1)
                        dve.tensor_tensor(wl[:, e, :], raw[e % len(raw)], wh[:, e, :].bitcast(F32),
                                          ALU.subtract).then_inc(lo_done, 1)

        def w13(half, e, k, gate):
            w = (wh, wl)[half]
            return w[:, e, k * 2 * INTER + (1 - gate) * INTER:k * 2 * INTER + (2 - gate) * INTER]

        def w2(half, e):
            return (wh, wl)[half][:, e, KD * 2 * INTER:EW]

        GATE, UP = (bank[0], bank[1]), (bank[2], bank[3])
        ROUTE, PREP = bank[4], bank[5]
        ACC = (bank[6], bank[7])

        ROUTE_LINKS = 13
        counts = []

        def counted(name, per_group):
            counts.append((sem(name), per_group))
            return counts[-1][0]

        x2_in = counted("x2_in", 16)
        ln = counted("mln", 3)
        mroot = counted("mroot", 1)
        n_done = counted("n_done", 1)
        nT_ps = counted("nT_ps", KD)
        mh_done = counted("mh_done", KD)
        mhh_done = counted("mhh_done", KD)
        mhl_done = counted("mhl_done", KD)
        logit_ps = counted("logit_ps", 1)
        tanh_done = counted("tanh_done", 1)
        route = counted("route", ROUTE_LINKS)
        comb_done = counted("comb_done", 1)
        combT_ps = counted("combT_ps", 1)
        combT_done = counted("combT_done", 1)
        gate_ps = counted("gate_ps", ALL)
        up_ps = counted("up_ps", ALL)
        gs_done = counted("gs_done", ALL)
        gc_done = counted("gc_done", NE)
        ff_done = counted("ff_done", ALL)
        fh_done = counted("fh_done", ALL)
        fl_done = counted("fl_done", ALL)
        down_ps = counted("down_ps", ALL)
        scaled = counted("scaled", 1)
        res_in = counted("res_in", 16)
        yo_done2 = counted("yo_done2", 1)
        out_stored = counted("out_stored", 16)

        prime(counts)
        held_dve = sem("mheld_dve")

        def x2_rows(b, j):
            return x2_dram[b, bass.ds(j * (MT // CH), MT // CH)].rearrange("s p c d -> p s c d")

        def tiles(ap):
            return ap.rearrange("p (s c) d -> p s c d", c=CH)

        def walk(eng, prepare_first, group):
            prepare_first()
            group(1, 0, 0, first=True)
            with eng.Fori(0, MSTEPS - 1) as i:
                group(2 * i + 2, 1, i)
                group(2 * i + 3, 0, i + 1)
            group(GROUPS, 1, MSTEPS - 1, last=True)

        with nc.Block() as block:
            @block.sync
            def _(sp):
                def load(n, b, j):
                    sp.wait_ge(nT_ps, KD * n)
                    sp.dma_start(tiles(x2[:, :, :]), x2_rows(b, j)).then_inc(x2_in, 16)

                def store(n, b, j):
                    sp.wait_ge(yo_done2, n + 1)
                    sp.dma_start(out[b, bass.ds(j * MGROUP, MGROUP), :].rearrange("(c p) d -> p c d", p=P),
                                 yo[:, :, :]).then_inc(out_stored, 16)

                def group(n, b, j, first=False, last=False):
                    if not last:
                        load(n + 1, 1 - b, j + b)
                    if not first:
                        store(n - 1, 1 - b, j - 1 + b)
                    sp.dma_start(tiles(xres[:, :, :]), x2_rows(b, j)).then_inc(res_in, 16)
                    if last:
                        store(n, b, j)

                walk(sp, lambda: load(1, 0, 0), group)
                sp.wait_ge(out_stored, 16 * (GROUPS + 1))

            @block.tensor
            def _(pe):
                def transpose_n(k, n):
                    if k == 0:
                        pe.wait_ge(n_done, n + 1)
                        pe.wait_ge(combT_done, n)
                    else:
                        pe.wait_ge(mhh_done, KD * n + k)
                    for c in range(MT):
                        last = pe.transpose(PREP[:, c * P:(c + 1) * P], x2[:, c, k * P:(k + 1) * P], ident[:, :])
                    last.then_inc(nT_ps, 1)

                def logits(n):
                    pe.wait_ge(mh_done, KD * n + KD)
                    pe.wait_ge(mhh_done, KD * n + KD)
                    for c in range(MT):
                        for k in range(KD):
                            last = pe.matmul(PREP[:, c * NE:(c + 1) * NE], hT[:, k, c * P:(c + 1) * P],
                                             gatew[:, k, :], start=(k == 0), stop=(k == KD - 1))
                    last.then_inc(logit_ps, 1)

                def transpose_comb(n):
                    pe.wait_ge(comb_done, n + 1)
                    for c in range(MT):
                        last = pe.transpose(PREP[0:2 * NE, c * P:(c + 1) * P], comb2[:, c, :], ident[:, :])
                    last.then_inc(combT_ps, 1)

                def prepare(slot, n):
                    if slot in (2, 4):
                        transpose_n(slot // 2 - 1, n)
                    if slot == 6:
                        logits(n)
                    if slot == 12:
                        transpose_comb(n)

                def up(e, n, b):
                    s = n * ALL + e
                    if e == 0:
                        pe.wait_ge(mhh_done, KD * n + KD)
                        pe.wait_ge(mhl_done, KD * n + KD)
                        pe.wait_ge(combT_done, n + 1)
                    par = e % 2
                    if e >= 2:
                        pe.wait_ge(ff_done, s - 1)
                    else:
                        pe.wait_ge(ff_done, n * ALL)
                    for k in range(KD):
                        last = split3(pe, GATE[par][:, :], w13(0, e, k, 1), w13(1, e, k, 1),
                                      hh[b][:, k, :], hl[b][:, k, :], k == 0, k == KD - 1)
                    last.then_inc(gate_ps, 1)
                    for k in range(KD):
                        last = split3(pe, UP[par][:, :], w13(0, e, k, 0), w13(1, e, k, 0),
                                      hh[b][:, k, :], hl[b][:, k, :], k == 0, k == KD - 1)
                    if e < NE:
                        pe.wait_ge(gc_done, n * NE + e)
                        last = pe.matmul(ROUTE[:, :], pick[:, e, :], combT[b][:, :], start=True, stop=True)
                    last.then_inc(up_ps, 1)

                def down(e, n):
                    s = n * ALL + e
                    pe.wait_ge(fh_done, s + 1)
                    pe.wait_ge(fl_done, s + 1)
                    if e == 0:
                        pe.wait_ge(scaled, n)
                    for c in range(MT):
                        tok = slice(c * P, (c + 1) * P)
                        last = split3(pe, ACC[c // 2][:, c % 2 * D:(c % 2 + 1) * D], fh[e % 2][:, tok],
                                      fl[e % 2][:, tok], w2(0, e), w2(1, e), e == 0 and c % 2 == 0, e == ALL - 1)
                    last.then_inc(down_ps, 1)

                def group(n, b, j, first=False, last=False):
                    for e in range(ALL):
                        up(e, n, b)
                        if e > 0:
                            down(e - 1, n)
                        elif not first:
                            down(ALL - 1, n - 1)
                        if not last:
                            prepare(e, n + 1)
                    if last:
                        down(ALL - 1, n)

                def prepare_first():
                    for slot in range(ALL):
                        prepare(slot, 1)

                walk(pe, prepare_first, group)

            @block.scalar
            def _(act):
                def modulate(k, n, b):
                    act.wait_ge(nT_ps, KD * n + k + 1)
                    act.wait_ge(logit_ps, n)
                    act.wait_ge(mhl_done, KD * n + k)
                    args = dict(bias=mod[b][:, 3, k:k + 1], scale=mod[b][:, 2, k:k + 1])
                    act.activation(hT[:, k, :], PREP[:, :], ACT.Identity, **args).then_inc(mh_done, 1)
                    act.activation(hh[b][:, k, :], PREP[:, :], ACT.Identity, **args).then_inc(mhh_done, 1)

                def prepare(slot, n, b):
                    if slot in (3, 5):
                        modulate(slot // 2 - 1, n, b)
                    if slot == 7:
                        act.wait_ge(logit_ps, n + 1)
                        act.wait_ge(comb_done, n)
                        act.activation(score[:, :, :].rearrange("p c e -> p (c e)"), PREP[:, 0:MT * NE],
                                       ACT.Tanh, scale=0.5).then_inc(tanh_done, 1)
                    if slot == 13:
                        act.wait_ge(combT_ps, n + 1)
                        act.activation(combT[b][:, :], PREP[0:2 * NE, :], ACT.Copy).then_inc(combT_done, 1)

                def silu_gate(e, n):
                    s = n * ALL + e
                    act.wait_ge(gate_ps, s + 1)
                    if e >= 2:
                        act.wait_ge(ff_done, s - 1)
                    else:
                        act.wait_ge(ff_done, n * ALL)
                    act.activation(gs[e % 2][:, :], GATE[e % 2][:, :], ACT.Silu).then_inc(gs_done, 1)

                def hi(e, n):
                    s = n * ALL + e
                    act.wait_ge(ff_done, s + 1)
                    if e >= 2:
                        act.wait_ge(down_ps, s - 1)
                    else:
                        act.wait_ge(down_ps, n * ALL)
                    act.activation(fh[e % 2][:, :], ff[e % 2][:, :], ACT.Copy).then_inc(fh_done, 1)

                def group(n, b, j, first=False, last=False):
                    for e in range(ALL):
                        silu_gate(e, n)
                        if not last:
                            prepare(e, n + 1, 1 - b)
                        hi(e, n)

                def prepare_first():
                    for slot in range(ALL):
                        prepare(slot, 1, 0)

                walk(act, prepare_first, group)

            @block.vector
            def _(dve):
                def norm(n):
                    dve.wait_ge(x2_in, 16 * (n + 1))
                    for c in range(MT):
                        last = dve.bn_stats(st[:, c, :], x2[:, c, :])
                    last.then_inc(ln, 1)
                    dve.wait_ge(ln, 3 * n + 1)
                    stand_alone(dve, held_dve)
                    for c in range(MT):
                        last = dve.bn_aggr(mv[:, c, :], st[:, c, :])
                    last.then_inc(ln, 1)
                    dve.wait_ge(ln, 3 * n + 2)
                    dve.tensor_scalar(rs[:, :], mv[:, :, 1], EPS, None, ALU.add).then_inc(ln, 1)

                def apply(n):
                    dve.wait_ge(mroot, n + 1)
                    for c in range(MT):
                        last = dve.tensor_scalar(x2[:, c, :], x2[:, c, :], mv[:, c, 0:1], rs[:, c:c + 1],
                                                 ALU.subtract, ALU.mult)
                    last.then_inc(n_done, 1)

                def routing(n):
                    k = [0]

                    def link(ins):
                        k[0] += 1
                        ins.then_inc(route, 1)
                        dve.wait_ge(route, ROUTE_LINKS * n + k[0])

                    dve.wait_ge(tanh_done, n + 1)
                    dve.wait_ge(combT_ps, n)
                    link(dve.tensor_scalar(score[:, :, :], score[:, :, :], 0.5, 0.5, ALU.mult, ALU.add))
                    link(dve.tensor_tensor(biased[:, :, :], score[:, :, :], gateb[:, :, :], ALU.add))
                    stand_alone(dve, held_dve)
                    for c in range(MT):
                        last = dve.max(top[:, c, :], biased[:, c, :])
                    link(last)
                    link(dve.tensor_copy(best[:, :, 0:TOPK], top[:, :, 0:TOPK]))
                    stand_alone(dve, held_dve)
                    for c in range(MT):
                        last = dve.match_replace(rest[:, c, :], best[:, c, :], biased[:, c, :], -3.0e38)
                    link(last)
                    link(dve.tensor_scalar(rest[:, :, :], rest[:, :, :], -1.0e38, None, ALU.is_lt))
                    link(dve.tensor_tensor(comb[:, :, :], score[:, :, :], rest[:, :, :], ALU.mult))
                    link(dve.tensor_reduce(wsum[:, :], comb[:, :, :], mybir.AxisListType.X, ALU.add))
                    link(dve.reciprocal(wsum[:, :], wsum[:, :]))
                    link(dve.tensor_scalar(wsum[:, :], wsum[:, :], ROUTE_SCALE, None, ALU.mult))
                    link(dve.tensor_tensor(comb[:, :, :], comb[:, :, :],
                                           wsum[:, :].unsqueeze(2).to_broadcast([P, MT, NE]), ALU.mult))
                    link(dve.tensor_copy(comb_hi[:, :, :], comb[:, :, :]))
                    link(dve.tensor_copy(comb2[:, :, 0:NE], comb_hi[:, :, :].bitcast(F32)))
                    assert k[0] == ROUTE_LINKS
                    dve.tensor_tensor(comb2[:, :, NE:2 * NE], comb[:, :, :], comb_hi[:, :, :].bitcast(F32),
                                      ALU.subtract).then_inc(comb_done, 1)

                def prepare(slot, n):
                    if slot == 0:
                        norm(n)
                    if slot == 1:
                        apply(n)
                    if slot == 8:
                        routing(n)

                def times(e, n):
                    s = n * ALL + e
                    g = gs[e % 2][:, :]
                    dve.wait_ge(gs_done, s + 1)
                    dve.wait_ge(up_ps, s + 1)
                    if e < NE:
                        dve.tensor_tensor(g, g, ROUTE[:, :], ALU.mult).then_inc(gc_done, 1)
                        dve.wait_ge(gc_done, n * NE + e + 1)
                    if e >= 2:
                        dve.wait_ge(fl_done, s - 1)
                    else:
                        dve.wait_ge(fl_done, n * ALL)
                    dve.tensor_tensor(ff[e % 2][:, :], g, UP[e % 2][:, :], ALU.mult).then_inc(ff_done, 1)

                def scale(n, b):
                    dve.wait_ge(down_ps, ALL * (n + 1))
                    dve.wait_ge(out_stored, 16 * n)
                    for half in range(2):
                        last = dve.tensor_tensor(yo[:, 2 * half:2 * half + 2, :],
                                                 ACC[half][:, :].rearrange("p (c d) -> p c d", c=2),
                                                 gate_b_row[b][:, :].unsqueeze(1).to_broadcast([P, 2, D]), ALU.mult)
                    last.then_inc(scaled, 1)

                def group(n, b, j, first=False, last=False):
                    for e in range(ALL):
                        times(e, n)
                        if e == 0 and not first:
                            scale(n - 1, 1 - b)
                        if not last:
                            prepare(e, n + 1)
                    if last:
                        scale(n, b)

                def prepare_first():
                    for slot in range(ALL):
                        prepare(slot, 1)

                walk(dve, prepare_first, group)

            @block.gpsimd
            def _(pool):
                def split_h(k, n, b):
                    pool.wait_ge(mh_done, KD * n + k + 1)
                    pool.wait_ge(mhh_done, KD * n + k + 1)
                    pool.tensor_tensor(hl[b][:, k, :], hT[:, k, :], hh[b][:, k, :].bitcast(F32),
                                       ALU.subtract).then_inc(mhl_done, 1)

                def prepare(slot, n, b):
                    if slot == 0:
                        pool.wait_ge(ln, 3 * n + 3)
                        pool.tensor_tensor(rs[:, :], rs[:, :], minus_half[:, :], ALU.pow).then_inc(mroot, 1)
                    if slot in (3, 5):
                        split_h(slot // 2 - 1, n, b)

                def lo(e, n):
                    s = n * ALL + e
                    pool.wait_ge(fh_done, s + 1)
                    if e >= 2:
                        pool.wait_ge(down_ps, s - 1)
                    else:
                        pool.wait_ge(down_ps, n * ALL)
                    pool.tensor_tensor(fl[e % 2][:, :], ff[e % 2][:, :], fh[e % 2][:, :].bitcast(F32),
                                       ALU.subtract).then_inc(fl_done, 1)

                def residual(n):
                    pool.wait_ge(scaled, n + 1)
                    pool.wait_ge(res_in, 16 * (n + 1))
                    pool.tensor_tensor(yo[:, :, :], yo[:, :, :], xres[:, :, :], ALU.add).then_inc(yo_done2, 1)

                def group(n, b, j, first=False, last=False):
                    for e in range(ALL):
                        lo(e, n)
                        if e == 1 and not first:
                            residual(n - 1)
                        if not last:
                            prepare(e, n + 1, 1 - b)
                    if last:
                        residual(n)

                def prepare_first():
                    for slot in range(ALL):
                        prepare(slot, 1, 0)

                walk(pool, prepare_first, group)


def host_layout(inputs):
    a = {k.replace("L0_attn_", "").replace("L0_ffn_", "").replace("L0_", ""): np.asarray(v) for k, v in inputs.items()}

    def slices(w):
        return w.reshape(-1, P, w.shape[-1]).transpose(1, 0, 2)

    def columns(v):
        return v.reshape(-1, P).T

    def everywhere(v, *shape):
        return np.broadcast_to(v, (P, *shape))

    def expert(w13, w2):
        return np.concatenate([slices(w13.T).reshape(P, KD * 2 * INTER), w2.T], axis=1)

    r = np.arange(P)
    out = {
        "x": a["x"].reshape(NB, STEPS, CH, P, D).transpose(0, 1, 3, 2, 4),
        "c_col": a["c"].T.reshape(KD, P, NB).transpose(1, 0, 2),
        "wmod": slices(a["wmod"]),
        "ln_wb": everywhere(np.stack([a["ln_w"], a["ln_b"]]), 2, D),
        "W_in": slices(a["W_in"]),
        "W_out": slices(a["W_out"]).reshape(P, KI * D),
        "glu_w": slices(a["glu_w"]).reshape(P, KD * 2 * D),
        "rms_w": columns(a["rms_w"]),
        "conv_w": a["conv_w"].reshape(MC, P, TAPS).transpose(1, 0, 2),
        "conv_b": columns(a["conv_b"]),
        "dt_bias": everywhere(a["dt_bias"], CH, H),
        "A_log": everywhere(a["A_log"], CH, H),
        "D_skip": everywhere(np.repeat(a["D_skip"], HD), DI),
        "glu_b": columns(a["glu_b"]),
        "gate_w": slices(a["gate_w"].T),
        "gate_b": everywhere(a["gate_b"], MT, NE),
        "experts": np.stack([expert(a["w13"][e], a["w2"][e]) for e in range(NE)] + [expert(a["w13_s"], a["w2_s"])]),
        "ident": np.eye(P, dtype=np.float32),
        "upto": (r[:, None] <= r[None, :]).astype(np.float32),
        "after": (r[:, None] > r[None, :]).astype(np.float32),
        "ones": np.ones((P, P), np.float32),
        "pick": np.broadcast_to((np.arange(2 * NE)[:, None] % NE == np.arange(NE)[None, :])[:, :, None],
                                (2 * NE, NE, P)).astype(np.float32),
    }
    return {k: np.ascontiguousarray(v) for k, v in out.items()}


def kernel(**inputs):
    import concourse.bacc as _bacc
    from concourse.bass_utils import run_bass_kernel_spmd as _run

    nc = _bacc.Bacc("TRN2", target_bir_lowering=False, num_devices=1)
    arrays, t = {}, {}
    for name, a in host_layout(inputs).items():
        arrays[f"in_{name}"] = a
        t[name] = nc.dram_tensor(f"in_{name}", a.shape, mybir.dt.from_np(a.dtype), kind="ExternalInput").ap()
    x2_dram = nc.dram_tensor("x2_dram", (NB, STEPS, P, CH, D), F32, kind="Internal").ap()
    out = nc.dram_tensor("out", (NB, SEQ, D), F32, kind="ExternalOutput").ap()
    build(nc, t, x2_dram, out)
    r = _run(nc, [arrays], core_ids=[0])
    return r.results[0]["out"]
```

```python
from contextlib import ExitStack

import numpy as np
import concourse.bass as bass
from concourse import mybir

ALU = mybir.AluOpType
ACT = mybir.ActivationFunctionType
F32 = mybir.dt.float32
F32R = mybir.dt.float32r

P = 128
NB = 2
SEQ = 4096
D = 256
DI = 512
H = 8
HD = DI // H
NS = 128
CONV = DI + 2 * NS
TAPS = 4
KD = D // P
KI = DI // P
MC = CONV // P
IN_COLS = 2 * DI + 2 * NS + H
EPS = 1e-5
NE = 16
INTER = 128
TOPK = 4
ROUTE_SCALE = 2.5

GROUP = 256
CH = GROUP // P
STEPS = SEQ // GROUP
MGROUP = 512
MT = MGROUP // P
MSTEPS = SEQ // MGROUP
DT_LINKS = 16
SERIES = [1.0 / (2 * n + 1) for n in range(8, -1, -1)]


def build(nc, t, x2_dram, out):
    ctx = ExitStack()

    def sb(name, shape, dt=F32):
        return ctx.enter_context(nc.sbuf_tensor(name, shape, dt))

    taken = []

    def sem(name):
        taken.append(nc.alloc_semaphore(name=name))
        return taken[-1]

    def prime(counts):
        with nc.Block() as block:
            @block.sync
            def _(sp):
                for semaphore, per_step in counts:
                    sp.sem_inc(semaphore, per_step)

    def clear_semaphores():
        nc.all_engine_barrier()
        nc.clear_and_free_semaphores(taken)
        nc.all_engine_barrier()
        taken.clear()

    with ctx:
        bank = [ctx.enter_context(nc.psum_tensor(f"bank{n}", [P, 512], F32)) for n in range(8)]
        mod = [sb(f"mod{b}", [P, 4, KD]) for b in range(NB)]
        gate_b_row = [sb(f"gb_row{b}", [P, D]) for b in range(NB)]
        ident = sb("ident", [P, P])
        minus_half = sb("minus_half", [P, MT])
        gate_ln = sb("gate_ln", [P, NB, 2, D])
        setup(nc, sem, t, mod, gate_b_row, gate_ln, ident, minus_half, bank)
        mixer(nc, sem, prime, t, mod, gate_ln, ident, minus_half, bank, x2_dram)
        clear_semaphores()
        experts(nc, sem, prime, t, mod, gate_b_row, ident, minus_half, bank, x2_dram, out)


def split3(pe, out, a_hi, a_lo, b_hi, b_lo, start, stop):
    pe.matmul(out, a_hi, b_hi, start=start, stop=False, skip_group_check=True)
    pe.matmul(out, a_hi, b_lo, start=False, stop=False, skip_group_check=True)
    return pe.matmul(out, a_lo, b_hi, start=False, stop=stop, skip_group_check=True)


def stand_alone(eng, counter):
    eng.sem_inc(counter, 1)


def setup(nc, sem, t, mod, gate_b_row, gate_ln, ident, minus_half, bank):
    with ExitStack() as ctx:
        c_col = ctx.enter_context(nc.sbuf_tensor("c_col", [P, KD, NB], F32))
        c_silu = ctx.enter_context(nc.sbuf_tensor("c_silu", [P, KD, NB], F32))
        c_wide = ctx.enter_context(nc.sbuf_tensor("c_wide", [P, KD, NB, P], F32))
        wmod = ctx.enter_context(nc.sbuf_tensor("wmod", [P, KD, 6 * D], F32))
        pos = ctx.enter_context(nc.sbuf_tensor("pos", [P, 2, D], F32))
        mag = ctx.enter_context(nc.sbuf_tensor("mag", [P, 2, D], F32))
        lnw = ctx.enter_context(nc.sbuf_tensor("lnw", [P, 2, D], F32))
        loaded = sem("mod_loaded")
        silu_done = sem("c_silu_done")
        wide_done = sem("c_wide_done")
        cols_done = sem("mod_cols_done")
        rows_done = sem("mod_rows_done")
        link = sem("mod_link")
        with nc.Block() as block:
            @block.sync
            def _(sp):
                sp.dma_start(c_col[:, :, :], t["c_col"]).then_inc(loaded, 16)
                sp.dma_start(wmod[:, :, :], t["wmod"]).then_inc(loaded, 16)
                sp.dma_start(ident[:, :], t["ident"]).then_inc(loaded, 16)
                sp.dma_start(lnw[:, :, :], t["ln_wb"]).then_inc(loaded, 16)

            @block.gpsimd
            def _(pool):
                pool.memset(minus_half[:, :], -0.5)

            @block.scalar
            def _(act):
                act.wait_ge(loaded, 64)
                act.activation(c_silu[:, :, :], c_col[:, :, :], ACT.Silu).then_inc(silu_done, 1)
                act.wait_ge(silu_done, 1)
                act.activation(c_wide[:, :, :, :], c_silu[:, :, :].unsqueeze(3).to_broadcast([P, KD, NB, P]),
                               ACT.Copy).then_inc(wide_done, 1)

            @block.tensor
            def _(pe):
                pe.wait_ge(wide_done, 1)
                for b in range(NB):
                    for n, chunk in enumerate((1, 0, 4, 3)):
                        for m in range(KD):
                            for k in range(KD):
                                last = pe.matmul(bank[b][:, (n * KD + m) * 2:(n * KD + m) * 2 + 2],
                                                 wmod[:, k, chunk * D + m * P:chunk * D + (m + 1) * P],
                                                 c_silu[:, k, :], start=(k == 0), stop=(k == KD - 1))
                    last.then_inc(cols_done, 1)
                    for n, chunk in enumerate((2, 5)):
                        for k in range(KD):
                            last = pe.matmul(bank[2 + b][:, n * D:(n + 1) * D], c_wide[:, k, b, :],
                                             wmod[:, k, chunk * D:(chunk + 1) * D],
                                             start=(k == 0), stop=(k == KD - 1))
                    last.then_inc(rows_done, 1)

            @block.vector
            def _(dve):
                n = [0]

                def then_wait(ins):
                    n[0] += 1
                    ins.then_inc(link, 1)
                    dve.wait_ge(link, n[0])

                for b in range(NB):
                    dve.wait_ge(cols_done, b + 1)
                    col = bank[b][:, 0:8 * KD].rearrange("p (n m b) -> p n m b", n=4, b=NB)[:, :, :, b]
                    for j in range(2):
                        then_wait(dve.tensor_scalar(mod[b][:, 2 * j, :], col[:, 2 * j, :], 1.0, None, ALU.add))
                        then_wait(dve.tensor_copy(mod[b][:, 2 * j + 1, :], col[:, 2 * j + 1, :]))
                dve.wait_ge(loaded, 64)
                for b in range(NB):
                    dve.wait_ge(rows_done, b + 1)
                    g = bank[2 + b][:, :].rearrange("p (n d) -> p n d", n=2)
                    dve.tensor_scalar(pos[:, :, :], g, 0.0, 2.0, ALU.is_ge, ALU.mult)
                    then_wait(dve.tensor_scalar(mag[:, :, :], g, -1.0, None, ALU.mult))
                    then_wait(dve.tensor_tensor(mag[:, :, :], mag[:, :, :], g, ALU.max))
                    then_wait(dve.tensor_scalar(mag[:, :, :], mag[:, :, :], 0.25, None, ALU.max))
                    then_wait(dve.scalar_tensor_tensor(pos[:, :, :], pos[:, :, :], -1.0, mag[:, :, :],
                                                       ALU.add, ALU.mult))
                    dve.tensor_copy(gate_b_row[b][:, :], pos[:, 1, :])
                    for n2 in range(2):
                        last = dve.tensor_tensor(gate_ln[:, b, n2, :], pos[:, 0, :], lnw[:, n2, :], ALU.mult)
                    then_wait(last)


def mixer(nc, sem, prime, t, mod, gate_ln, ident, minus_half, bank, x2_dram):
    with ExitStack() as ctx:
        def sb(name, shape, dt=F32):
            return ctx.enter_context(nc.sbuf_tensor(name, shape, dt))

        def both(name, shape, dt=F32):
            return [sb(f"{name}{b}", shape, dt) for b in range(NB)]

        counts = []

        def sems(name, per_step=None):
            pair = [sem(f"{name}{b}") for b in range(NB)]
            if per_step:
                counts.extend((s, per_step) for s in pair)
            return pair

        win = [sb(f"win_{h}", [P, KD, IN_COLS], F32R) for h in ("hi", "lo")]
        wout = [sb(f"wout_{h}", [P, KI, D], F32R) for h in ("hi", "lo")]
        wglu = [sb(f"wglu_{h}", [P, KD, 2 * D], F32R) for h in ("hi", "lo")]
        upto = sb("upto", [P, P])
        after = sb("after", [P, P])
        ones = sb("ones", [P, P])
        convw = sb("convw", [P, MC, TAPS])
        convb = sb("convb", [P, MC])
        dtb = sb("dtb", [P, CH, H])
        negA = sb("negA", [P, CH, H])
        dskip = sb("dskip", [P, KI])
        dskip_diag = sb("dskip_diag", [P, KI, P])
        glub = sb("glub", [P, 2 * KD])
        xt = both("xt", [P, CH, D])
        xr = both("xr", [P, CH, D])
        st1 = both("st1_", [P, CH, 6])
        mv1 = both("mv1_", [P, CH, 2])
        rs1 = both("rs1_", [P, CH])
        st = both("st", [P, CH, 6])
        mv = both("mv", [P, CH, 2])
        rs = both("rs", [P, CH])
        hT = both("hT", [P, KD, GROUP])
        hTh = both("hTh", [P, KD, GROUP], F32R)
        hTl = both("hTl", [P, KD, GROUP], F32R)
        zs = both("zs", [P, CH, DI])
        xc = both("xc", [P, MC, TAPS - 1 + GROUP])
        cv = both("cv", [P, MC, GROUP])
        dts = both("dts", [P, 8, CH, H])
        ex = both("ex", [P, 3, CH, H])
        xtok = both("xtok", [P, CH, DI])
        xdt = both("xdt", [P, CH, DI])
        xend = both("xend", [P, CH, DI])
        btok = both("btok", [P, CH, NS])
        dec = both("dec", [P, CH, H, P])
        gm = both("gm", [P, CH, P])
        state = both("state", [P, DI])
        yy = both("yy", [P, CH, DI])
        ss = both("ss", [P, CH])
        rr = both("rr", [P, CH])
        yTh = both("yTh", [P, KI, GROUP], F32R)
        yTl = both("yTl", [P, KI, GROUP], F32R)
        y1 = both("y1", [P, KD, GROUP])
        y1h = both("y1h", [P, KD, GROUP], F32R)
        y1l = both("y1l", [P, KD, GROUP], F32R)
        sg = both("sg", [P, KD, GROUP])
        half_a = both("half_a", [P, KD, GROUP])
        xo = both("xo", [P, CH, D])

        w_in, w_ready, w_hi, link = sems("w_in"), sem("w_ready"), sem("w_hi"), sem("w_link")
        with nc.Block() as block:
            raws = [cv[b][:, :, :].rearrange("p a b -> p (a b)") for b in range(NB)]
            pieces = []
            for k in range(KD):
                pieces.append((t["W_in"][:, k, :], IN_COLS, win[0][:, k, :], win[1][:, k, :]))
            pieces.append((t["W_out"], KI * D, wout[0][:, :, :].rearrange("p a b -> p (a b)"),
                           wout[1][:, :, :].rearrange("p a b -> p (a b)")))
            pieces.append((t["glu_w"], KD * 2 * D, wglu[0][:, :, :].rearrange("p a b -> p (a b)"),
                           wglu[1][:, :, :].rearrange("p a b -> p (a b)")))
            OUT_PIECE = 2
            consts = [(upto, "upto"), (after, "after"), (ones, "ones"), (convw, "conv_w"), (convb, "conv_b"),
                      (dtb, "dt_bias"), (negA, "A_log"), (dskip, "D_skip"), (glub, "glu_b"),
                      ]
            c_in = sem("c_in")
            rms = sg[0][:, 0, 0:KI]
            CONSTS = len(consts) + 1

            @block.sync
            def _(sp):
                for n, (src, cols, _, _) in enumerate(pieces):
                    if n >= 2:
                        sp.wait_ge(w_ready, n - 1)
                    sp.dma_start(raws[n % 2][:, 0:cols], src).then_inc(w_in[n % 2], 16)
                    if n == 1:
                        for dst, name in consts:
                            sp.dma_start(dst[tuple(slice(None) for _ in dst.shape)], t[name]).then_inc(c_in, 16)
                        sp.dma_start(rms, t["rms_w"]).then_inc(c_in, 16)
                        sp.wait_ge(c_in, 16 * CONSTS)

            @block.vector
            def _(dve):
                for n, (_, cols, hi, lo) in enumerate(pieces):
                    dve.wait_ge(w_in[n % 2], 16 * (n // 2 + 1))
                    raw = raws[n % 2][:, 0:cols]
                    if n == OUT_PIECE:
                        dve.wait_ge(c_in, 16 * CONSTS)
                        for k in range(KI):
                            last = dve.tensor_scalar(raw[:, k * D:(k + 1) * D], raw[:, k * D:(k + 1) * D],
                                                     rms[:, k:k + 1], None, ALU.mult)
                        last.then_inc(link, 1)
                        dve.wait_ge(link, 1)
                    dve.tensor_copy(hi, raw).then_inc(w_hi, 1)
                    dve.wait_ge(w_hi, n + 1)
                    dve.tensor_tensor(lo, raw, hi.bitcast(F32), ALU.subtract).then_inc(w_ready, 1)
                dve.tensor_scalar(glub[:, :], glub[:, :], 0.5, None, ALU.mult)
                for k in range(KI):
                    dve.tensor_scalar(dskip_diag[:, k, :], ident[:, :], dskip[:, k:k + 1], None, ALU.mult)

            @block.scalar
            def _(act):
                act.wait_ge(c_in, 16 * CONSTS)
                act.activation(negA[:, :, :], negA[:, :, :], ACT.Exp)

            @block.gpsimd
            def _(pool):
                for b in range(NB):
                    pool.memset(state[b][:, :], 0.0)
                    pool.memset(xc[b][:, :, GROUP:GROUP + TAPS - 1], 0.0)

        x_in = sems("x_in", 16)
        xr_in = sems("xr_in", 16)
        ln1 = sems("ln1", 3)
        root1 = sems("root1", 1)
        xn_done = sems("xn_done", 1)
        xnT_ps = sems("xnT_ps", 1)
        hT_done = sems("hT_done", 1)
        hTh_done = sems("hTh_done", 1)
        hTl_done = sems("hTl_done", 1)
        z_ps = sems("z_ps", CH)
        dt_ps = sems("dt_ps", 1)
        xbc_ps = sems("xbc_ps", 3)
        zs_done = sems("zs_done", CH)
        halo_done = sems("halo_done", 1)
        xc_done = sems("xc_done", 3)
        tap_done = sems("tap_done", MC * TAPS)
        xs_done = sems("xs_done", 3)
        dt_abs = sems("dt_abs", 1)
        dt_exp = sems("dt_exp", 1)
        dt_link = sems("dt_link", DT_LINKS)
        a_done = sems("a_done", 1)
        sums_ps = sems("sums_ps", 1)
        ex_done = sems("ex_done", 1)
        wend_done = sems("wend_done", 1)
        xT_ps = sems("xT_ps", CH)
        btg_ps = sems("btg_ps", 1)
        xtok_done = sems("xtok_done", CH)
        xdt_done = sems("xdt_done", CH)
        btok_done = sems("btok_done", 1)
        gm_done = sems("gm_done", 1)
        au_done = sems("au_done", CH)
        dec_ps = sems("dec_ps", CH)
        dec_done = sems("dec_done", CH)
        w_done = sems("w_done", CH)
        xend_done = sems("xend_done", CH)
        yin_ps = sems("yin_ps", CH)
        yst_ps = sems("yst_ps", CH)
        add_ps = sems("add_ps", CH)
        sdec_done = sems("sdec_done", CH)
        st_done = sems("st_done", CH)
        y1s_done = sems("y1s_done", CH)
        y2s_done = sems("y2s_done", CH)
        y4_done = sems("y4_done", CH)
        sq_done = sems("sq_done", CH)
        ms_done = sems("ms_done", CH)
        rr_done = sems("rr_done", CH)
        yn_done = sems("yn_done", CH)
        yT_ps = sems("yT_ps", CH)
        yTh_done = sems("yTh_done", CH)
        yTl_done = sems("yTl_done", CH)
        o_ps = sems("o_ps", 1)
        y1_done = sems("y1_done", 1)
        y1h_done = sems("y1h_done", 1)
        y1l_done = sems("y1l_done", 1)
        glu_ps = sems("glu_ps", 1)
        tanh_done = sems("tanh_done", 1)
        ag_done = sems("ag_done", 1)
        y2_done = sems("y2_done", 1)
        y2T_ps = sems("y2T_ps", 1)
        ln2 = sems("ln2", 3)
        root2 = sems("root2", 1)
        xb_done = sems("xb_done", 1)
        xo_link = sems("xo_link", 1)
        xo_done = sems("xo_done", 1)
        stored = sems("x2_stored", 16)

        prime(counts)
        held_dve = sem("held_dve")

        def Q(b, n):
            return bank[4 * b + n]

        def following(done):
            b, i = done
            return b, i + 1

        def halves(eng, first_only, half, second_only, tail_only, last_half=None):
            first_only((0, 1))
            half((1, 1), (0, 1), None)
            half((0, 2), (1, 1), (0, 1))
            with eng.Fori(2, STEPS) as i:
                half((1, i), (0, i), (1, i - 1))
                half((0, i + 1), (1, i), (0, i))
            (last_half or half)((1, STEPS), (0, STEPS), (1, STEPS - 1))
            second_only((1, STEPS), (0, STEPS))
            tail_only((1, STEPS))

        with nc.Block() as block:
            @block.sync
            def _(sp):
                def step(dram, b, i):
                    return dram[b, bass.ds(i - 1, 1)].rearrange("o p c d -> p (o c) d")

                def load_x(b, i):
                    sp.wait_ge(xnT_ps[b], i)
                    sp.dma_start(xt[b][:, :, :], step(t["x"], b, i)).then_inc(x_in[b], 16)

                def load_again(b, i):
                    sp.wait_ge(xo_done[b], i)
                    sp.dma_start(xr[b][:, :, :], step(t["x"], b, i)).then_inc(xr_in[b], 16)

                def store(b, i):
                    sp.wait_ge(xo_done[b], i + 1)
                    sp.dma_start(step(x2_dram, b, i), xo[b][:, :, :]).then_inc(stored[b], 16)

                def half(first, second, tail, more=True):
                    if tail:
                        store(*tail)
                    if second:
                        load_again(*second)
                        if more:
                            load_x(*following(second))

                for b in range(NB):
                    load_x(b, 1)
                halves(sp, lambda first: None, half, lambda second, tail: half(None, second, tail, False),
                       lambda tail: store(*tail), lambda first, second, tail: half(first, second, tail, False))
                for b in range(NB):
                    sp.wait_ge(stored[b], 16 * (STEPS + 1))

            @block.tensor
            def _(pe):
                def transpose_xn(b, i):
                    pe.wait_ge(xn_done[b], i + 1)
                    pe.wait_ge(tanh_done[b], i)
                    for k in range(KD):
                        for c in range(CH):
                            last = pe.transpose(Q(b, 0)[:, k * GROUP + c * P:k * GROUP + (c + 1) * P],
                                                xt[b][:, c, k * P:(k + 1) * P], ident[:, :])
                    last.then_inc(xnT_ps[b], 1)

                def project_dt_xbc(b, i):
                    pe.wait_ge(hTh_done[b], i + 1)
                    pe.wait_ge(hTl_done[b], i + 1)
                    pe.wait_ge(tanh_done[b], i)
                    for c in range(CH):
                        tok = slice(c * P, (c + 1) * P)
                        for k in range(KD):
                            last = split3(pe, Q(b, 3)[:, c * H:(c + 1) * H], hTh[b][:, k, tok], hTl[b][:, k, tok],
                                          win[0][:, k, IN_COLS - H:IN_COLS], win[1][:, k, IN_COLS - H:IN_COLS],
                                          k == 0, k == KD - 1)
                    last.then_inc(dt_ps[b], 1)
                    pe.wait_ge(yTl_done[b], CH * i)
                    for pair in range(MC // 2):
                        if pair == 2:
                            pe.wait_ge(xo_done[b], i)
                        for m in range(2):
                            col = DI + (2 * pair + m) * P
                            for k in range(KD):
                                last = split3(pe, Q(b, pair)[:, m * GROUP:(m + 1) * GROUP],
                                              win[0][:, k, col:col + P], win[1][:, k, col:col + P],
                                              hTh[b][:, k, :], hTl[b][:, k, :], k == 0, k == KD - 1)
                        last.then_inc(xbc_ps[b], 1)

                def project_z(b, i, c):
                    tok = slice(c * P, (c + 1) * P)
                    pe.wait_ge(xc_done[b], 3 * i + c + 1)
                    for k in range(KD):
                        last = split3(pe, Q(b, c)[:, :], hTh[b][:, k, tok], hTl[b][:, k, tok],
                                      win[0][:, k, 0:DI], win[1][:, k, 0:DI], k == 0, k == KD - 1)
                    last.then_inc(z_ps[b], 1)

                def sums(b, i):
                    pe.wait_ge(a_done[b], i + 1)
                    a = dts[b][:, 7, :, :]
                    for n, m in enumerate((upto, after, ones)):
                        last = pe.matmul(Q(b, 3)[:, 64 + n * CH * H:64 + (n + 1) * CH * H], m[:, :],
                                         a.rearrange("p c h -> p (c h)"), start=True, stop=True)
                    last.then_inc(sums_ps[b], 1)

                def x_by_token(b, i):
                    pe.wait_ge(xs_done[b], 3 * i + 2)
                    for c in range(CH):
                        pe.wait_ge(zs_done[b], CH * i + c + 1)
                        for m in range(KI):
                            last = pe.transpose(Q(b, c)[:, m * P:(m + 1) * P], cv[b][:, m, c * P:(c + 1) * P],
                                                ident[:, :])
                        last.then_inc(xT_ps[b], 1)

                def b_by_token(b, i):
                    pe.wait_ge(xs_done[b], 3 * i + 3)
                    pe.wait_ge(dec_done[b], CH * i + CH)
                    for c in range(CH):
                        tok = slice(c * P, (c + 1) * P)
                        pe.transpose(Q(b, 2)[:, tok], cv[b][:, KI, tok], ident[:, :])
                    for c in range(CH):
                        tok = slice(c * P, (c + 1) * P)
                        last = pe.matmul(Q(b, 2)[:, GROUP + c * P:GROUP + (c + 1) * P], cv[b][:, KI, tok],
                                         cv[b][:, KI + 1, tok], start=True, stop=True)
                    last.then_inc(btg_ps[b], 1)

                def exponents(b, i, c):
                    pe.wait_ge(au_done[b], CH * i + c + 1)
                    if c == 0:
                        pe.wait_ge(xc_done[b], 3 * i + 3)
                        pe.wait_ge(ex_done[b], i + 1)
                    else:
                        pe.wait_ge(dec_done[b], CH * i + c)
                    for half_heads in range(2):
                        last = pe.matmul(Q(b, 2 + half_heads)[:, :], after[:, :],
                                         dec[b][:, c, half_heads * 4:half_heads * 4 + 4, :].rearrange("p h i -> p (h i)"),
                                         start=True, stop=True)
                    last.then_inc(dec_ps[b], 1)

                def within(b, i, c):
                    pe.wait_ge(w_done[b], CH * i + c + 1)
                    pe.wait_ge(xdt_done[b], CH * i + c + 1)
                    pe.wait_ge(xtok_done[b], CH * i + c + 1)
                    for h in range(H):
                        pe.matmul(Q(b, c)[:, h * HD:(h + 1) * HD], dec[b][:, c, h, :],
                                  xdt[b][:, c, h * HD:(h + 1) * HD], start=(h == 0), stop=False,
                                  skip_group_check=True)
                    for m in range(KI):
                        last = pe.matmul(Q(b, c)[:, m * P:(m + 1) * P], cv[b][:, m, c * P:(c + 1) * P],
                                         dskip_diag[:, m, :], start=False, stop=(m == KI - 1),
                                         skip_group_check=True)
                    last.then_inc(yin_ps[b], 1)

                def from_state(b, i, c):
                    pe.wait_ge(st_done[b], CH * i + c)
                    if c == 0:
                        pe.wait_ge(gm_done[b], i + 1)
                    else:
                        pe.wait_ge(y1s_done[b], CH * i + c)
                    pe.matmul(Q(b, 2)[:, :], cv[b][:, KI + 1, c * P:(c + 1) * P], state[b][:, :],
                              start=True, stop=True).then_inc(yst_ps[b], 1)

                def state_add(b, i, c):
                    pe.wait_ge(xend_done[b], CH * i + c + 1)
                    pe.wait_ge(btok_done[b], i + 1)
                    pe.wait_ge(dec_done[b], CH * i + CH)
                    pe.matmul(Q(b, 3)[:, :], btok[b][:, c, :], xend[b][:, c, :],
                              start=True, stop=True).then_inc(add_ps[b], 1)

                def transpose_y(b, i):
                    for c in range(CH):
                        pe.wait_ge(yn_done[b], CH * i + c + 1)
                        pe.wait_ge(y2s_done[b], CH * i + c + 1)
                        for m in range(KI):
                            last = pe.transpose(Q(b, c)[:, m * P:(m + 1) * P], yy[b][:, c, m * P:(m + 1) * P],
                                                ident[:, :])
                        last.then_inc(yT_ps[b], 1)

                def project_out(b, i):
                    pe.wait_ge(yTh_done[b], CH * i + CH)
                    pe.wait_ge(yTl_done[b], CH * i + CH)
                    pe.wait_ge(y1s_done[b], CH * i + CH)
                    for m in range(KD):
                        for k in range(KI):
                            last = split3(pe, Q(b, 2)[:, m * GROUP:(m + 1) * GROUP],
                                          wout[0][:, k, m * P:(m + 1) * P], wout[1][:, k, m * P:(m + 1) * P],
                                          yTh[b][:, k, :], yTl[b][:, k, :], k == 0, k == KI - 1)
                    last.then_inc(o_ps[b], 1)

                def glu(b, i):
                    pe.wait_ge(y1h_done[b], i + 1)
                    pe.wait_ge(y1l_done[b], i + 1)
                    pe.wait_ge(st_done[b], CH * i + CH)
                    for m in range(2 * KD):
                        for k in range(KD):
                            last = split3(pe, Q(b, 0 if m < KD else 3)[:, m % KD * GROUP:(m % KD + 1) * GROUP],
                                          wglu[0][:, k, m * P:(m + 1) * P], wglu[1][:, k, m * P:(m + 1) * P],
                                          y1h[b][:, k, :], y1l[b][:, k, :], k == 0, k == KD - 1)
                    last.then_inc(glu_ps[b], 1)

                def transpose_y2(b, i):
                    pe.wait_ge(y2_done[b], i + 1)
                    pe.wait_ge(y1_done[b], i + 1)
                    for c in range(CH):
                        for k in range(KD):
                            last = pe.transpose(Q(b, 2)[:, c * D + k * P:c * D + (k + 1) * P],
                                                y1[b][:, k, c * P:(c + 1) * P], ident[:, :])
                    last.then_inc(y2T_ps[b], 1)

                def half(first, second, tail):
                    if tail:
                        transpose_y2(*tail)
                    if first:
                        transpose_xn(*first)
                    if second:
                        for c in range(CH):
                            from_state(*second, c)
                            state_add(*second, c)
                            within(*second, c)
                    if first:
                        project_dt_xbc(*first)
                    if second:
                        transpose_y(*second)
                    if first:
                        project_z(*first, 0)
                        project_z(*first, 1)
                        sums(*first)
                        exponents(*first, 0)
                    if second:
                        project_out(*second)
                    if first:
                        exponents(*first, 1)
                        x_by_token(*first)
                    if second:
                        glu(*second)
                    if first:
                        b_by_token(*first)

                halves(pe, lambda first: half(first, None, None), half,
                       lambda second, tail: half(None, second, tail), lambda tail: half(None, None, tail))

            @block.scalar
            def _(act):
                def modulate(b, i):
                    act.wait_ge(xnT_ps[b], i + 1)
                    act.wait_ge(y1_done[b], i)
                    act.wait_ge(xbc_ps[b], 3 * i)
                    for k in range(KD):
                        last = act.activation(hT[b][:, k, :], Q(b, 0)[:, k * GROUP:(k + 1) * GROUP], ACT.Identity,
                                              bias=mod[b][:, 1, k:k + 1], scale=mod[b][:, 0, k:k + 1])
                    last.then_inc(hT_done[b], 1)
                    for k in range(KD):
                        last = act.activation(hTh[b][:, k, :], Q(b, 0)[:, k * GROUP:(k + 1) * GROUP], ACT.Identity,
                                              bias=mod[b][:, 1, k:k + 1], scale=mod[b][:, 0, k:k + 1])
                    last.then_inc(hTh_done[b], 1)

                def silu_z(b, i):
                    for c in range(CH):
                        act.wait_ge(z_ps[b], CH * i + c + 1)
                        act.wait_ge(y4_done[b], CH * i)
                        act.activation(zs[b][:, c, :], Q(b, c)[:, :], ACT.Silu).then_inc(zs_done[b], 1)

                def copy_xbc(b, i, pair):
                    if pair == 0:
                        act.wait_ge(tap_done[b], MC * TAPS * i)
                        act.activation(xc[b][:, :, 0:TAPS - 1], xc[b][:, :, GROUP:GROUP + TAPS - 1],
                                       ACT.Copy).then_inc(halo_done[b], 1)
                        act.wait_ge(halo_done[b], i + 1)
                    act.wait_ge(xbc_ps[b], 3 * i + pair + 1)
                    act.activation(xc[b][:, 2 * pair:2 * pair + 2, TAPS - 1:],
                                   Q(b, pair)[:, :].rearrange("p (m t) -> p m t", m=2),
                                   ACT.Copy).then_inc(xc_done[b], 1)

                def silu_xbc(b, i, pair):
                    act.wait_ge(tap_done[b], MC * TAPS * i + 2 * TAPS * (pair + 1))
                    v = cv[b][:, 2 * pair:2 * pair + 2, :]
                    act.activation(v, v, ACT.Silu).then_inc(xs_done[b], 1)

                def exp_dt(b, i):
                    act.wait_ge(dt_abs[b], i + 1)
                    act.activation(dts[b][:, 2, :, :], dts[b][:, 1, :, :], ACT.Exp, scale=-1.0).then_inc(dt_exp[b], 1)

                def exp_sums(b, i):
                    act.wait_ge(sums_ps[b], i + 1)
                    act.wait_ge(sdec_done[b], CH * i)
                    act.wait_ge(wend_done[b], i)
                    act.wait_ge(y1s_done[b], CH * i)
                    act.activation(ex[b][:, :, :, :].rearrange("p n c h -> p (n c h)"),
                                   Q(b, 3)[:, 64:64 + 3 * CH * H], ACT.Exp).then_inc(ex_done[b], 1)

                def copy_tokens(b, i):
                    for c in range(CH):
                        act.wait_ge(xT_ps[b], CH * i + c + 1)
                        act.wait_ge(xdt_done[b], CH * i)
                        act.wait_ge(xend_done[b], CH * i)
                        act.activation(xtok[b][:, c, :], Q(b, c)[:, :], ACT.Copy).then_inc(xtok_done[b], 1)

                def copy_b(b, i):
                    act.wait_ge(btg_ps[b], i + 1)
                    act.wait_ge(add_ps[b], CH * i)
                    act.activation(btok[b][:, :, :].rearrange("p c n -> p (c n)"), Q(b, 2)[:, 0:GROUP],
                                   ACT.Copy).then_inc(btok_done[b], 1)

                def decays(b, i, c):
                    act.wait_ge(dec_ps[b], CH * i + c + 1)
                    for half_heads in range(2):
                        last = act.activation(
                            dec[b][:, c, 4 * half_heads:4 * half_heads + 4, :].rearrange("p h i -> p (h i)"),
                            Q(b, 2 + half_heads)[:, :], ACT.Exp)
                    last.then_inc(dec_done[b], 1)

                def squares(b, i, c):
                    act.wait_ge(y4_done[b], CH * i + c + 1)
                    act.wait_ge(yT_ps[b], CH * i)
                    act.activation(xdt[b][:, c, :], yy[b][:, c, :], ACT.Square,
                                   accum_out=ss[b][:, c:c + 1]).then_inc(sq_done[b], 1)

                def split_yT(b, i):
                    for c in range(CH):
                        act.wait_ge(yT_ps[b], CH * i + c + 1)
                        act.wait_ge(o_ps[b], i)
                        act.activation(yTh[b][:, :, c * P:(c + 1) * P],
                                       Q(b, c)[:, :].rearrange("p (k t) -> p k t", k=KI),
                                       ACT.Copy).then_inc(yTh_done[b], 1)

                def split_y1(b, i):
                    act.wait_ge(y1_done[b], i + 1)
                    act.wait_ge(glu_ps[b], i)
                    act.activation(y1h[b][:, :, :], y1[b][:, :, :], ACT.Copy).then_inc(y1h_done[b], 1)

                def halve_and_tanh(b, i):
                    act.wait_ge(glu_ps[b], i + 1)
                    act.wait_ge(ag_done[b], i)
                    for m in range(KD):
                        act.activation(half_a[b][:, m, :], Q(b, 0)[:, m * GROUP:(m + 1) * GROUP], ACT.Identity,
                                       bias=glub[:, m:m + 1], scale=0.5)
                    for m in range(KD):
                        last = act.activation(sg[b][:, m, :], Q(b, 3)[:, m * GROUP:(m + 1) * GROUP], ACT.Tanh,
                                              bias=glub[:, KD + m:KD + m + 1], scale=0.5)
                    last.then_inc(tanh_done[b], 1)

                def half(first, second, tail):
                    if first:
                        modulate(*first)
                    if second:
                        squares(*second, 0)
                        squares(*second, 1)
                    if first:
                        exp_dt(*first)
                        for pair in range(MC // 2):
                            copy_xbc(*first, pair)
                    if second:
                        split_yT(*second)
                    if first:
                        silu_z(*first)
                        silu_xbc(*first, 0)
                        exp_sums(*first)
                        decays(*first, 0)
                    if second:
                        split_y1(*second)
                    if first:
                        silu_xbc(*first, 1)
                        silu_xbc(*first, 2)
                        decays(*first, 1)
                        copy_tokens(*first)
                    if second:
                        halve_and_tanh(*second)
                    if first:
                        copy_b(*first)

                halves(act, lambda first: half(first, None, None), half,
                       lambda second, tail: half(None, second, tail), lambda tail: None)

            @block.vector
            def _(dve):
                def norm1(b, i):
                    dve.wait_ge(x_in[b], 16 * (i + 1))
                    for c in range(CH):
                        last = dve.bn_stats(st1[b][:, c, :], xt[b][:, c, :])
                    last.then_inc(ln1[b], 1)
                    dve.wait_ge(ln1[b], 3 * i + 1)
                    stand_alone(dve, held_dve)
                    for c in range(CH):
                        last = dve.bn_aggr(mv1[b][:, c, :], st1[b][:, c, :])
                    last.then_inc(ln1[b], 1)
                    dve.wait_ge(ln1[b], 3 * i + 2)
                    dve.tensor_scalar(rs1[b][:, :], mv1[b][:, :, 1], EPS, None, ALU.add).then_inc(ln1[b], 1)

                def apply1(b, i):
                    dve.wait_ge(root1[b], i + 1)
                    for c in range(CH):
                        last = dve.tensor_scalar(xt[b][:, c, :], xt[b][:, c, :], mv1[b][:, c, 0:1],
                                                 rs1[b][:, c:c + 1], ALU.subtract, ALU.mult)
                    last.then_inc(xn_done[b], 1)

                def conv(b, i, pair, between=lambda step: None):
                    n = MC * TAPS * i
                    if pair == 0:
                        dve.wait_ge(halo_done[b], i + 1)
                        dve.wait_ge(yst_ps[b], CH * i)
                        dve.wait_ge(yin_ps[b], CH * i)
                    dve.wait_ge(xc_done[b], 3 * i + pair + 1)
                    for tap in range(TAPS):
                        for m in (2 * pair, 2 * pair + 1):
                            src = xc[b][:, m, tap:tap + GROUP]
                            w = convw[:, m, tap:tap + 1]
                            if tap == 0:
                                last = dve.tensor_scalar(cv[b][:, m, :], src, w, convb[:, m:m + 1],
                                                         ALU.mult, ALU.add)
                            else:
                                dve.wait_ge(tap_done[b], n + (pair * TAPS + tap - 1) * 2 + m % 2 + 1)
                                last = dve.scalar_tensor_tensor(cv[b][:, m, :], src, w, cv[b][:, m, :],
                                                                ALU.mult, ALU.add)
                            last.then_inc(tap_done[b], 1)
                            between(tap * 2 + m % 2)

                def softplus_head(b, i):
                    v, size = dts[b][:, 0, :, :], dts[b][:, 1, :, :]
                    dve.wait_ge(dt_ps[b], i + 1)
                    dve.wait_ge(xdt_done[b], CH * i)
                    dve.wait_ge(au_done[b], CH * i)
                    dve.wait_ge(xend_done[b], CH * i)
                    dve.wait_ge(sums_ps[b], i)
                    dve.tensor_tensor(v, Q(b, 3)[:, 0:CH * H].rearrange("p (c h) -> p c h", c=CH),
                                      dtb[:, :, :], ALU.add).then_inc(dt_link[b], 1)
                    dve.wait_ge(dt_link[b], DT_LINKS * i + 1)
                    dve.scalar_tensor_tensor(size, v, -1.0, v, ALU.mult, ALU.max).then_inc(dt_abs[b], 1)

                def softplus_step(b, i, n):
                    v, _, u, s, s2, acc, dt, a = (dts[b][:, k, :, :] for k in range(8))
                    if n == 0:
                        dve.wait_ge(dt_exp[b], i + 1)
                    else:
                        dve.wait_ge(dt_link[b], DT_LINKS * i + 1 + n)
                    if n == 0:
                        last = dve.tensor_scalar(s, u, 2.0, None, ALU.add)
                    elif n == 1:
                        last = dve.reciprocal(s, s)
                    elif n == 2:
                        last = dve.tensor_tensor(s, s, u, ALU.mult)
                    elif n == 3:
                        last = dve.tensor_tensor(s2, s, s, ALU.mult)
                    elif n == 4:
                        last = dve.tensor_scalar(acc, s2, SERIES[0], None, ALU.mult)
                    elif n < 5 + len(SERIES) - 2:
                        last = dve.scalar_tensor_tensor(acc, acc, SERIES[n - 4], s2, ALU.add, ALU.mult)
                    elif n == DT_LINKS - 4:
                        last = dve.scalar_tensor_tensor(acc, acc, 1.0, s, ALU.add, ALU.mult)
                    elif n == DT_LINKS - 3:
                        last = dve.tensor_scalar(v, v, 0.0, None, ALU.max)
                    elif n == DT_LINKS - 2:
                        last = dve.scalar_tensor_tensor(dt, acc, 2.0, v, ALU.mult, ALU.add)
                    else:
                        dve.scalar_tensor_tensor(a, dt, -1.0, negA[:, :, :], ALU.mult, ALU.mult
                                                 ).then_inc(a_done[b], 1)
                        return
                    last.then_inc(dt_link[b], 1)

                def mask_bc(b, i):
                    dve.wait_ge(btok_done[b], i + 1)
                    dve.wait_ge(w_done[b], CH * i)
                    dve.tensor_tensor(gm[b][:, :, :], Q(b, 2)[:, GROUP:2 * GROUP].rearrange("p (c t) -> p c t", c=CH),
                                      upto[:, :].unsqueeze(1).to_broadcast([P, CH, P]),
                                      ALU.mult).then_inc(gm_done[b], 1)

                def times_decay(b, i, c):
                    dve.wait_ge(dec_done[b], CH * i + c + 1)
                    dve.wait_ge(gm_done[b], i + 1)
                    dve.tensor_tensor(dec[b][:, c, :, :], dec[b][:, c, :, :],
                                      gm[b][:, c, :].unsqueeze(1).to_broadcast([P, H, P]),
                                      ALU.mult).then_inc(w_done[b], 1)

                def scale_from_state(b, i, c):
                    dve.wait_ge(yst_ps[b], CH * i + c + 1)
                    dve.wait_ge(ex_done[b], i + 1)
                    dve.wait_ge(yT_ps[b], CH * i)
                    dve.tensor_tensor(yy[b][:, c, :].rearrange("p (h e) -> p h e", h=H),
                                      Q(b, 2)[:, :].rearrange("p (h e) -> p h e", h=H),
                                      ex[b][:, 0, c, :].unsqueeze(2).to_broadcast([P, H, HD]),
                                      ALU.mult).then_inc(y1s_done[b], 1)

                def add_within(b, i, c):
                    dve.wait_ge(y1s_done[b], CH * i + c + 1)
                    dve.wait_ge(yin_ps[b], CH * i + c + 1)
                    dve.tensor_tensor(yy[b][:, c, :], yy[b][:, c, :], Q(b, c)[:, :],
                                      ALU.add).then_inc(y2s_done[b], 1)

                def new_state(b, i, c):
                    dve.wait_ge(add_ps[b], CH * i + c + 1)
                    dve.wait_ge(sdec_done[b], CH * i + c + 1)
                    dve.tensor_tensor(state[b][:, :], state[b][:, :], Q(b, 3)[:, :], ALU.add).then_inc(st_done[b], 1)

                def mean_square(b, i, c):
                    dve.wait_ge(sq_done[b], CH * i + c + 1)
                    dve.tensor_scalar(rr[b][:, c:c + 1], ss[b][:, c:c + 1], 1.0 / DI, EPS, ALU.mult,
                                      ALU.add).then_inc(ms_done[b], 1)

                def norm_y(b, i, c):
                    dve.wait_ge(rr_done[b], CH * i + c + 1)
                    dve.tensor_scalar(yy[b][:, c, :], yy[b][:, c, :], rr[b][:, c:c + 1], None,
                                      ALU.mult).then_inc(yn_done[b], 1)

                def split_yT(b, i):
                    for c in range(CH):
                        dve.wait_ge(yTh_done[b], CH * i + c + 1)
                        tok = slice(c * P, (c + 1) * P)
                        dve.tensor_tensor(yTl[b][:, :, tok], Q(b, c)[:, :].rearrange("p (k t) -> p k t", k=KI),
                                          yTh[b][:, :, tok].bitcast(F32), ALU.subtract).then_inc(yTl_done[b], 1)

                def add_h(b, i):
                    dve.wait_ge(o_ps[b], i + 1)
                    dve.wait_ge(y2T_ps[b], i)
                    dve.wait_ge(hT_done[b], i + 1)
                    dve.tensor_tensor(y1[b][:, :, :], Q(b, 2)[:, :].rearrange("p (k t) -> p k t", k=KD),
                                      hT[b][:, :, :], ALU.add).then_inc(y1_done[b], 1)

                def gated(b, i):
                    dve.wait_ge(tanh_done[b], i + 1)
                    dve.scalar_tensor_tensor(sg[b][:, :, :], sg[b][:, :, :], 1.0, half_a[b][:, :, :],
                                             ALU.add, ALU.mult).then_inc(ag_done[b], 1)
                    dve.wait_ge(ag_done[b], i + 1)
                    dve.wait_ge(y1l_done[b], i + 1)
                    dve.tensor_tensor(y1[b][:, :, :], y1[b][:, :, :], sg[b][:, :, :], ALU.add).then_inc(y2_done[b], 1)

                def norm2(b, i):
                    dve.wait_ge(y2T_ps[b], i + 1)
                    y = Q(b, 2)[:, :].rearrange("p (c d) -> p c d", c=CH)
                    for c in range(CH):
                        last = dve.bn_stats(st[b][:, c, :], y[:, c, :])
                    last.then_inc(ln2[b], 1)
                    dve.wait_ge(ln2[b], 3 * i + 1)
                    stand_alone(dve, held_dve)
                    for c in range(CH):
                        last = dve.bn_aggr(mv[b][:, c, :], st[b][:, c, :])
                    last.then_inc(ln2[b], 1)
                    dve.wait_ge(ln2[b], 3 * i + 2)
                    dve.tensor_scalar(rs[b][:, :], mv[b][:, :, 1], EPS, None, ALU.add).then_inc(ln2[b], 1)

                def apply2(b, i):
                    y = Q(b, 2)[:, :].rearrange("p (c d) -> p c d", c=CH)
                    dve.wait_ge(stored[b], 16 * i)
                    for c in range(CH):
                        last = dve.scalar_tensor_tensor(xo[b][:, c, :], y[:, c, :], mv[b][:, c, 0:1],
                                                        gate_ln[:, b, 0, :], ALU.subtract, ALU.mult)
                    last.then_inc(xo_link[b], 1)
                    dve.wait_ge(xo_link[b], i + 1)
                    dve.wait_ge(root2[b], i + 1)
                    dve.wait_ge(xb_done[b], i + 1)
                    for c in range(CH):
                        last = dve.scalar_tensor_tensor(xo[b][:, c, :], xo[b][:, c, :], rs[b][:, c:c + 1],
                                                        xr[b][:, c, :], ALU.mult, ALU.add)
                    last.then_inc(xo_done[b], 1)

                def half(first, second, tail, more=True):
                    if second:
                        new_state(*second, 0)
                        scale_from_state(*second, 0)
                    if tail:
                        norm2(*tail)
                    if second:
                        add_within(*second, 0)
                        scale_from_state(*second, 1)
                        new_state(*second, 1)
                    if tail:
                        apply2(*tail)
                    if second:
                        add_within(*second, 1)
                    if first:
                        softplus_head(*first)
                    if second:
                        mean_square(*second, 0)
                        norm_y(*second, 0)
                    if first:
                        for step in range(DT_LINKS // 2):
                            softplus_step(*first, step)
                    if second:
                        mean_square(*second, 1)
                        norm_y(*second, 1)
                    if first:
                        for step in range(DT_LINKS // 2, DT_LINKS):
                            softplus_step(*first, step)
                        conv(*first, 0)
                    if second:
                        split_yT(*second)
                    if first:
                        conv(*first, 1)
                        conv(*first, 2, lambda step: add_h(*second) if second and step == 3 else None)
                    elif second:
                        add_h(*second)
                    if more:
                        norm1(*following(second))
                    if second:
                        gated(*second)
                    if more:
                        apply1(*following(second))
                    if first:
                        mask_bc(*first)
                        times_decay(*first, 0)
                        times_decay(*first, 1)

                for b in range(NB):
                    norm1(b, 1)
                    apply1(b, 1)
                halves(dve, lambda first: half(first, None, None, False), half,
                       lambda second, tail: half(None, second, tail, False),
                       lambda tail: half(None, None, tail, False),
                       lambda first, second, tail: half(first, second, tail, False))

            @block.gpsimd
            def _(pool):
                def root(out, n):
                    return pool.tensor_tensor(out, out, minus_half[:, 0:n], ALU.pow)

                def root_norm1(b, i):
                    pool.wait_ge(ln1[b], 3 * i + 3)
                    root(rs1[b][:, :], CH).then_inc(root1[b], 1)

                def root_norm2(b, i):
                    pool.wait_ge(ln2[b], 3 * i + 3)
                    root(rs[b][:, :], CH).then_inc(root2[b], 1)

                def root_y(b, i, c):
                    pool.wait_ge(ms_done[b], CH * i + c + 1)
                    root(rr[b][:, c:c + 1], 1).then_inc(rr_done[b], 1)

                def split_h(b, i):
                    pool.wait_ge(hT_done[b], i + 1)
                    pool.wait_ge(hTh_done[b], i + 1)
                    pool.tensor_tensor(hTl[b][:, :, :], hT[b][:, :, :], hTh[b][:, :, :].bitcast(F32),
                                       ALU.subtract).then_inc(hTl_done[b], 1)

                def mask_a(b, i, c):
                    pool.wait_ge(a_done[b], i + 1)
                    pool.wait_ge(yin_ps[b], CH * i)
                    pool.tensor_tensor(dec[b][:, c, :, :], upto[:, :].unsqueeze(1).to_broadcast([P, H, P]),
                                       dts[b][:, 7, c, :].unsqueeze(2).to_broadcast([P, H, P]),
                                       ALU.mult).then_inc(au_done[b], 1)

                def end_weights(b, i):
                    pool.wait_ge(ex_done[b], i + 1)
                    pool.tensor_tensor(dts[b][:, 1, :, :], dts[b][:, 6, :, :], ex[b][:, 1, :, :],
                                       ALU.mult).then_inc(wend_done[b], 1)

                def times_dt(b, i, c):
                    pool.wait_ge(xtok_done[b], CH * i + c + 1)
                    pool.wait_ge(sq_done[b], CH * i)
                    pool.tensor_tensor(xdt[b][:, c, :].rearrange("p (h e) -> p h e", h=H),
                                       xtok[b][:, c, :].rearrange("p (h e) -> p h e", h=H),
                                       dts[b][:, 6, c, :].unsqueeze(2).to_broadcast([P, H, HD]),
                                       ALU.mult).then_inc(xdt_done[b], 1)

                def times_end(b, i, c):
                    pool.wait_ge(wend_done[b], i + 1)
                    pool.wait_ge(add_ps[b], CH * i)
                    pool.tensor_tensor(xend[b][:, c, :].rearrange("p (h e) -> p h e", h=H),
                                       xtok[b][:, c, :].rearrange("p (h e) -> p h e", h=H),
                                       dts[b][:, 1, c, :].unsqueeze(2).to_broadcast([P, H, HD]),
                                       ALU.mult).then_inc(xend_done[b], 1)

                def decay_state(b, i, c):
                    pool.wait_ge(yst_ps[b], CH * i + c + 1)
                    s = state[b][:, :].rearrange("p (h e) -> p h e", h=H)
                    pool.tensor_tensor(s, s, ex[b][:, 2, c, :].unsqueeze(2).to_broadcast([P, H, HD]),
                                       ALU.mult).then_inc(sdec_done[b], 1)

                def gate_y(b, i, c):
                    y = yy[b][:, c, :]
                    pool.wait_ge(y2s_done[b], CH * i + c + 1)
                    pool.tensor_tensor(y, y, zs[b][:, c, :], ALU.mult).then_inc(y4_done[b], 1)

                def split_y1(b, i):
                    pool.wait_ge(y1h_done[b], i + 1)
                    pool.wait_ge(y1_done[b], i + 1)
                    pool.tensor_tensor(y1l[b][:, :, :], y1[b][:, :, :], y1h[b][:, :, :].bitcast(F32),
                                       ALU.subtract).then_inc(y1l_done[b], 1)

                def shift_x(b, i):
                    pool.wait_ge(xr_in[b], 16 * (i + 1))
                    pool.tensor_tensor(xr[b][:, :, :], xr[b][:, :, :],
                                       gate_ln[:, b, 1, :].unsqueeze(1).to_broadcast([P, CH, D]),
                                       ALU.add).then_inc(xb_done[b], 1)

                def half(first, second, tail, more=True):
                    if second:
                        decay_state(*second, 0)
                    if first:
                        split_h(*first)
                    if tail:
                        root_norm2(*tail)
                    if second:
                        gate_y(*second, 0)
                        decay_state(*second, 1)
                        root_y(*second, 0)
                        gate_y(*second, 1)
                        root_y(*second, 1)
                    if first:
                        mask_a(*first, 0)
                        mask_a(*first, 1)
                    if second:
                        shift_x(*second)
                        split_y1(*second)
                    if first:
                        end_weights(*first)
                        for c in range(CH):
                            times_dt(*first, c)
                    if more:
                        root_norm1(*following(second))
                    if first:
                        for c in range(CH):
                            times_end(*first, c)

                for b in range(NB):
                    root_norm1(b, 1)
                halves(pool, lambda first: half(first, None, None, False), half,
                       lambda second, tail: half(None, second, tail, False),
                       lambda tail: half(None, None, tail, False),
                       lambda first, second, tail: half(first, second, tail, False))


def experts(nc, sem, prime, t, mod, gate_b_row, ident, minus_half, bank, x2_dram, out):
    ALL = NE + 1
    GROUPS = NB * MSTEPS
    with ExitStack() as ctx:
        def sb(name, shape, dt=F32):
            return ctx.enter_context(nc.sbuf_tensor(name, shape, dt))

        def two(name, shape, dt=F32):
            return [sb(f"{name}{b}", shape, dt) for b in range(2)]

        EW = KD * 2 * INTER + D
        wh = sb("wh", [P, ALL, EW], F32R)
        wl = sb("wl", [P, ALL, EW], F32R)
        gatew = sb("gatew", [P, KD, NE])
        gateb = sb("gateb", [P, MT, NE])
        pick_raw = sb("pick_raw", [2 * NE, NE, P])
        pick = sb("pick", [2 * NE, NE, P], F32R)
        x2 = sb("x2", [P, MT, D])
        st = sb("mst", [P, MT, 6])
        mv = sb("mmv", [P, MT, 2])
        rs = sb("mrs", [P, MT])
        hT = sb("mhT", [P, KD, MGROUP])
        hh = two("mhh", [P, KD, MGROUP], F32R)
        hl = two("mhl", [P, KD, MGROUP], F32R)
        score = sb("score", [P, MT, NE])
        biased = sb("biased", [P, MT, NE])
        top = sb("top", [P, MT, 8])
        best = sb("best", [P, MT, 8])
        rest = sb("rest", [P, MT, NE])
        wsum = sb("wsum", [P, MT])
        comb = sb("comb", [P, MT, NE])
        comb_hi = sb("comb_hi", [P, MT, NE], F32R)
        comb2 = sb("comb2", [P, MT, 2 * NE])
        combT = two("combT", [2 * NE, MGROUP], F32R)
        gs = two("gs", [P, MGROUP])
        ff = two("ff", [P, MGROUP])
        fh = two("fh", [P, MGROUP], F32R)
        fl = two("fl", [P, MGROUP], F32R)
        xres = sb("xres", [P, MT, D])
        yo = sb("yo", [P, MT, D])

        if True:
            raw = [hT[:, :, :].rearrange("p k t -> p (k t)")[:, 0:EW],
                   x2[:, :, :].rearrange("p k t -> p (k t)")[:, 0:EW],
                   xres[:, :, :].rearrange("p k t -> p (k t)")[:, 0:EW],
                   yo[:, :, :].rearrange("p k t -> p (k t)")[:, 0:EW]]
            raw_in = [sem(f"ew_in{r}") for r in range(len(raw))]
            hi_done = sem("ew_hi")
            lo_done = sem("ew_lo")
            k_in = sem("k_in")
            with nc.Block() as block:
                @block.sync
                def _(sp):
                    sp.dma_start(gatew[:, :, :], t["gate_w"]).then_inc(k_in, 16)
                    sp.dma_start(gateb[:, :, :], t["gate_b"]).then_inc(k_in, 16)
                    sp.dma_start(pick_raw[:, :, :], t["pick"]).then_inc(k_in, 16)
                    for e in range(ALL):
                        if e >= len(raw):
                            sp.wait_ge(lo_done, e - len(raw) + 1)
                        sp.dma_start(raw[e % len(raw)], t["experts"][e]).then_inc(raw_in[e % len(raw)], 16)
                    sp.wait_ge(k_in, 48)

                @block.scalar
                def _(act):
                    for e in range(ALL):
                        act.wait_ge(raw_in[e % len(raw)], 16 * (e // len(raw) + 1))
                        act.activation(wh[:, e, :], raw[e % len(raw)], ACT.Copy).then_inc(hi_done, 1)

                @block.vector
                def _(dve):
                    dve.wait_ge(k_in, 48)
                    dve.tensor_copy(pick[:, :, :], pick_raw[:, :, :])
                    dve.memset(best[:, :, :], 3.0e38)
                    for e in range(ALL):
                        dve.wait_ge(hi_done, e + 1)
                        dve.tensor_tensor(wl[:, e, :], raw[e % len(raw)], wh[:, e, :].bitcast(F32),
                                          ALU.subtract).then_inc(lo_done, 1)

        def w13(half, e, k, gate):
            w = (wh, wl)[half]
            return w[:, e, k * 2 * INTER + (1 - gate) * INTER:k * 2 * INTER + (2 - gate) * INTER]

        def w2(half, e):
            return (wh, wl)[half][:, e, KD * 2 * INTER:EW]

        GATE, UP = (bank[0], bank[1]), (bank[2], bank[3])
        ROUTE, PREP = bank[4], bank[5]
        ACC = (bank[6], bank[7])

        ROUTE_LINKS = 13
        counts = []

        def counted(name, per_group):
            counts.append((sem(name), per_group))
            return counts[-1][0]

        x2_in = counted("x2_in", 16)
        ln = counted("mln", 3)
        mroot = counted("mroot", 1)
        n_done = counted("n_done", 1)
        nT_ps = counted("nT_ps", KD)
        mh_done = counted("mh_done", KD)
        mhh_done = counted("mhh_done", KD)
        mhl_done = counted("mhl_done", KD)
        logit_ps = counted("logit_ps", 1)
        tanh_done = counted("tanh_done", 1)
        route = counted("route", ROUTE_LINKS)
        comb_done = counted("comb_done", 1)
        combT_ps = counted("combT_ps", 1)
        combT_done = counted("combT_done", 1)
        gate_ps = counted("gate_ps", ALL)
        up_ps = counted("up_ps", ALL)
        gs_done = counted("gs_done", ALL)
        gc_done = counted("gc_done", NE)
        ff_done = counted("ff_done", ALL)
        fh_done = counted("fh_done", ALL)
        fl_done = counted("fl_done", ALL)
        down_ps = counted("down_ps", ALL)
        scaled = counted("scaled", 1)
        res_in = counted("res_in", 16)
        yo_done2 = counted("yo_done2", 1)
        out_stored = counted("out_stored", 16)

        prime(counts)
        held_dve = sem("mheld_dve")

        def x2_rows(b, j):
            return x2_dram[b, bass.ds(j * (MT // CH), MT // CH)].rearrange("s p c d -> p s c d")

        def tiles(ap):
            return ap.rearrange("p (s c) d -> p s c d", c=CH)

        def walk(eng, prepare_first, group):
            prepare_first()
            group(1, 0, 0, first=True)
            with eng.Fori(0, MSTEPS - 1) as i:
                group(2 * i + 2, 1, i)
                group(2 * i + 3, 0, i + 1)
            group(GROUPS, 1, MSTEPS - 1, last=True)

        with nc.Block() as block:
            @block.sync
            def _(sp):
                def load(n, b, j):
                    sp.wait_ge(nT_ps, KD * n)
                    sp.dma_start(tiles(x2[:, :, :]), x2_rows(b, j)).then_inc(x2_in, 16)

                def store(n, b, j):
                    sp.wait_ge(yo_done2, n + 1)
                    sp.dma_start(out[b, bass.ds(j * MGROUP, MGROUP), :].rearrange("(c p) d -> p c d", p=P),
                                 yo[:, :, :]).then_inc(out_stored, 16)

                def group(n, b, j, first=False, last=False):
                    if not last:
                        load(n + 1, 1 - b, j + b)
                    if not first:
                        store(n - 1, 1 - b, j - 1 + b)
                    sp.dma_start(tiles(xres[:, :, :]), x2_rows(b, j)).then_inc(res_in, 16)
                    if last:
                        store(n, b, j)

                walk(sp, lambda: load(1, 0, 0), group)
                sp.wait_ge(out_stored, 16 * (GROUPS + 1))

            @block.tensor
            def _(pe):
                def transpose_n(k, n):
                    if k == 0:
                        pe.wait_ge(n_done, n + 1)
                        pe.wait_ge(combT_done, n)
                    else:
                        pe.wait_ge(mhh_done, KD * n + k)
                    for c in range(MT):
                        last = pe.transpose(PREP[:, c * P:(c + 1) * P], x2[:, c, k * P:(k + 1) * P], ident[:, :])
                    last.then_inc(nT_ps, 1)

                def logits(n):
                    pe.wait_ge(mh_done, KD * n + KD)
                    pe.wait_ge(mhh_done, KD * n + KD)
                    for c in range(MT):
                        for k in range(KD):
                            last = pe.matmul(PREP[:, c * NE:(c + 1) * NE], hT[:, k, c * P:(c + 1) * P],
                                             gatew[:, k, :], start=(k == 0), stop=(k == KD - 1))
                    last.then_inc(logit_ps, 1)

                def transpose_comb(n):
                    pe.wait_ge(comb_done, n + 1)
                    for c in range(MT):
                        last = pe.transpose(PREP[0:2 * NE, c * P:(c + 1) * P], comb2[:, c, :], ident[:, :])
                    last.then_inc(combT_ps, 1)

                def prepare(slot, n):
                    if slot in (2, 4):
                        transpose_n(slot // 2 - 1, n)
                    if slot == 6:
                        logits(n)
                    if slot == 12:
                        transpose_comb(n)

                def up(e, n, b):
                    s = n * ALL + e
                    if e == 0:
                        pe.wait_ge(mhh_done, KD * n + KD)
                        pe.wait_ge(mhl_done, KD * n + KD)
                        pe.wait_ge(combT_done, n + 1)
                    par = e % 2
                    if e >= 2:
                        pe.wait_ge(ff_done, s - 1)
                    else:
                        pe.wait_ge(ff_done, n * ALL)
                    for k in range(KD):
                        last = split3(pe, GATE[par][:, :], w13(0, e, k, 1), w13(1, e, k, 1),
                                      hh[b][:, k, :], hl[b][:, k, :], k == 0, k == KD - 1)
                    last.then_inc(gate_ps, 1)
                    for k in range(KD):
                        last = split3(pe, UP[par][:, :], w13(0, e, k, 0), w13(1, e, k, 0),
                                      hh[b][:, k, :], hl[b][:, k, :], k == 0, k == KD - 1)
                    if e < NE:
                        pe.wait_ge(gc_done, n * NE + e)
                        last = pe.matmul(ROUTE[:, :], pick[:, e, :], combT[b][:, :], start=True, stop=True)
                    last.then_inc(up_ps, 1)

                def down(e, n):
                    s = n * ALL + e
                    pe.wait_ge(fh_done, s + 1)
                    pe.wait_ge(fl_done, s + 1)
                    if e == 0:
                        pe.wait_ge(scaled, n)
                    for c in range(MT):
                        tok = slice(c * P, (c + 1) * P)
                        last = split3(pe, ACC[c // 2][:, c % 2 * D:(c % 2 + 1) * D], fh[e % 2][:, tok],
                                      fl[e % 2][:, tok], w2(0, e), w2(1, e), e == 0 and c % 2 == 0, e == ALL - 1)
                    last.then_inc(down_ps, 1)

                def group(n, b, j, first=False, last=False):
                    for e in range(ALL):
                        up(e, n, b)
                        if e > 0:
                            down(e - 1, n)
                        elif not first:
                            down(ALL - 1, n - 1)
                        if not last:
                            prepare(e, n + 1)
                    if last:
                        down(ALL - 1, n)

                def prepare_first():
                    for slot in range(ALL):
                        prepare(slot, 1)

                walk(pe, prepare_first, group)

            @block.scalar
            def _(act):
                def modulate(k, n, b):
                    act.wait_ge(nT_ps, KD * n + k + 1)
                    act.wait_ge(logit_ps, n)
                    act.wait_ge(mhl_done, KD * n + k)
                    args = dict(bias=mod[b][:, 3, k:k + 1], scale=mod[b][:, 2, k:k + 1])
                    act.activation(hT[:, k, :], PREP[:, :], ACT.Identity, **args).then_inc(mh_done, 1)
                    act.activation(hh[b][:, k, :], PREP[:, :], ACT.Identity, **args).then_inc(mhh_done, 1)

                def prepare(slot, n, b):
                    if slot in (3, 5):
                        modulate(slot // 2 - 1, n, b)
                    if slot == 7:
                        act.wait_ge(logit_ps, n + 1)
                        act.wait_ge(comb_done, n)
                        act.activation(score[:, :, :].rearrange("p c e -> p (c e)"), PREP[:, 0:MT * NE],
                                       ACT.Tanh, scale=0.5).then_inc(tanh_done, 1)
                    if slot == 13:
                        act.wait_ge(combT_ps, n + 1)
                        act.activation(combT[b][:, :], PREP[0:2 * NE, :], ACT.Copy).then_inc(combT_done, 1)

                def silu_gate(e, n):
                    s = n * ALL + e
                    act.wait_ge(gate_ps, s + 1)
                    if e >= 2:
                        act.wait_ge(ff_done, s - 1)
                    else:
                        act.wait_ge(ff_done, n * ALL)
                    act.activation(gs[e % 2][:, :], GATE[e % 2][:, :], ACT.Silu).then_inc(gs_done, 1)

                def hi(e, n):
                    s = n * ALL + e
                    act.wait_ge(ff_done, s + 1)
                    if e >= 2:
                        act.wait_ge(down_ps, s - 1)
                    else:
                        act.wait_ge(down_ps, n * ALL)
                    act.activation(fh[e % 2][:, :], ff[e % 2][:, :], ACT.Copy).then_inc(fh_done, 1)

                def group(n, b, j, first=False, last=False):
                    for e in range(ALL):
                        silu_gate(e, n)
                        if not last:
                            prepare(e, n + 1, 1 - b)
                        hi(e, n)

                def prepare_first():
                    for slot in range(ALL):
                        prepare(slot, 1, 0)

                walk(act, prepare_first, group)

            @block.vector
            def _(dve):
                def norm(n):
                    dve.wait_ge(x2_in, 16 * (n + 1))
                    for c in range(MT):
                        last = dve.bn_stats(st[:, c, :], x2[:, c, :])
                    last.then_inc(ln, 1)
                    dve.wait_ge(ln, 3 * n + 1)
                    stand_alone(dve, held_dve)
                    for c in range(MT):
                        last = dve.bn_aggr(mv[:, c, :], st[:, c, :])
                    last.then_inc(ln, 1)
                    dve.wait_ge(ln, 3 * n + 2)
                    dve.tensor_scalar(rs[:, :], mv[:, :, 1], EPS, None, ALU.add).then_inc(ln, 1)

                def apply(n):
                    dve.wait_ge(mroot, n + 1)
                    for c in range(MT):
                        last = dve.tensor_scalar(x2[:, c, :], x2[:, c, :], mv[:, c, 0:1], rs[:, c:c + 1],
                                                 ALU.subtract, ALU.mult)
                    last.then_inc(n_done, 1)

                def routing(n):
                    k = [0]

                    def link(ins):
                        k[0] += 1
                        ins.then_inc(route, 1)
                        dve.wait_ge(route, ROUTE_LINKS * n + k[0])

                    dve.wait_ge(tanh_done, n + 1)
                    dve.wait_ge(combT_ps, n)
                    link(dve.tensor_scalar(score[:, :, :], score[:, :, :], 0.5, 0.5, ALU.mult, ALU.add))
                    link(dve.tensor_tensor(biased[:, :, :], score[:, :, :], gateb[:, :, :], ALU.add))
                    stand_alone(dve, held_dve)
                    for c in range(MT):
                        last = dve.max(top[:, c, :], biased[:, c, :])
                    link(last)
                    link(dve.tensor_copy(best[:, :, 0:TOPK], top[:, :, 0:TOPK]))
                    stand_alone(dve, held_dve)
                    for c in range(MT):
                        last = dve.match_replace(rest[:, c, :], best[:, c, :], biased[:, c, :], -3.0e38)
                    link(last)
                    link(dve.tensor_scalar(rest[:, :, :], rest[:, :, :], -1.0e38, None, ALU.is_lt))
                    link(dve.tensor_tensor(comb[:, :, :], score[:, :, :], rest[:, :, :], ALU.mult))
                    link(dve.tensor_reduce(wsum[:, :], comb[:, :, :], mybir.AxisListType.X, ALU.add))
                    link(dve.reciprocal(wsum[:, :], wsum[:, :]))
                    link(dve.tensor_scalar(wsum[:, :], wsum[:, :], ROUTE_SCALE, None, ALU.mult))
                    link(dve.tensor_tensor(comb[:, :, :], comb[:, :, :],
                                           wsum[:, :].unsqueeze(2).to_broadcast([P, MT, NE]), ALU.mult))
                    link(dve.tensor_copy(comb_hi[:, :, :], comb[:, :, :]))
                    link(dve.tensor_copy(comb2[:, :, 0:NE], comb_hi[:, :, :].bitcast(F32)))
                    assert k[0] == ROUTE_LINKS
                    dve.tensor_tensor(comb2[:, :, NE:2 * NE], comb[:, :, :], comb_hi[:, :, :].bitcast(F32),
                                      ALU.subtract).then_inc(comb_done, 1)

                def prepare(slot, n):
                    if slot == 0:
                        norm(n)
                    if slot == 1:
                        apply(n)
                    if slot == 8:
                        routing(n)

                def times(e, n):
                    s = n * ALL + e
                    g = gs[e % 2][:, :]
                    dve.wait_ge(gs_done, s + 1)
                    dve.wait_ge(up_ps, s + 1)
                    if e < NE:
                        dve.tensor_tensor(g, g, ROUTE[:, :], ALU.mult).then_inc(gc_done, 1)
                        dve.wait_ge(gc_done, n * NE + e + 1)
                    if e >= 2:
                        dve.wait_ge(fl_done, s - 1)
                    else:
                        dve.wait_ge(fl_done, n * ALL)
                    dve.tensor_tensor(ff[e % 2][:, :], g, UP[e % 2][:, :], ALU.mult).then_inc(ff_done, 1)

                def scale(n, b):
                    dve.wait_ge(down_ps, ALL * (n + 1))
                    dve.wait_ge(out_stored, 16 * n)
                    for half in range(2):
                        last = dve.tensor_tensor(yo[:, 2 * half:2 * half + 2, :],
                                                 ACC[half][:, :].rearrange("p (c d) -> p c d", c=2),
                                                 gate_b_row[b][:, :].unsqueeze(1).to_broadcast([P, 2, D]), ALU.mult)
                    last.then_inc(scaled, 1)

                def group(n, b, j, first=False, last=False):
                    for e in range(ALL):
                        times(e, n)
                        if e == 0 and not first:
                            scale(n - 1, 1 - b)
                        if not last:
                            prepare(e, n + 1)
                    if last:
                        scale(n, b)

                def prepare_first():
                    for slot in range(ALL):
                        prepare(slot, 1)

                walk(dve, prepare_first, group)

            @block.gpsimd
            def _(pool):
                def split_h(k, n, b):
                    pool.wait_ge(mh_done, KD * n + k + 1)
                    pool.wait_ge(mhh_done, KD * n + k + 1)
                    pool.tensor_tensor(hl[b][:, k, :], hT[:, k, :], hh[b][:, k, :].bitcast(F32),
                                       ALU.subtract).then_inc(mhl_done, 1)

                def prepare(slot, n, b):
                    if slot == 0:
                        pool.wait_ge(ln, 3 * n + 3)
                        pool.tensor_tensor(rs[:, :], rs[:, :], minus_half[:, :], ALU.pow).then_inc(mroot, 1)
                    if slot in (3, 5):
                        split_h(slot // 2 - 1, n, b)

                def lo(e, n):
                    s = n * ALL + e
                    pool.wait_ge(fh_done, s + 1)
                    if e >= 2:
                        pool.wait_ge(down_ps, s - 1)
                    else:
                        pool.wait_ge(down_ps, n * ALL)
                    pool.tensor_tensor(fl[e % 2][:, :], ff[e % 2][:, :], fh[e % 2][:, :].bitcast(F32),
                                       ALU.subtract).then_inc(fl_done, 1)

                def residual(n):
                    pool.wait_ge(scaled, n + 1)
                    pool.wait_ge(res_in, 16 * (n + 1))
                    pool.tensor_tensor(yo[:, :, :], yo[:, :, :], xres[:, :, :], ALU.add).then_inc(yo_done2, 1)

                def group(n, b, j, first=False, last=False):
                    for e in range(ALL):
                        lo(e, n)
                        if e == 1 and not first:
                            residual(n - 1)
                        if not last:
                            prepare(e, n + 1, 1 - b)
                    if last:
                        residual(n)

                def prepare_first():
                    for slot in range(ALL):
                        prepare(slot, 1, 0)

                walk(pool, prepare_first, group)


def host_layout(inputs):
    a = {k.replace("L0_attn_", "").replace("L0_ffn_", "").replace("L0_", ""): np.asarray(v) for k, v in inputs.items()}

    def slices(w):
        return w.reshape(-1, P, w.shape[-1]).transpose(1, 0, 2)

    def columns(v):
        return v.reshape(-1, P).T

    def everywhere(v, *shape):
        return np.broadcast_to(v, (P, *shape))

    def expert(w13, w2):
        return np.concatenate([slices(w13.T).reshape(P, KD * 2 * INTER), w2.T], axis=1)

    r = np.arange(P)
    out = {
        "x": a["x"].reshape(NB, STEPS, CH, P, D).transpose(0, 1, 3, 2, 4),
        "c_col": a["c"].T.reshape(KD, P, NB).transpose(1, 0, 2),
        "wmod": slices(a["wmod"]),
        "ln_wb": everywhere(np.stack([a["ln_w"], a["ln_b"]]), 2, D),
        "W_in": slices(a["W_in"]),
        "W_out": slices(a["W_out"]).reshape(P, KI * D),
        "glu_w": slices(a["glu_w"]).reshape(P, KD * 2 * D),
        "rms_w": columns(a["rms_w"]),
        "conv_w": a["conv_w"].reshape(MC, P, TAPS).transpose(1, 0, 2),
        "conv_b": columns(a["conv_b"]),
        "dt_bias": everywhere(a["dt_bias"], CH, H),
        "A_log": everywhere(a["A_log"], CH, H),
        "D_skip": columns(np.repeat(a["D_skip"], HD)),
        "glu_b": columns(a["glu_b"]),
        "gate_w": slices(a["gate_w"].T),
        "gate_b": everywhere(a["gate_b"], MT, NE),
        "experts": np.stack([expert(a["w13"][e], a["w2"][e]) for e in range(NE)] + [expert(a["w13_s"], a["w2_s"])]),
        "ident": np.eye(P, dtype=np.float32),
        "upto": (r[:, None] <= r[None, :]).astype(np.float32),
        "after": (r[:, None] > r[None, :]).astype(np.float32),
        "ones": np.ones((P, P), np.float32),
        "pick": np.broadcast_to((np.arange(2 * NE)[:, None] % NE == np.arange(NE)[None, :])[:, :, None],
                                (2 * NE, NE, P)).astype(np.float32),
    }
    return {k: np.ascontiguousarray(v) for k, v in out.items()}


def kernel(**inputs):
    import concourse.bacc as _bacc
    from concourse.bass_utils import run_bass_kernel_spmd as _run

    nc = _bacc.Bacc("TRN2", target_bir_lowering=False, num_devices=1)
    arrays, t = {}, {}
    for name, a in host_layout(inputs).items():
        arrays[f"in_{name}"] = a
        t[name] = nc.dram_tensor(f"in_{name}", a.shape, mybir.dt.from_np(a.dtype), kind="ExternalInput").ap()
    x2_dram = nc.dram_tensor("x2_dram", (NB, STEPS, P, CH, D), F32, kind="Internal").ap()
    out = nc.dram_tensor("out", (NB, SEQ, D), F32, kind="ExternalOutput").ap()
    build(nc, t, x2_dram, out)
    r = _run(nc, [arrays], core_ids=[0])
    return r.results[0]["out"]
```

```python
from contextlib import ExitStack

import numpy as np
import concourse.bass as bass
from concourse import mybir

ALU = mybir.AluOpType
ACT = mybir.ActivationFunctionType
F32 = mybir.dt.float32
F32R = mybir.dt.float32r

P = 128
NB = 2
SEQ = 4096
D = 256
DI = 512
H = 8
HD = DI // H
NS = 128
CONV = DI + 2 * NS
TAPS = 4
KD = D // P
KI = DI // P
MC = CONV // P
IN_COLS = 2 * DI + 2 * NS + H
EPS = 1e-5
NE = 16
INTER = 128
TOPK = 4
ROUTE_SCALE = 2.5

GROUP = 256
CH = GROUP // P
STEPS = SEQ // GROUP
MGROUP = 512
MT = MGROUP // P
MSTEPS = SEQ // MGROUP
DT_LINKS = 16
SERIES = [1.0 / (2 * n + 1) for n in range(8, -1, -1)]


def build(nc, t, x2_dram, out):
    ctx = ExitStack()

    def sb(name, shape, dt=F32):
        return ctx.enter_context(nc.sbuf_tensor(name, shape, dt))

    taken = []

    def sem(name):
        taken.append(nc.alloc_semaphore(name=name))
        return taken[-1]

    def prime(counts):
        with nc.Block() as block:
            @block.sync
            def _(sp):
                for semaphore, per_step in counts[0::3]:
                    sp.sem_inc(semaphore, per_step)

            @block.vector
            def _(dve):
                for semaphore, per_step in counts[1::3]:
                    dve.sem_inc(semaphore, per_step)

            @block.gpsimd
            def _(pool):
                for semaphore, per_step in counts[2::3]:
                    pool.sem_inc(semaphore, per_step)

    def clear_semaphores():
        nc.all_engine_barrier()
        nc.clear_and_free_semaphores(taken)
        nc.all_engine_barrier()
        taken.clear()

    with ctx:
        bank = [ctx.enter_context(nc.psum_tensor(f"bank{n}", [P, 512], F32)) for n in range(8)]
        mod = [sb(f"mod{b}", [P, 4, KD]) for b in range(NB)]
        gate_b_row = [sb(f"gb_row{b}", [P, D]) for b in range(NB)]
        ident = sb("ident", [P, P])
        minus_half = sb("minus_half", [P, MT])
        gate_ln = sb("gate_ln", [P, NB, 2, D])
        setup(nc, sem, t, mod, gate_b_row, gate_ln, ident, minus_half, bank)
        mixer(nc, sem, prime, t, mod, gate_ln, ident, minus_half, bank, x2_dram)
        clear_semaphores()
        experts(nc, sem, prime, t, mod, gate_b_row, ident, minus_half, bank, x2_dram, out)


def split3(pe, out, a_hi, a_lo, b_hi, b_lo, start, stop):
    pe.matmul(out, a_hi, b_hi, start=start, stop=False, skip_group_check=True)
    pe.matmul(out, a_hi, b_lo, start=False, stop=False, skip_group_check=True)
    return pe.matmul(out, a_lo, b_hi, start=False, stop=stop, skip_group_check=True)


def stand_alone(eng, counter):
    eng.sem_inc(counter, 1)


def setup(nc, sem, t, mod, gate_b_row, gate_ln, ident, minus_half, bank):
    with ExitStack() as ctx:
        c_col = ctx.enter_context(nc.sbuf_tensor("c_col", [P, KD, NB], F32))
        c_silu = ctx.enter_context(nc.sbuf_tensor("c_silu", [P, KD, NB], F32))
        c_wide = ctx.enter_context(nc.sbuf_tensor("c_wide", [P, KD, NB, P], F32))
        wmod = ctx.enter_context(nc.sbuf_tensor("wmod", [P, KD, 6 * D], F32))
        pos = ctx.enter_context(nc.sbuf_tensor("pos", [P, 2, D], F32))
        mag = ctx.enter_context(nc.sbuf_tensor("mag", [P, 2, D], F32))
        lnw = ctx.enter_context(nc.sbuf_tensor("lnw", [P, 2, D], F32))
        loaded = sem("mod_loaded")
        silu_done = sem("c_silu_done")
        wide_done = sem("c_wide_done")
        cols_done = sem("mod_cols_done")
        rows_done = sem("mod_rows_done")
        link = sem("mod_link")
        with nc.Block() as block:
            @block.sync
            def _(sp):
                sp.dma_start(c_col[:, :, :], t["c_col"]).then_inc(loaded, 16)
                sp.dma_start(wmod[:, :, :], t["wmod"]).then_inc(loaded, 16)
                sp.dma_start(ident[:, :], t["ident"]).then_inc(loaded, 16)
                sp.dma_start(lnw[:, :, :], t["ln_wb"]).then_inc(loaded, 16)

            @block.gpsimd
            def _(pool):
                pool.memset(minus_half[:, :], -0.5)

            @block.scalar
            def _(act):
                act.wait_ge(loaded, 64)
                act.activation(c_silu[:, :, :], c_col[:, :, :], ACT.Silu).then_inc(silu_done, 1)
                act.wait_ge(silu_done, 1)
                act.activation(c_wide[:, :, :, :], c_silu[:, :, :].unsqueeze(3).to_broadcast([P, KD, NB, P]),
                               ACT.Copy).then_inc(wide_done, 1)

            @block.tensor
            def _(pe):
                pe.wait_ge(wide_done, 1)
                for n, chunk in enumerate((1, 0, 4, 3)):
                    for m in range(KD):
                        for k in range(KD):
                            last = pe.matmul(bank[0][:, (n * KD + m) * 2:(n * KD + m) * 2 + 2],
                                             wmod[:, k, chunk * D + m * P:chunk * D + (m + 1) * P],
                                             c_silu[:, k, :], start=(k == 0), stop=(k == KD - 1))
                last.then_inc(cols_done, 1)
                for b in range(NB):
                    for n, chunk in enumerate((2, 5)):
                        for k in range(KD):
                            last = pe.matmul(bank[2 + b][:, n * D:(n + 1) * D], c_wide[:, k, b, :],
                                             wmod[:, k, chunk * D:(chunk + 1) * D],
                                             start=(k == 0), stop=(k == KD - 1))
                    last.then_inc(rows_done, 1)

            @block.vector
            def _(dve):
                n = [0]

                def then_wait(ins):
                    n[0] += 1
                    ins.then_inc(link, 1)
                    dve.wait_ge(link, n[0])

                dve.wait_ge(cols_done, 1)
                for b in range(NB):
                    col = bank[0][:, 0:8 * KD].rearrange("p (n m b) -> p n m b", n=4, b=NB)[:, :, :, b]
                    for j in range(2):
                        then_wait(dve.tensor_scalar(mod[b][:, 2 * j, :], col[:, 2 * j, :], 1.0, None, ALU.add))
                        then_wait(dve.tensor_copy(mod[b][:, 2 * j + 1, :], col[:, 2 * j + 1, :]))
                dve.wait_ge(loaded, 64)
                for b in range(NB):
                    dve.wait_ge(rows_done, b + 1)
                    g = bank[2 + b][:, :].rearrange("p (n d) -> p n d", n=2)
                    dve.tensor_scalar(pos[:, :, :], g, 0.0, 2.0, ALU.is_ge, ALU.mult)
                    then_wait(dve.tensor_scalar(mag[:, :, :], g, -1.0, None, ALU.mult))
                    then_wait(dve.tensor_tensor(mag[:, :, :], mag[:, :, :], g, ALU.max))
                    then_wait(dve.tensor_scalar(mag[:, :, :], mag[:, :, :], 0.25, None, ALU.max))
                    then_wait(dve.scalar_tensor_tensor(pos[:, :, :], pos[:, :, :], -1.0, mag[:, :, :],
                                                       ALU.add, ALU.mult))
                    dve.tensor_copy(gate_b_row[b][:, :], pos[:, 1, :])
                    for n2 in range(2):
                        last = dve.tensor_tensor(gate_ln[:, b, n2, :], pos[:, 0, :], lnw[:, n2, :], ALU.mult)
                    then_wait(last)


def mixer(nc, sem, prime, t, mod, gate_ln, ident, minus_half, bank, x2_dram):
    with ExitStack() as ctx:
        def sb(name, shape, dt=F32):
            return ctx.enter_context(nc.sbuf_tensor(name, shape, dt))

        def both(name, shape, dt=F32):
            return [sb(f"{name}{b}", shape, dt) for b in range(NB)]

        counts = []

        def sems(name, per_step=None):
            pair = [sem(f"{name}{b}") for b in range(NB)]
            if per_step:
                counts.extend((s, per_step) for s in pair)
            return pair

        win = [sb(f"win_{h}", [P, KD, IN_COLS], F32R) for h in ("hi", "lo")]
        wout = [sb(f"wout_{h}", [P, KI, D], F32R) for h in ("hi", "lo")]
        wglu = [sb(f"wglu_{h}", [P, KD, 2 * D], F32R) for h in ("hi", "lo")]
        upto = sb("upto", [P, P])
        after = sb("after", [P, P])
        after_r = sb("after_r", [P, P], F32R)
        ones = sb("ones", [P, P])
        convw = sb("convw", [P, MC, TAPS])
        convb = sb("convb", [P, MC])
        dtb = sb("dtb", [P, CH, H])
        negA = sb("negA", [P, CH, H])
        dskip = sb("dskip", [P, DI])
        w_dt = sb("w_dt", [P, KD, H])
        glub = sb("glub", [P, 2 * KD])
        xt = both("xt", [P, CH, D])
        xr = both("xr", [P, CH, D])
        st1 = both("st1_", [P, CH, 6])
        mv1 = both("mv1_", [P, CH, 2])
        rs1 = both("rs1_", [P, CH])
        st = both("st", [P, CH, 6])
        mv = both("mv", [P, CH, 2])
        rs = both("rs", [P, CH])
        hT = both("hT", [P, KD, GROUP])
        hTh = both("hTh", [P, KD, GROUP], F32R)
        hTl = both("hTl", [P, KD, GROUP], F32R)
        zs = both("zs", [P, CH, DI])
        xc = both("xc", [P, MC, TAPS - 1 + GROUP])
        cv = both("cv", [P, MC, GROUP])
        dts = both("dts", [P, 8, CH, H])
        ex = both("ex", [P, 3, CH, H])
        xtok = both("xtok", [P, CH, DI])
        xdt = both("xdt", [P, CH, DI])
        xend = both("xend", [P, CH, DI])
        btok = both("btok", [P, CH, NS])
        a_hi = both("a_hi", [P, CH, H], F32R)
        a_lo = both("a_lo", [P, CH, H])
        masked_hi = both("masked_hi", [P, H, P], F32R)
        masked_lo = both("masked_lo", [P, H, P], F32R)
        dec = both("dec", [P, CH, H, P])
        gm = both("gm", [P, CH, P])
        state = both("state", [P, DI])
        yy = both("yy", [P, CH, DI])
        ss = both("ss", [P, CH])
        rr = both("rr", [P, CH])
        yTh = both("yTh", [P, KI, GROUP], F32R)
        yTl = both("yTl", [P, KI, GROUP], F32R)
        y1 = both("y1", [P, KD, GROUP])
        y1h = both("y1h", [P, KD, GROUP], F32R)
        y1l = both("y1l", [P, KD, GROUP], F32R)
        sg = both("sg", [P, KD, GROUP])
        half_a = [x[:, 0, :].rearrange("p (k t) -> p k t", k=KD) for x in xend]

        w_in, w_hi, link = [sem(f"w_in{n}") for n in range(4)], sem("w_hi"), sem("w_link")
        with nc.Block() as block:
            raws = ([cv[b][:, :, :].rearrange("p a b -> p (a b)") for b in range(NB)]
                    + [dec[b][:, :, :, :].rearrange("p a b c -> p (a b c)") for b in range(NB)])
            pieces = []
            for k in range(KD):
                pieces.append((t["W_in"][:, k, :], IN_COLS, win[0][:, k, :], win[1][:, k, :]))
            pieces.append((t["W_out"], KI * D, wout[0][:, :, :].rearrange("p a b -> p (a b)"),
                           wout[1][:, :, :].rearrange("p a b -> p (a b)")))
            pieces.append((t["glu_w"], KD * 2 * D, wglu[0][:, :, :].rearrange("p a b -> p (a b)"),
                           wglu[1][:, :, :].rearrange("p a b -> p (a b)")))
            OUT_PIECE = 2
            consts = [(upto, "upto"), (after, "after"), (ones, "ones"), (convw, "conv_w"), (convb, "conv_b"),
                      (dtb, "dt_bias"), (negA, "A_log"), (dskip, "D_skip"), (w_dt, "W_dt"), (glub, "glu_b"),
                      ]
            c_in = sem("c_in")
            rms = sg[0][:, 0, 0:KI]
            CONSTS = len(consts) + 1

            @block.sync
            def _(sp):
                for n, (src, cols, _, _) in enumerate(pieces):
                    sp.dma_start(raws[n][:, 0:cols], src).then_inc(w_in[n], 16)
                sp.dma_start(rms, t["rms_w"]).then_inc(c_in, 16)
                for dst, name in consts:
                    sp.dma_start(dst[tuple(slice(None) for _ in dst.shape)], t[name]).then_inc(c_in, 16)
                sp.wait_ge(c_in, 16 * CONSTS)

            @block.vector
            def _(dve):
                for n, (_, cols, hi, lo) in enumerate(pieces):
                    dve.wait_ge(w_in[n], 16)
                    raw = raws[n][:, 0:cols]
                    if n == OUT_PIECE:
                        dve.wait_ge(c_in, 16 * CONSTS)
                        for k in range(KI):
                            last = dve.tensor_scalar(raw[:, k * D:(k + 1) * D], raw[:, k * D:(k + 1) * D],
                                                     rms[:, k:k + 1], None, ALU.mult)
                        last.then_inc(link, 1)
                    dve.wait_ge(w_hi, n + 1)
                    dve.tensor_tensor(lo, raw, hi.bitcast(F32), ALU.subtract)
                dve.wait_ge(c_in, 16 * CONSTS)
                dve.tensor_copy(after_r[:, :], after[:, :])
                dve.tensor_scalar(glub[:, :], glub[:, :], 0.5, None, ALU.mult)

            @block.scalar
            def _(act):
                for n, (_, cols, hi, _) in enumerate(pieces):
                    act.wait_ge(w_in[n], 16)
                    if n == OUT_PIECE:
                        act.wait_ge(link, 1)
                    act.activation(hi, raws[n][:, 0:cols], ACT.Copy).then_inc(w_hi, 1)
                act.wait_ge(c_in, 16 * CONSTS)
                act.activation(negA[:, :, :], negA[:, :, :], ACT.Exp)

            @block.gpsimd
            def _(pool):
                for b in range(NB):
                    pool.memset(state[b][:, :], 0.0)
                    pool.memset(xc[b][:, :, GROUP:GROUP + TAPS - 1], 0.0)

        x_in = sems("x_in", 16)
        xr_in = sems("xr_in", 16)
        ln1 = sems("ln1", 3)
        root1 = sems("root1", 1)
        xn_done = sems("xn_done", 1)
        xnT_ps = sems("xnT_ps", 1)
        hT_done = sems("hT_done", 1)
        hTh_done = sems("hTh_done", 1)
        hTl_done = sems("hTl_done", 1)
        z_ps = sems("z_ps", CH)
        dt_ps = sems("dt_ps", 1)
        xbc_ps = sems("xbc_ps", 3)
        zs_done = sems("zs_done", CH)
        halo_done = sems("halo_done", 1)
        xc_done = sems("xc_done", 3)
        tap0_done = sems("tap0_done", 3)
        tap_done = sems("tap_done", MC * (TAPS - 1))
        xs_done = sems("xs_done", 3)
        dt_abs = sems("dt_abs", 1)
        dt_exp = sems("dt_exp", 1)
        dt_link = sems("dt_link", DT_LINKS)
        a_done = sems("a_done", 1)
        sums_ps = sems("sums_ps", 1)
        ex_done = sems("ex_done", 1)
        wend_done = sems("wend_done", 1)
        xT_ps = sems("xT_ps", CH)
        btg_ps = sems("btg_ps", 1)
        xtok_done = sems("xtok_done", CH)
        xdt_done = sems("xdt_done", CH)
        btok_done = sems("btok_done", 1)
        gm_done = sems("gm_done", 1)
        au_done = sems("au_done", CH)
        ahi_done = sems("ahi_done", 1)
        alo_done = sems("alo_done", 1)
        lo_done = sems("lo_done", CH)
        dec_ps = sems("dec_ps", CH)
        dec_done = sems("dec_done", CH)
        w_done = sems("w_done", CH)
        xend_done = sems("xend_done", CH)
        yin_ps = sems("yin_ps", CH)
        yst_ps = sems("yst_ps", CH)
        add_ps = sems("add_ps", CH)
        sdec_done = sems("sdec_done", CH)
        st_done = sems("st_done", CH)
        y1s_done = sems("y1s_done", CH)
        dx_done = sems("dx_done", CH)
        skip_done = sems("skip_done", CH)
        y2s_done = sems("y2s_done", CH)
        y4_done = sems("y4_done", CH)
        sq_done = sems("sq_done", CH)
        ms_done = sems("ms_done", CH)
        rr_done = sems("rr_done", CH)
        yn_done = sems("yn_done", CH)
        yT_ps = sems("yT_ps", CH)
        yTh_done = sems("yTh_done", CH)
        yTl_done = sems("yTl_done", CH)
        o_ps = sems("o_ps", 1)
        y1_done = sems("y1_done", 1)
        y1h_done = sems("y1h_done", 1)
        y1l_done = sems("y1l_done", 1)
        glu_ps = sems("glu_ps", 1)
        tanh_done = sems("tanh_done", 1)
        ag_done = sems("ag_done", 1)
        y2_done = sems("y2_done", 1)
        y2T_ps = sems("y2T_ps", 1)
        ln2 = sems("ln2", 3)
        root2 = sems("root2", 1)
        xb_done = sems("xb_done", 1)
        xo_link = sems("xo_link", 1)
        xo_done = sems("xo_done", 1)
        stored = sems("x2_stored", 16)

        prime(counts)
        held_dve = sem("held_dve")

        def Q(b, n):
            return bank[4 * b + n]

        def following(done):
            b, i = done
            return b, i + 1

        def halves(eng, half):
            half((0, 1), None, None, False)
            half((1, 1), (0, 1), None)
            half((0, 2), (1, 1), (0, 1))
            with eng.Fori(2, STEPS) as i:
                half((1, i), (0, i), (1, i - 1))
                half((0, i + 1), (1, i), (0, i))
            half((1, STEPS), (0, STEPS), (1, STEPS - 1), False)
            half(None, (1, STEPS), (0, STEPS), False)
            half(None, None, (1, STEPS), False)

        with nc.Block() as block:
            @block.sync
            def _(sp):
                def step(dram, b, i):
                    return dram[b, bass.ds(i - 1, 1)].rearrange("o p c d -> p (o c) d")

                def load_x(b, i):
                    sp.wait_ge(xnT_ps[b], i)
                    sp.dma_start(xt[b][:, :, :], step(t["x"], b, i)).then_inc(x_in[b], 16)

                def load_again(b, i):
                    sp.wait_ge(stored[b], 16 * i)
                    sp.dma_start(xr[b][:, :, :], step(t["x"], b, i)).then_inc(xr_in[b], 16)

                def store(b, i):
                    sp.wait_ge(xo_done[b], i + 1)
                    sp.dma_start(step(x2_dram, b, i), xr[b][:, :, :]).then_inc(stored[b], 16)

                def half(first, second, tail, more=True):
                    if second:
                        load_again(*second)
                    if more:
                        load_x(*following(second))
                    if tail:
                        store(*tail)

                for b in range(NB):
                    load_x(b, 1)
                halves(sp, half)
                for b in range(NB):
                    sp.wait_ge(stored[b], 16 * (STEPS + 1))

            @block.tensor
            def _(pe):
                def transpose_xn(b, i):
                    pe.wait_ge(xn_done[b], i + 1)
                    pe.wait_ge(yTl_done[b], CH * i)
                    for k in range(KD):
                        for c in range(CH):
                            last = pe.transpose(Q(b, 0)[:, k * GROUP + c * P:k * GROUP + (c + 1) * P],
                                                xt[b][:, c, k * P:(k + 1) * P], ident[:, :])
                    last.then_inc(xnT_ps[b], 1)

                def project_dt(b, i):
                    pe.wait_ge(hT_done[b], i + 1)
                    pe.wait_ge(st_done[b], CH * i)
                    for c in range(CH):
                        for k in range(KD):
                            last = pe.matmul(Q(b, 3)[:, c * H:(c + 1) * H], hT[b][:, k, c * P:(c + 1) * P],
                                             w_dt[:, k, :], start=(k == 0), stop=(k == KD - 1))
                    last.then_inc(dt_ps[b], 1)

                def project_xbc(b, i, pair):
                    if pair == 0:
                        pe.wait_ge(hTh_done[b], i + 1)
                        pe.wait_ge(hTl_done[b], i + 1)
                    if pair == 1:
                        pe.wait_ge(xo_done[b], i)
                    if pair == 2:
                        pe.wait_ge(tanh_done[b], i)
                    for m in range(2):
                        col = DI + (2 * pair + m) * P
                        for k in range(KD):
                            last = split3(pe, Q(b, pair)[:, m * GROUP:(m + 1) * GROUP],
                                          win[0][:, k, col:col + P], win[1][:, k, col:col + P],
                                          hTh[b][:, k, :], hTl[b][:, k, :], k == 0, k == KD - 1)
                    last.then_inc(xbc_ps[b], 1)

                def project_z(b, i, c):
                    tok = slice(c * P, (c + 1) * P)
                    pe.wait_ge(xc_done[b], 3 * i + c + 1)
                    pe.wait_ge(tap0_done[b], 3 * i + c + 1)
                    for k in range(KD):
                        last = split3(pe, Q(b, c)[:, :], hTh[b][:, k, tok], hTl[b][:, k, tok],
                                      win[0][:, k, 0:DI], win[1][:, k, 0:DI], k == 0, k == KD - 1)
                    last.then_inc(z_ps[b], 1)

                def sums(b, i):
                    pe.wait_ge(a_done[b], i + 1)
                    a = dts[b][:, 7, :, :]
                    for n, m in enumerate((upto, after, ones)):
                        last = pe.matmul(Q(b, 3)[:, 64 + n * CH * H:64 + (n + 1) * CH * H], m[:, :],
                                         a.rearrange("p c h -> p (c h)"), start=True, stop=True)
                    last.then_inc(sums_ps[b], 1)

                def x_by_token(b, i, c):
                    pe.wait_ge(xs_done[b], 3 * i + 2)
                    pe.wait_ge(zs_done[b], CH * i + c + 1)
                    for m in range(KI):
                        last = pe.transpose(Q(b, c)[:, m * P:(m + 1) * P], cv[b][:, m, c * P:(c + 1) * P],
                                            ident[:, :])
                    last.then_inc(xT_ps[b], 1)

                def b_by_token(b, i):
                    pe.wait_ge(xs_done[b], 3 * i + 3)
                    pe.wait_ge(dec_done[b], CH * i + CH)
                    for c in range(CH):
                        tok = slice(c * P, (c + 1) * P)
                        pe.transpose(Q(b, 2)[:, tok], cv[b][:, KI, tok], ident[:, :])
                    for c in range(CH):
                        tok = slice(c * P, (c + 1) * P)
                        last = pe.matmul(Q(b, 2)[:, GROUP + c * P:GROUP + (c + 1) * P], cv[b][:, KI, tok],
                                         cv[b][:, KI + 1, tok], start=True, stop=True)
                    last.then_inc(btg_ps[b], 1)

                def exponents(b, i, c):
                    pe.wait_ge(au_done[b], CH * i + c + 1)
                    pe.wait_ge(lo_done[b], CH * i + c + 1)
                    if c == 0:
                        pe.wait_ge(xc_done[b], 3 * i + 3)
                        pe.wait_ge(tap0_done[b], 3 * i + 3)
                        pe.wait_ge(ex_done[b], i + 1)
                    else:
                        pe.wait_ge(dec_done[b], CH * i + c)
                    for half_heads in range(2):
                        heads = slice(half_heads * 4, half_heads * 4 + 4)
                        pe.matmul(Q(b, 2 + half_heads)[:, :], after_r[:, :],
                                  masked_hi[b][:, heads, :].rearrange("p h i -> p (h i)"), start=True, stop=False)
                        last = pe.matmul(Q(b, 2 + half_heads)[:, :], after_r[:, :],
                                         masked_lo[b][:, heads, :].rearrange("p h i -> p (h i)"),
                                         start=False, stop=True)
                    last.then_inc(dec_ps[b], 1)

                def within(b, i, c):
                    pe.wait_ge(w_done[b], CH * i + c + 1)
                    pe.wait_ge(xdt_done[b], CH * i + c + 1)
                    pe.wait_ge(xtok_done[b], CH * i + c + 1)
                    for h in range(H):
                        last = pe.matmul(Q(b, c)[:, h * HD:(h + 1) * HD], dec[b][:, c, h, :],
                                         xdt[b][:, c, h * HD:(h + 1) * HD], start=True, stop=True)
                    last.then_inc(yin_ps[b], 1)

                def from_state(b, i, c):
                    pe.wait_ge(st_done[b], CH * i + c)
                    if c == 0:
                        pe.wait_ge(gm_done[b], i + 1)
                    else:
                        pe.wait_ge(y1s_done[b], CH * i + c)
                    pe.matmul(Q(b, 2)[:, :], cv[b][:, KI + 1, c * P:(c + 1) * P], state[b][:, :],
                              start=True, stop=True).then_inc(yst_ps[b], 1)

                def state_add(b, i, c):
                    pe.wait_ge(xend_done[b], CH * i + c + 1)
                    pe.wait_ge(btok_done[b], i + 1)
                    pe.wait_ge(dec_done[b], CH * i + CH)
                    pe.matmul(Q(b, 3)[:, :], btok[b][:, c, :], xend[b][:, c, :],
                              start=True, stop=True).then_inc(add_ps[b], 1)

                def transpose_y(b, i, c):
                    pe.wait_ge(yn_done[b], CH * i + c + 1)
                    pe.wait_ge(y2s_done[b], CH * i + c + 1)
                    for m in range(KI):
                        last = pe.transpose(Q(b, c)[:, m * P:(m + 1) * P], yy[b][:, c, m * P:(m + 1) * P],
                                            ident[:, :])
                    last.then_inc(yT_ps[b], 1)

                def project_out(b, i):
                    pe.wait_ge(yTh_done[b], CH * i + CH)
                    pe.wait_ge(yTl_done[b], CH * i + CH)
                    pe.wait_ge(y1s_done[b], CH * i + CH)
                    for m in range(KD):
                        for k in range(KI):
                            last = split3(pe, Q(b, 2)[:, m * GROUP:(m + 1) * GROUP],
                                          wout[0][:, k, m * P:(m + 1) * P], wout[1][:, k, m * P:(m + 1) * P],
                                          yTh[b][:, k, :], yTl[b][:, k, :], k == 0, k == KI - 1)
                    last.then_inc(o_ps[b], 1)

                def glu(b, i):
                    pe.wait_ge(y1h_done[b], i + 1)
                    pe.wait_ge(y1l_done[b], i + 1)
                    pe.wait_ge(yTl_done[b], CH * i + CH)
                    pe.wait_ge(y1_done[b], i + 1)
                    for m in range(2 * KD):
                        for k in range(KD):
                            last = split3(pe, Q(b, 1 if m < KD else 2)[:, m % KD * GROUP:(m % KD + 1) * GROUP],
                                          wglu[0][:, k, m * P:(m + 1) * P], wglu[1][:, k, m * P:(m + 1) * P],
                                          y1h[b][:, k, :], y1l[b][:, k, :], k == 0, k == KD - 1)
                    last.then_inc(glu_ps[b], 1)

                def transpose_y2(b, i):
                    pe.wait_ge(y2_done[b], i + 1)
                    pe.wait_ge(tanh_done[b], i + 1)
                    for c in range(CH):
                        for k in range(KD):
                            last = pe.transpose(Q(b, 1)[:, c * D + k * P:c * D + (k + 1) * P],
                                                y1[b][:, k, c * P:(c + 1) * P], ident[:, :])
                    last.then_inc(y2T_ps[b], 1)

                def half(first, second, tail, more=True):
                    if second:
                        project_z(*second, 1)
                    if tail:
                        project_out(*tail)
                    if second:
                        exponents(*second, 0)
                    if first:
                        transpose_xn(*first)
                    if second:
                        x_by_token(*second, 0)
                        x_by_token(*second, 1)
                    if tail:
                        state_add(*tail, 1)
                        glu(*tail)
                    if first:
                        project_dt(*first)
                    if second:
                        exponents(*second, 1)
                    if first:
                        project_xbc(*first, 0)
                    if second:
                        b_by_token(*second)
                    if tail:
                        transpose_y2(*tail)
                    if second:
                        from_state(*second, 0)
                        state_add(*second, 0)
                        within(*second, 0)
                        from_state(*second, 1)
                        within(*second, 1)
                    if first:
                        project_xbc(*first, 1)
                        project_xbc(*first, 2)
                    if second:
                        transpose_y(*second, 0)
                    if first:
                        project_z(*first, 0)
                        sums(*first)
                    if second:
                        transpose_y(*second, 1)

                halves(pe, half)

            @block.scalar
            def _(act):
                def modulate(b, i):
                    act.wait_ge(xnT_ps[b], i + 1)
                    act.wait_ge(y1_done[b], i)
                    act.wait_ge(xbc_ps[b], 3 * i)
                    for k in range(KD):
                        last = act.activation(hT[b][:, k, :], Q(b, 0)[:, k * GROUP:(k + 1) * GROUP], ACT.Identity,
                                              bias=mod[b][:, 1, k:k + 1], scale=mod[b][:, 0, k:k + 1])
                    last.then_inc(hT_done[b], 1)
                    act.wait_ge(hT_done[b], i + 1)
                    act.activation(hTh[b][:, :, :], hT[b][:, :, :], ACT.Copy).then_inc(hTh_done[b], 1)

                def silu_z(b, i, c):
                    act.wait_ge(z_ps[b], CH * i + c + 1)
                    act.wait_ge(y4_done[b], CH * i)
                    act.activation(zs[b][:, c, :], Q(b, c)[:, :], ACT.Silu).then_inc(zs_done[b], 1)

                def start_conv(b, i, pair):
                    act.wait_ge(xbc_ps[b], 3 * i + pair + 1)
                    if pair == 0:
                        act.wait_ge(yst_ps[b], CH * i)
                        act.wait_ge(yin_ps[b], CH * i)
                    for m in range(2):
                        n = 2 * pair + m
                        last = act.activation(cv[b][:, n, :], Q(b, pair)[:, m * GROUP:(m + 1) * GROUP], ACT.Identity,
                                              bias=convb[:, n:n + 1], scale=convw[:, n, TAPS - 1:TAPS])
                    last.then_inc(tap0_done[b], 1)

                def copy_xbc(b, i, pair):
                    if pair == 0:
                        act.wait_ge(tap_done[b], MC * (TAPS - 1) * i)
                        act.activation(xc[b][:, :, 0:TAPS - 1], xc[b][:, :, GROUP:GROUP + TAPS - 1],
                                       ACT.Copy).then_inc(halo_done[b], 1)
                        act.wait_ge(halo_done[b], i + 1)
                    act.wait_ge(xbc_ps[b], 3 * i + pair + 1)
                    act.activation(xc[b][:, 2 * pair:2 * pair + 2, TAPS - 1:],
                                   Q(b, pair)[:, :].rearrange("p (m t) -> p m t", m=2),
                                   ACT.Copy).then_inc(xc_done[b], 1)

                def silu_xbc(b, i, pair):
                    act.wait_ge(tap_done[b], (MC * i + 2 * (pair + 1)) * (TAPS - 1))
                    v = cv[b][:, 2 * pair:2 * pair + 2, :]
                    act.activation(v, v, ACT.Silu).then_inc(xs_done[b], 1)

                def exp_dt(b, i):
                    act.wait_ge(dt_abs[b], i + 1)
                    act.activation(dts[b][:, 2, :, :], dts[b][:, 1, :, :], ACT.Exp, scale=-1.0).then_inc(dt_exp[b], 1)

                def exp_sums(b, i):
                    act.wait_ge(sums_ps[b], i + 1)
                    act.wait_ge(sdec_done[b], CH * i)
                    act.wait_ge(wend_done[b], i)
                    act.wait_ge(y1s_done[b], CH * i)
                    act.activation(ex[b][:, :, :, :].rearrange("p n c h -> p (n c h)"),
                                   Q(b, 3)[:, 64:64 + 3 * CH * H], ACT.Exp).then_inc(ex_done[b], 1)

                def copy_tokens(b, i, c):
                    act.wait_ge(xT_ps[b], CH * i + c + 1)
                    act.wait_ge(skip_done[b], CH * i)
                    act.activation(xtok[b][:, c, :], Q(b, c)[:, :], ACT.Copy).then_inc(xtok_done[b], 1)

                def copy_b(b, i):
                    act.wait_ge(btg_ps[b], i + 1)
                    act.wait_ge(add_ps[b], CH * i)
                    act.activation(btok[b][:, :, :].rearrange("p c n -> p (c n)"), Q(b, 2)[:, 0:GROUP],
                                   ACT.Copy).then_inc(btok_done[b], 1)

                def decays(b, i, c):
                    act.wait_ge(dec_ps[b], CH * i + c + 1)
                    act.wait_ge(yin_ps[b], CH * i)
                    for half_heads in range(2):
                        last = act.activation(
                            dec[b][:, c, 4 * half_heads:4 * half_heads + 4, :].rearrange("p h i -> p (h i)"),
                            Q(b, 2 + half_heads)[:, :], ACT.Exp)
                    last.then_inc(dec_done[b], 1)

                def squares(b, i, c):
                    act.wait_ge(y4_done[b], CH * i + c + 1)
                    act.wait_ge(yT_ps[b], CH * i)
                    act.activation(xdt[b][:, c, :], yy[b][:, c, :], ACT.Square,
                                   accum_out=ss[b][:, c:c + 1]).then_inc(sq_done[b], 1)

                def norm_y(b, i, c):
                    act.wait_ge(rr_done[b], CH * i + c + 1)
                    act.activation(yy[b][:, c, :], yy[b][:, c, :], ACT.Copy,
                                   scale=rr[b][:, c:c + 1]).then_inc(yn_done[b], 1)

                def split_yT(b, i, c):
                    act.wait_ge(yT_ps[b], CH * i + c + 1)
                    act.wait_ge(o_ps[b], i)
                    act.activation(yTh[b][:, :, c * P:(c + 1) * P],
                                   Q(b, c)[:, :].rearrange("p (k t) -> p k t", k=KI),
                                   ACT.Copy).then_inc(yTh_done[b], 1)

                def split_y1(b, i):
                    act.wait_ge(y1_done[b], i + 1)
                    act.wait_ge(glu_ps[b], i)
                    act.activation(y1h[b][:, :, :], y1[b][:, :, :], ACT.Copy).then_inc(y1h_done[b], 1)

                def halve_and_tanh(b, i):
                    act.wait_ge(glu_ps[b], i + 1)
                    act.wait_ge(ag_done[b], i)
                    act.wait_ge(xo_done[b], i)
                    for m in range(KD):
                        act.activation(half_a[b][:, m, :], Q(b, 1)[:, m * GROUP:(m + 1) * GROUP], ACT.Identity,
                                       bias=glub[:, m:m + 1], scale=0.5)
                    for m in range(KD):
                        last = act.activation(sg[b][:, m, :], Q(b, 2)[:, m * GROUP:(m + 1) * GROUP], ACT.Tanh,
                                              bias=glub[:, KD + m:KD + m + 1], scale=0.5)
                    last.then_inc(tanh_done[b], 1)

                def half(first, second, tail, more=True):
                    if second:
                        silu_z(*second, 1)
                        silu_xbc(*second, 1)
                    if tail:
                        split_y1(*tail)
                    if first:
                        modulate(*first)
                    if second:
                        copy_tokens(*second, 0)
                        silu_xbc(*second, 2)
                        decays(*second, 0)
                    if tail:
                        halve_and_tanh(*tail)
                    if second:
                        decays(*second, 1)
                    if first:
                        exp_dt(*first)
                    if second:
                        copy_tokens(*second, 1)
                        copy_b(*second)
                    if first:
                        copy_xbc(*first, 0)
                        start_conv(*first, 0)
                    if second:
                        squares(*second, 0)
                        norm_y(*second, 0)
                    if first:
                        start_conv(*first, 1)
                    if second:
                        squares(*second, 1)
                        split_yT(*second, 0)
                    if first:
                        copy_xbc(*first, 1)
                    if second:
                        norm_y(*second, 1)
                    if first:
                        copy_xbc(*first, 2)
                        exp_sums(*first)
                    if second:
                        split_yT(*second, 1)
                    if first:
                        start_conv(*first, 2)
                        silu_xbc(*first, 0)
                        silu_z(*first, 0)

                halves(act, half)

            @block.vector
            def _(dve):
                def norm1(b, i):
                    dve.wait_ge(x_in[b], 16 * (i + 1))
                    for c in range(CH):
                        last = dve.bn_stats(st1[b][:, c, :], xt[b][:, c, :])
                    last.then_inc(ln1[b], 1)
                    dve.wait_ge(ln1[b], 3 * i + 1)
                    stand_alone(dve, held_dve)
                    for c in range(CH):
                        last = dve.bn_aggr(mv1[b][:, c, :], st1[b][:, c, :])
                    last.then_inc(ln1[b], 1)
                    dve.wait_ge(ln1[b], 3 * i + 2)
                    dve.tensor_scalar(rs1[b][:, :], mv1[b][:, :, 1], EPS, None, ALU.add).then_inc(ln1[b], 1)

                def apply1(b, i):
                    dve.wait_ge(root1[b], i + 1)
                    for c in range(CH):
                        last = dve.tensor_scalar(xt[b][:, c, :], xt[b][:, c, :], mv1[b][:, c, 0:1],
                                                 rs1[b][:, c:c + 1], ALU.subtract, ALU.mult)
                    last.then_inc(xn_done[b], 1)

                def conv(b, i, pair):
                    n = MC * (TAPS - 1) * i
                    if pair == 0:
                        dve.wait_ge(halo_done[b], i + 1)
                    dve.wait_ge(xc_done[b], 3 * i + pair + 1)
                    dve.wait_ge(tap0_done[b], 3 * i + pair + 1)
                    for tap in range(TAPS - 1):
                        for m in (2 * pair, 2 * pair + 1):
                            if tap > 0:
                                dve.wait_ge(tap_done[b], n + (pair * (TAPS - 1) + tap - 1) * 2 + m % 2 + 1)
                            dve.scalar_tensor_tensor(cv[b][:, m, :], xc[b][:, m, tap:tap + GROUP],
                                                     convw[:, m, tap:tap + 1], cv[b][:, m, :],
                                                     ALU.mult, ALU.add).then_inc(tap_done[b], 1)

                def softplus_head(b, i):
                    v, size = dts[b][:, 0, :, :], dts[b][:, 1, :, :]
                    dve.wait_ge(dt_ps[b], i + 1)
                    dve.wait_ge(xdt_done[b], CH * i)
                    dve.wait_ge(au_done[b], CH * i)
                    dve.wait_ge(xend_done[b], CH * i)
                    dve.wait_ge(sums_ps[b], i)
                    dve.tensor_tensor(v, Q(b, 3)[:, 0:CH * H].rearrange("p (c h) -> p c h", c=CH),
                                      dtb[:, :, :], ALU.add).then_inc(dt_link[b], 1)
                    dve.wait_ge(dt_link[b], DT_LINKS * i + 1)
                    dve.scalar_tensor_tensor(size, v, -1.0, v, ALU.mult, ALU.max).then_inc(dt_abs[b], 1)

                def softplus_step(b, i, n):
                    v, _, u, s, s2, acc, dt, a = (dts[b][:, k, :, :] for k in range(8))
                    if n == 0:
                        dve.wait_ge(dt_exp[b], i + 1)
                    else:
                        dve.wait_ge(dt_link[b], DT_LINKS * i + 1 + n)
                    if n == 0:
                        last = dve.tensor_scalar(s, u, 2.0, None, ALU.add)
                    elif n == 1:
                        last = dve.reciprocal(s, s)
                    elif n == 2:
                        last = dve.tensor_tensor(s, s, u, ALU.mult)
                    elif n == 3:
                        last = dve.tensor_tensor(s2, s, s, ALU.mult)
                    elif n == 4:
                        last = dve.tensor_scalar(acc, s2, SERIES[0], None, ALU.mult)
                    elif n < 5 + len(SERIES) - 2:
                        last = dve.scalar_tensor_tensor(acc, acc, SERIES[n - 4], s2, ALU.add, ALU.mult)
                    elif n == DT_LINKS - 4:
                        last = dve.scalar_tensor_tensor(acc, acc, 1.0, s, ALU.add, ALU.mult)
                    elif n == DT_LINKS - 3:
                        last = dve.tensor_scalar(v, v, 0.0, None, ALU.max)
                    elif n == DT_LINKS - 2:
                        last = dve.scalar_tensor_tensor(dt, acc, 2.0, v, ALU.mult, ALU.add)
                    else:
                        dve.scalar_tensor_tensor(a, dt, -1.0, negA[:, :, :], ALU.mult, ALU.mult
                                                 ).then_inc(a_done[b], 1)
                        return
                    last.then_inc(dt_link[b], 1)

                def split_a(b, i):
                    dve.wait_ge(a_done[b], i + 1)
                    dve.wait_ge(lo_done[b], CH * i)
                    dve.tensor_copy(a_hi[b][:, :, :], dts[b][:, 7, :, :]).then_inc(ahi_done[b], 1)
                    dve.wait_ge(ahi_done[b], i + 1)
                    dve.tensor_tensor(a_lo[b][:, :, :], dts[b][:, 7, :, :], a_hi[b][:, :, :].bitcast(F32),
                                      ALU.subtract).then_inc(alo_done[b], 1)

                def mask_a_lo(b, i, c):
                    dve.wait_ge(alo_done[b], i + 1)
                    dve.wait_ge(dec_ps[b], CH * i + c)
                    dve.tensor_tensor(masked_lo[b][:, :, :], upto[:, :].unsqueeze(1).to_broadcast([P, H, P]),
                                      a_lo[b][:, c, :].unsqueeze(2).to_broadcast([P, H, P]),
                                      ALU.mult).then_inc(lo_done[b], 1)

                def mask_bc(b, i):
                    dve.wait_ge(btok_done[b], i + 1)
                    dve.wait_ge(w_done[b], CH * i)
                    dve.tensor_tensor(gm[b][:, :, :], Q(b, 2)[:, GROUP:2 * GROUP].rearrange("p (c t) -> p c t", c=CH),
                                      upto[:, :].unsqueeze(1).to_broadcast([P, CH, P]),
                                      ALU.mult).then_inc(gm_done[b], 1)

                def times_decay(b, i, c):
                    dve.wait_ge(dec_done[b], CH * i + c + 1)
                    dve.wait_ge(gm_done[b], i + 1)
                    dve.tensor_tensor(dec[b][:, c, :, :], dec[b][:, c, :, :],
                                      gm[b][:, c, :].unsqueeze(1).to_broadcast([P, H, P]),
                                      ALU.mult).then_inc(w_done[b], 1)

                def scale_from_state(b, i, c):
                    dve.wait_ge(yst_ps[b], CH * i + c + 1)
                    dve.wait_ge(ex_done[b], i + 1)
                    dve.wait_ge(yT_ps[b], CH * i)
                    dve.tensor_tensor(yy[b][:, c, :].rearrange("p (h e) -> p h e", h=H),
                                      Q(b, 2)[:, :].rearrange("p (h e) -> p h e", h=H),
                                      ex[b][:, 0, c, :].unsqueeze(2).to_broadcast([P, H, HD]),
                                      ALU.mult).then_inc(y1s_done[b], 1)

                def add_within(b, i, c):
                    dve.wait_ge(skip_done[b], CH * i + c + 1)
                    dve.wait_ge(yin_ps[b], CH * i + c + 1)
                    dve.tensor_tensor(yy[b][:, c, :], yy[b][:, c, :], Q(b, c)[:, :],
                                      ALU.add).then_inc(y2s_done[b], 1)

                def new_state(b, i, c):
                    dve.wait_ge(add_ps[b], CH * i + c + 1)
                    dve.wait_ge(sdec_done[b], CH * i + c + 1)
                    dve.tensor_tensor(state[b][:, :], state[b][:, :], Q(b, 3)[:, :], ALU.add).then_inc(st_done[b], 1)

                def mean_square(b, i, c):
                    dve.wait_ge(sq_done[b], CH * i + c + 1)
                    dve.tensor_scalar(rr[b][:, c:c + 1], ss[b][:, c:c + 1], 1.0 / DI, EPS, ALU.mult,
                                      ALU.add).then_inc(ms_done[b], 1)

                def split_yT(b, i, c):
                    dve.wait_ge(yTh_done[b], CH * i + c + 1)
                    tok = slice(c * P, (c + 1) * P)
                    dve.tensor_tensor(yTl[b][:, :, tok], Q(b, c)[:, :].rearrange("p (k t) -> p k t", k=KI),
                                      yTh[b][:, :, tok].bitcast(F32), ALU.subtract).then_inc(yTl_done[b], 1)

                def add_h(b, i):
                    dve.wait_ge(o_ps[b], i + 1)
                    dve.wait_ge(y2T_ps[b], i)
                    dve.wait_ge(hT_done[b], i + 1)
                    dve.tensor_tensor(y1[b][:, :, :], Q(b, 2)[:, :].rearrange("p (k t) -> p k t", k=KD),
                                      hT[b][:, :, :], ALU.add).then_inc(y1_done[b], 1)

                def gated(b, i):
                    dve.wait_ge(tanh_done[b], i + 1)
                    dve.scalar_tensor_tensor(sg[b][:, :, :], sg[b][:, :, :], 1.0, half_a[b][:, :, :],
                                             ALU.add, ALU.mult).then_inc(ag_done[b], 1)
                    dve.wait_ge(ag_done[b], i + 1)
                    dve.wait_ge(y1l_done[b], i + 1)
                    dve.tensor_tensor(y1[b][:, :, :], y1[b][:, :, :], sg[b][:, :, :], ALU.add).then_inc(y2_done[b], 1)

                def norm2(b, i):
                    dve.wait_ge(y2T_ps[b], i + 1)
                    y = Q(b, 1)[:, :].rearrange("p (c d) -> p c d", c=CH)
                    for c in range(CH):
                        last = dve.bn_stats(st[b][:, c, :], y[:, c, :])
                    last.then_inc(ln2[b], 1)
                    dve.wait_ge(ln2[b], 3 * i + 1)
                    stand_alone(dve, held_dve)
                    for c in range(CH):
                        last = dve.bn_aggr(mv[b][:, c, :], st[b][:, c, :])
                    last.then_inc(ln2[b], 1)
                    dve.wait_ge(ln2[b], 3 * i + 2)
                    dve.tensor_scalar(rs[b][:, :], mv[b][:, :, 1], EPS, None, ALU.add).then_inc(ln2[b], 1)

                def apply2(b, i):
                    y = Q(b, 1)[:, :].rearrange("p (c d) -> p c d", c=CH)
                    xo = sg[b][:, :, :].rearrange("p k t -> p (k t)").rearrange("p (c d) -> p c d", c=CH)
                    for c in range(CH):
                        last = dve.scalar_tensor_tensor(xo[:, c, :], y[:, c, :], mv[b][:, c, 0:1],
                                                        gate_ln[:, b, 0, :], ALU.subtract, ALU.mult)
                    last.then_inc(xo_link[b], 1)
                    dve.wait_ge(xo_link[b], i + 1)
                    dve.wait_ge(root2[b], i + 1)
                    dve.wait_ge(xb_done[b], i + 1)
                    for c in range(CH):
                        last = dve.scalar_tensor_tensor(xr[b][:, c, :], xo[:, c, :], rs[b][:, c:c + 1],
                                                        xr[b][:, c, :], ALU.mult, ALU.add)
                    last.then_inc(xo_done[b], 1)

                def half(first, second, tail, more=True):
                    if tail:
                        add_h(*tail)
                    if second:
                        conv(*second, 2)
                    if tail:
                        new_state(*tail, 1)
                    if second:
                        mask_a_lo(*second, 1)
                    if more:
                        norm1(*following(second))
                    if first:
                        softplus_head(*first)
                    if tail:
                        gated(*tail)
                    if first:
                        for step in range(5):
                            softplus_step(*first, step)
                    if second:
                        mask_bc(*second)
                    if tail:
                        norm2(*tail)
                    if second:
                        times_decay(*second, 0)
                        scale_from_state(*second, 0)
                        new_state(*second, 0)
                        times_decay(*second, 1)
                        add_within(*second, 0)
                    if first:
                        softplus_step(*first, 5)
                    if second:
                        scale_from_state(*second, 1)
                    if first:
                        softplus_step(*first, 6)
                    if tail:
                        apply2(*tail)
                    if first:
                        softplus_step(*first, 7)
                    if second:
                        mean_square(*second, 0)
                    if first:
                        softplus_step(*first, 8)
                        softplus_step(*first, 9)
                    if second:
                        add_within(*second, 1)
                    if first:
                        softplus_step(*first, 10)
                        conv(*first, 0)
                    if second:
                        mean_square(*second, 1)
                    if first:
                        for step in range(11, DT_LINKS):
                            softplus_step(*first, step)
                    if second:
                        split_yT(*second, 0)
                    if first:
                        split_a(*first)
                        mask_a_lo(*first, 0)
                    if second:
                        split_yT(*second, 1)
                    if more:
                        apply1(*following(second))
                    if first:
                        conv(*first, 1)

                for b in range(NB):
                    norm1(b, 1)
                    apply1(b, 1)
                halves(dve, half)

            @block.gpsimd
            def _(pool):
                def root(out, n):
                    return pool.tensor_tensor(out, out, minus_half[:, 0:n], ALU.pow)

                def root_norm1(b, i):
                    pool.wait_ge(ln1[b], 3 * i + 3)
                    root(rs1[b][:, :], CH).then_inc(root1[b], 1)

                def root_norm2(b, i):
                    pool.wait_ge(ln2[b], 3 * i + 3)
                    root(rs[b][:, :], CH).then_inc(root2[b], 1)

                def root_y(b, i, c):
                    pool.wait_ge(ms_done[b], CH * i + c + 1)
                    root(rr[b][:, c:c + 1], 1).then_inc(rr_done[b], 1)

                def split_h(b, i):
                    pool.wait_ge(hT_done[b], i + 1)
                    pool.wait_ge(hTh_done[b], i + 1)
                    pool.tensor_tensor(hTl[b][:, :, :], hT[b][:, :, :], hTh[b][:, :, :].bitcast(F32),
                                       ALU.subtract).then_inc(hTl_done[b], 1)

                def mask_a(b, i, c):
                    pool.wait_ge(a_done[b], i + 1)
                    pool.wait_ge(dec_ps[b], CH * i + c)
                    pool.tensor_tensor(masked_hi[b][:, :, :], upto[:, :].unsqueeze(1).to_broadcast([P, H, P]),
                                       dts[b][:, 7, c, :].unsqueeze(2).to_broadcast([P, H, P]),
                                       ALU.mult).then_inc(au_done[b], 1)

                def end_weights(b, i):
                    pool.wait_ge(ex_done[b], i + 1)
                    pool.tensor_tensor(dts[b][:, 1, :, :], dts[b][:, 6, :, :], ex[b][:, 1, :, :],
                                       ALU.mult).then_inc(wend_done[b], 1)

                def times_dt(b, i, c):
                    pool.wait_ge(xtok_done[b], CH * i + c + 1)
                    pool.wait_ge(sq_done[b], CH * i)
                    pool.tensor_tensor(xdt[b][:, c, :].rearrange("p (h e) -> p h e", h=H),
                                       xtok[b][:, c, :].rearrange("p (h e) -> p h e", h=H),
                                       dts[b][:, 6, c, :].unsqueeze(2).to_broadcast([P, H, HD]),
                                       ALU.mult).then_inc(xdt_done[b], 1)

                def times_end(b, i, c):
                    pool.wait_ge(wend_done[b], i + 1)
                    pool.wait_ge(xtok_done[b], CH * i + c + 1)
                    pool.wait_ge(add_ps[b], CH * i)
                    pool.wait_ge(ag_done[b], i)
                    pool.tensor_tensor(xend[b][:, c, :].rearrange("p (h e) -> p h e", h=H),
                                       xtok[b][:, c, :].rearrange("p (h e) -> p h e", h=H),
                                       dts[b][:, 1, c, :].unsqueeze(2).to_broadcast([P, H, HD]),
                                       ALU.mult).then_inc(xend_done[b], 1)

                def times_d(b, i, c):
                    pool.wait_ge(xdt_done[b], CH * i + c + 1)
                    pool.wait_ge(xend_done[b], CH * i + c + 1)
                    pool.tensor_tensor(xtok[b][:, c, :], xtok[b][:, c, :], dskip[:, :],
                                       ALU.mult).then_inc(dx_done[b], 1)

                def add_d(b, i, c):
                    pool.wait_ge(dx_done[b], CH * i + c + 1)
                    pool.wait_ge(y1s_done[b], CH * i + c + 1)
                    pool.tensor_tensor(yy[b][:, c, :], yy[b][:, c, :], xtok[b][:, c, :],
                                       ALU.add).then_inc(skip_done[b], 1)

                def decay_state(b, i, c):
                    pool.wait_ge(yst_ps[b], CH * i + c + 1)
                    s = state[b][:, :].rearrange("p (h e) -> p h e", h=H)
                    pool.tensor_tensor(s, s, ex[b][:, 2, c, :].unsqueeze(2).to_broadcast([P, H, HD]),
                                       ALU.mult).then_inc(sdec_done[b], 1)

                def gate_y(b, i, c):
                    y = yy[b][:, c, :]
                    pool.wait_ge(y2s_done[b], CH * i + c + 1)
                    pool.tensor_tensor(y, y, zs[b][:, c, :], ALU.mult).then_inc(y4_done[b], 1)

                def split_y1(b, i):
                    pool.wait_ge(y1h_done[b], i + 1)
                    pool.wait_ge(y1_done[b], i + 1)
                    pool.tensor_tensor(y1l[b][:, :, :], y1[b][:, :, :], y1h[b][:, :, :].bitcast(F32),
                                       ALU.subtract).then_inc(y1l_done[b], 1)

                def shift_x(b, i):
                    pool.wait_ge(xr_in[b], 16 * (i + 1))
                    pool.tensor_tensor(xr[b][:, :, :], xr[b][:, :, :],
                                       gate_ln[:, b, 1, :].unsqueeze(1).to_broadcast([P, CH, D]),
                                       ALU.add).then_inc(xb_done[b], 1)

                def half(first, second, tail, more=True):
                    if tail:
                        decay_state(*tail, 1)
                    if second:
                        mask_a(*second, 0)
                    if tail:
                        shift_x(*tail)
                        split_y1(*tail)
                    if second:
                        end_weights(*second)
                        mask_a(*second, 1)
                    if first:
                        split_h(*first)
                    if second:
                        times_end(*second, 0)
                        times_dt(*second, 0)
                        times_d(*second, 0)
                        times_end(*second, 1)
                        times_dt(*second, 1)
                        decay_state(*second, 0)
                    if tail:
                        root_norm2(*tail)
                    if second:
                        add_d(*second, 0)
                        times_d(*second, 1)
                        gate_y(*second, 0)
                        add_d(*second, 1)
                        root_y(*second, 0)
                        gate_y(*second, 1)
                        root_y(*second, 1)
                    if more:
                        root_norm1(*following(second))

                for b in range(NB):
                    root_norm1(b, 1)
                halves(pool, half)


def experts(nc, sem, prime, t, mod, gate_b_row, ident, minus_half, bank, x2_dram, out):
    ALL = NE + 1
    GROUPS = NB * MSTEPS
    with ExitStack() as ctx:
        def sb(name, shape, dt=F32):
            return ctx.enter_context(nc.sbuf_tensor(name, shape, dt))

        def two(name, shape, dt=F32):
            return [sb(f"{name}{b}", shape, dt) for b in range(2)]

        EW = KD * 2 * INTER + D
        wh = sb("wh", [P, ALL, EW], F32R)
        wl = sb("wl", [P, ALL, EW], F32R)
        gatew = sb("gatew", [P, KD, NE])
        gateb = sb("gateb", [P, MT, NE])
        raw = [sb(f"raw{r}", [P, EW]) for r in range(4)]
        x2 = sb("x2", [P, MT, D])
        st = sb("mst", [P, MT, 6])
        mv = sb("mmv", [P, MT, 2])
        rs = sb("mrs", [P, MT])
        hT = sb("mhT", [P, KD, MGROUP])
        hh = two("mhh", [P, KD, MGROUP], F32R)
        hl = two("mhl", [P, KD, MGROUP], F32R)
        score = sb("score", [P, MT, NE])
        biased = sb("biased", [P, MT, NE])
        top = sb("top", [P, MT, 8])
        best = sb("best", [P, MT, 8])
        rest = sb("rest", [P, MT, NE])
        wsum = sb("wsum", [P, MT])
        comb = two("comb", [P, MT, NE])
        gs = two("gs", [P, MGROUP])
        ff = two("ff", [P, MGROUP])
        fh = two("fh", [P, MGROUP], F32R)
        fl = two("fl", [P, MGROUP], F32R)
        xres = sb("xres", [P, MT, D])
        acc = sb("acc", [P, MT, D])
        yo = sb("yo", [P, MT, D])

        raw_in = [sem(f"ew_in{r}") for r in range(len(raw))]
        hi_done = sem("ew_hi")
        lo_done = sem("ew_lo")
        gate_w_in = sem("gate_w_in")
        AHEAD = 6

        def w13(half, e, k, gate):
            w = (wh, wl)[half]
            return w[:, e, k * 2 * INTER + (1 - gate) * INTER:k * 2 * INTER + (2 - gate) * INTER]

        def w2(half, e):
            return (wh, wl)[half][:, e, KD * 2 * INTER:EW]

        GATE, UP = (bank[0], bank[1]), (bank[2], bank[3])
        PREP = bank[5]
        DOWN = (bank[6], bank[7])

        ROUTE_LINKS = 10
        counts = []

        def counted(name, per_group):
            counts.append((sem(name), per_group))
            return counts[-1][0]

        x2_in = counted("x2_in", 16)
        ln = counted("mln", 3)
        mroot = counted("mroot", 1)
        n_done = counted("n_done", 1)
        nT_ps = counted("nT_ps", KD)
        mh_done = counted("mh_done", KD)
        mhh_done = counted("mhh_done", KD)
        mhl_done = counted("mhl_done", KD)
        logit_ps = counted("logit_ps", 1)
        tanh_done = counted("tanh_done", 1)
        route = counted("route", ROUTE_LINKS)
        comb_done = counted("comb_done", 1)
        gate_ps = counted("gate_ps", ALL)
        up_ps = counted("up_ps", ALL)
        gs_done = counted("gs_done", ALL)
        ff_done = counted("ff_done", ALL)
        fh_done = counted("fh_done", ALL)
        fl_done = counted("fl_done", ALL)
        down_ps = counted("down_ps", 2 * ALL)
        acc_done = counted("acc_done", 2 * ALL)
        scaled = counted("scaled", 1)
        res_in = counted("res_in", 16)
        yo_done2 = counted("yo_done2", 1)
        out_stored = counted("out_stored", 16)

        prime(counts)
        held_dve = sem("mheld_dve")

        def x2_rows(b, j):
            return x2_dram[b, bass.ds(j * (MT // CH), MT // CH)].rearrange("s p c d -> p s c d")

        def tiles(ap):
            return ap.rearrange("p (s c) d -> p s c d", c=CH)

        def walk(eng, prepare_first, group):
            prepare_first()
            group(1, 0, 0, first=True)
            with eng.Fori(0, MSTEPS - 1) as i:
                group(2 * i + 2, 1, i)
                group(2 * i + 3, 0, i + 1)
            group(GROUPS, 1, MSTEPS - 1, last=True)

        with nc.Block() as block:
            @block.sync
            def _(sp):
                def load(n, b, j):
                    sp.wait_ge(nT_ps, KD * n)
                    sp.dma_start(tiles(x2[:, :, :]), x2_rows(b, j)).then_inc(x2_in, 16)

                def store(n, b, j):
                    sp.wait_ge(yo_done2, n + 1)
                    sp.dma_start(out[b, bass.ds(j * MGROUP, MGROUP), :].rearrange("(c p) d -> p c d", p=P),
                                 yo[:, :, :]).then_inc(out_stored, 16)

                def group(n, b, j, first=False, last=False):
                    if not last:
                        load(n + 1, 1 - b, j + b)
                    if first:
                        load_weights(range(AHEAD, ALL))
                    else:
                        store(n - 1, 1 - b, j - 1 + b)
                    sp.dma_start(tiles(xres[:, :, :]), x2_rows(b, j)).then_inc(res_in, 16)
                    if last:
                        store(n, b, j)

                def load_weights(experts):
                    for e in experts:
                        if e >= len(raw):
                            sp.wait_ge(lo_done, e - len(raw) + 1)
                        sp.dma_start(raw[e % len(raw)][:, :], t["experts"][e]).then_inc(raw_in[e % len(raw)], 16)

                def prepare_first():
                    load(1, 0, 0)
                    sp.dma_start(gatew[:, :, :], t["gate_w"]).then_inc(gate_w_in, 16)
                    sp.dma_start(gateb[:, :, :], t["gate_b"]).then_inc(gate_w_in, 16)
                    load_weights(range(AHEAD))

                walk(sp, prepare_first, group)
                sp.wait_ge(out_stored, 16 * (GROUPS + 1))

            @block.tensor
            def _(pe):
                def transpose_n(k, n):
                    if k == 0:
                        pe.wait_ge(n_done, n + 1)
                        pe.wait_ge(tanh_done, n)
                    else:
                        pe.wait_ge(mhh_done, KD * n + k)
                    for c in range(MT):
                        last = pe.transpose(PREP[:, c * P:(c + 1) * P], x2[:, c, k * P:(k + 1) * P], ident[:, :])
                    last.then_inc(nT_ps, 1)

                def logits(n, first):
                    if first:
                        pe.wait_ge(gate_w_in, 32)
                    pe.wait_ge(mh_done, KD * n + KD)
                    pe.wait_ge(mhh_done, KD * n + KD)
                    for c in range(MT):
                        for k in range(KD):
                            last = pe.matmul(PREP[:, c * NE:(c + 1) * NE], hT[:, k, c * P:(c + 1) * P],
                                             gatew[:, k, :], start=(k == 0), stop=(k == KD - 1))
                    last.then_inc(logit_ps, 1)

                def prepare(slot, n, first=False):
                    if slot in (3, 5):
                        transpose_n(slot // 2 - 1, n)
                    if slot == 7:
                        logits(n, first)

                def up(e, n, b, first):
                    if first:
                        pe.wait_ge(lo_done, e + 1)
                    s = n * ALL + e
                    if e == 0:
                        pe.wait_ge(mhh_done, KD * n + KD)
                        pe.wait_ge(mhl_done, KD * n + KD)
                    par = e % 2
                    if e >= 2:
                        pe.wait_ge(ff_done, s - 1)
                    else:
                        pe.wait_ge(ff_done, n * ALL)
                    for k in range(KD):
                        last = split3(pe, GATE[par][:, :], w13(0, e, k, 1), w13(1, e, k, 1),
                                      hh[b][:, k, :], hl[b][:, k, :], k == 0, k == KD - 1)
                    last.then_inc(gate_ps, 1)
                    for k in range(KD):
                        last = split3(pe, UP[par][:, :], w13(0, e, k, 0), w13(1, e, k, 0),
                                      hh[b][:, k, :], hl[b][:, k, :], k == 0, k == KD - 1)
                    last.then_inc(up_ps, 1)

                def down(e, n):
                    s = n * ALL + e
                    pe.wait_ge(fh_done, s + 1)
                    pe.wait_ge(fl_done, s + 1)
                    for c in range(MT):
                        tok = slice(c * P, (c + 1) * P)
                        if c % 2 == 0:
                            pe.wait_ge(acc_done, 2 * s - 1 + c // 2)
                        last = split3(pe, DOWN[c // 2][:, c % 2 * D:(c % 2 + 1) * D], fh[e % 2][:, tok],
                                      fl[e % 2][:, tok], w2(0, e), w2(1, e), c % 2 == 0, True)
                        if c % 2 == 1:
                            last.then_inc(down_ps, 1)

                def group(n, b, j, first=False, last=False):
                    for e in range(ALL):
                        up(e, n, b, first)
                        if e > 0:
                            down(e - 1, n)
                        elif not first:
                            down(ALL - 1, n - 1)
                        if not last:
                            prepare(e, n + 1)
                    if last:
                        down(ALL - 1, n)

                def prepare_first():
                    for slot in range(ALL):
                        prepare(slot, 1, first=True)

                walk(pe, prepare_first, group)

            @block.scalar
            def _(act):
                def modulate(k, n, b):
                    act.wait_ge(nT_ps, KD * n + k + 1)
                    act.wait_ge(logit_ps, n)
                    act.wait_ge(mhl_done, KD * n + k)
                    args = dict(bias=mod[b][:, 3, k:k + 1], scale=mod[b][:, 2, k:k + 1])
                    act.activation(hT[:, k, :], PREP[:, :], ACT.Identity, **args).then_inc(mh_done, 1)
                    act.activation(hh[b][:, k, :], PREP[:, :], ACT.Identity, **args).then_inc(mhh_done, 1)

                def prepare(slot, n, b):
                    if slot in (4, 6):
                        modulate(slot // 2 - 2, n, b)
                    if slot == 8:
                        act.wait_ge(logit_ps, n + 1)
                        act.wait_ge(comb_done, n)
                        act.activation(score[:, :, :].rearrange("p c e -> p (c e)"), PREP[:, 0:MT * NE],
                                       ACT.Tanh, scale=0.5).then_inc(tanh_done, 1)

                def silu_gate(e, n):
                    s = n * ALL + e
                    act.wait_ge(gate_ps, s + 1)
                    if e >= 2:
                        act.wait_ge(ff_done, s - 1)
                    else:
                        act.wait_ge(ff_done, n * ALL)
                    act.activation(gs[e % 2][:, :], GATE[e % 2][:, :], ACT.Silu).then_inc(gs_done, 1)

                def hi(e, n):
                    s = n * ALL + e
                    act.wait_ge(ff_done, s + 1)
                    act.wait_ge(down_ps, 2 * (s - 1) if e >= 2 else 2 * n * ALL)
                    act.activation(fh[e % 2][:, :], ff[e % 2][:, :], ACT.Copy).then_inc(fh_done, 1)

                def group(n, b, j, first=False, last=False):
                    for e in range(ALL):
                        silu_gate(e, n)
                        if not last:
                            prepare(e, n + 1, 1 - b)
                        hi(e, n)
                        if first and e + AHEAD < ALL:
                            weights_hi(e + AHEAD)

                def weights_hi(e):
                    act.wait_ge(raw_in[e % len(raw)], 16 * (e // len(raw) + 1))
                    act.activation(wh[:, e, :], raw[e % len(raw)][:, :], ACT.Copy).then_inc(hi_done, 1)

                def prepare_first():
                    weights_hi(0)
                    prepare(4, 1, 0)
                    weights_hi(1)
                    prepare(6, 1, 0)
                    weights_hi(2)
                    prepare(8, 1, 0)
                    for e in range(3, AHEAD):
                        weights_hi(e)

                walk(act, prepare_first, group)

            @block.vector
            def _(dve):
                def norm(n):
                    dve.wait_ge(x2_in, 16 * (n + 1))
                    for c in range(MT):
                        last = dve.bn_stats(st[:, c, :], x2[:, c, :])
                    last.then_inc(ln, 1)
                    dve.wait_ge(ln, 3 * n + 1)
                    stand_alone(dve, held_dve)
                    for c in range(MT):
                        last = dve.bn_aggr(mv[:, c, :], st[:, c, :])
                    last.then_inc(ln, 1)
                    dve.wait_ge(ln, 3 * n + 2)
                    dve.tensor_scalar(rs[:, :], mv[:, :, 1], EPS, None, ALU.add).then_inc(ln, 1)

                def apply(n):
                    dve.wait_ge(mroot, n + 1)
                    for c in range(MT):
                        last = dve.tensor_scalar(x2[:, c, :], x2[:, c, :], mv[:, c, 0:1], rs[:, c:c + 1],
                                                 ALU.subtract, ALU.mult)
                    last.then_inc(n_done, 1)

                def routing(n, b, first, part):
                    k = [(0, 3, 6)[part]]

                    def link(ins):
                        k[0] += 1
                        ins.then_inc(route, 1)

                    def linked():
                        dve.wait_ge(route, ROUTE_LINKS * n + k[0])

                    if part == 0:
                        dve.wait_ge(tanh_done, n + 1)
                        if first:
                            dve.wait_ge(gate_w_in, 32)
                        else:
                            dve.wait_ge(acc_done, 2 * ALL * (n - 1))
                        link(dve.tensor_scalar(score[:, :, :], score[:, :, :], 0.5, 0.5, ALU.mult, ALU.add))
                        linked()
                        link(dve.tensor_tensor(biased[:, :, :], score[:, :, :], gateb[:, :, :], ALU.add))
                        linked()
                        stand_alone(dve, held_dve)
                        for c in range(MT):
                            last = dve.max(top[:, c, :], biased[:, c, :])
                        link(last)
                    elif part == 1:
                        linked()
                        link(dve.tensor_copy(best[:, :, 0:TOPK], top[:, :, 0:TOPK]))
                        linked()
                        stand_alone(dve, held_dve)
                        for c in range(MT):
                            last = dve.match_replace(rest[:, c, :], best[:, c, :], biased[:, c, :], -3.0e38)
                        link(last)
                        linked()
                        link(dve.tensor_scalar(rest[:, :, :], rest[:, :, :], -1.0e38, None, ALU.is_lt))
                    else:
                        linked()
                        link(dve.tensor_tensor(rest[:, :, :], score[:, :, :], rest[:, :, :], ALU.mult))
                        linked()
                        link(dve.tensor_reduce(wsum[:, :], rest[:, :, :], mybir.AxisListType.X, ALU.add))
                        linked()
                        link(dve.reciprocal(wsum[:, :], wsum[:, :]))
                        linked()
                        link(dve.tensor_scalar(wsum[:, :], wsum[:, :], ROUTE_SCALE, None, ALU.mult))
                        linked()
                        assert k[0] == ROUTE_LINKS
                        dve.tensor_tensor(comb[b][:, :, :], rest[:, :, :],
                                          wsum[:, :].unsqueeze(2).to_broadcast([P, MT, NE]),
                                          ALU.mult).then_inc(comb_done, 1)

                def prepare(slot, n, b, first=False):
                    if slot == 1:
                        norm(n)
                    if slot == 2:
                        apply(n)
                    if slot in (9, 10, 11):
                        routing(n, b, first, slot - 9)

                def times(e, n):
                    s = n * ALL + e
                    g = gs[e % 2][:, :]
                    dve.wait_ge(gs_done, s + 1)
                    dve.wait_ge(up_ps, s + 1)
                    if e >= 2:
                        dve.wait_ge(fl_done, s - 1)
                    else:
                        dve.wait_ge(fl_done, n * ALL)
                    dve.tensor_tensor(ff[e % 2][:, :], g, UP[e % 2][:, :], ALU.mult).then_inc(ff_done, 1)

                def accumulate(e, n, b):
                    s = n * ALL + e
                    for half in range(2):
                        dve.wait_ge(down_ps, 2 * s + half + 1)
                        if e == 0:
                            dve.wait_ge(comb_done, n + 1)
                            dve.wait_ge(scaled, n)
                        else:
                            dve.wait_ge(acc_done, 2 * s - 1 + half)
                        ps = DOWN[half][:, :].rearrange("p (c d) -> p c d", c=2)
                        a = acc[:, 2 * half:2 * half + 2, :]
                        if e == ALL - 1:
                            last = dve.tensor_tensor(a, a, ps, ALU.add)
                        else:
                            for c in range(2):
                                w = comb[b][:, 2 * half + c, e:e + 1]
                                if e == 0:
                                    last = dve.tensor_scalar(a[:, c, :], ps[:, c, :], w, None, ALU.mult)
                                else:
                                    last = dve.scalar_tensor_tensor(a[:, c, :], ps[:, c, :], w, a[:, c, :],
                                                                    ALU.mult, ALU.add)
                        last.then_inc(acc_done, 1)

                def scale(n, b):
                    dve.wait_ge(acc_done, 2 * ALL * (n + 1))
                    dve.wait_ge(out_stored, 16 * n)
                    dve.tensor_tensor(yo[:, :, :], acc[:, :, :],
                                      gate_b_row[b][:, :].unsqueeze(1).to_broadcast([P, MT, D]),
                                      ALU.mult).then_inc(scaled, 1)

                def group(n, b, j, first=False, last=False):
                    for e in range(ALL):
                        times(e, n)
                        if e > 0:
                            accumulate(e - 1, n, b)
                        elif not first:
                            accumulate(ALL - 1, n - 1, 1 - b)
                            scale(n - 1, 1 - b)
                        if not last:
                            prepare(e, n + 1, 1 - b)
                        if first and e + AHEAD < ALL:
                            weights_lo(e + AHEAD)
                    if last:
                        accumulate(ALL - 1, n, b)
                        scale(n, b)

                def weights_lo(e):
                    dve.wait_ge(hi_done, e + 1)
                    dve.tensor_tensor(wl[:, e, :], raw[e % len(raw)][:, :], wh[:, e, :].bitcast(F32),
                                      ALU.subtract).then_inc(lo_done, 1)

                def prepare_first():
                    dve.memset(best[:, :, :], 3.0e38)
                    prepare(1, 1, 0)
                    prepare(2, 1, 0)
                    for e in range(3):
                        weights_lo(e)
                    for slot in (9, 10, 11):
                        prepare(slot, 1, 0, first=True)
                    for e in range(3, AHEAD):
                        weights_lo(e)

                walk(dve, prepare_first, group)

            @block.gpsimd
            def _(pool):
                def split_h(k, n, b):
                    pool.wait_ge(mh_done, KD * n + k + 1)
                    pool.wait_ge(mhh_done, KD * n + k + 1)
                    pool.tensor_tensor(hl[b][:, k, :], hT[:, k, :], hh[b][:, k, :].bitcast(F32),
                                       ALU.subtract).then_inc(mhl_done, 1)

                def prepare(slot, n, b):
                    if slot == 1:
                        pool.wait_ge(ln, 3 * n + 3)
                        pool.tensor_tensor(rs[:, :], rs[:, :], minus_half[:, :], ALU.pow).then_inc(mroot, 1)
                    if slot in (4, 6):
                        split_h(slot // 2 - 2, n, b)

                def lo(e, n):
                    s = n * ALL + e
                    pool.wait_ge(fh_done, s + 1)
                    pool.wait_ge(down_ps, 2 * (s - 1) if e >= 2 else 2 * n * ALL)
                    pool.tensor_tensor(fl[e % 2][:, :], ff[e % 2][:, :], fh[e % 2][:, :].bitcast(F32),
                                       ALU.subtract).then_inc(fl_done, 1)

                def residual(n):
                    pool.wait_ge(scaled, n + 1)
                    pool.wait_ge(res_in, 16 * (n + 1))
                    pool.tensor_tensor(yo[:, :, :], yo[:, :, :], xres[:, :, :], ALU.add).then_inc(yo_done2, 1)

                def group(n, b, j, first=False, last=False):
                    for e in range(ALL):
                        lo(e, n)
                        if e == 1 and not first:
                            residual(n - 1)
                        if not last:
                            prepare(e, n + 1, 1 - b)
                    if last:
                        residual(n)

                def prepare_first():
                    for slot in range(ALL):
                        prepare(slot, 1, 0)

                walk(pool, prepare_first, group)


def host_layout(inputs):
    a = {k.replace("L0_attn_", "").replace("L0_ffn_", "").replace("L0_", ""): np.asarray(v) for k, v in inputs.items()}

    def slices(w):
        return w.reshape(-1, P, w.shape[-1]).transpose(1, 0, 2)

    def columns(v):
        return v.reshape(-1, P).T

    def everywhere(v, *shape):
        return np.broadcast_to(v, (P, *shape))

    def expert(w13, w2):
        return np.concatenate([slices(w13.T).reshape(P, KD * 2 * INTER), w2.T], axis=1)

    r = np.arange(P)
    out = {
        "x": a["x"].reshape(NB, STEPS, CH, P, D).transpose(0, 1, 3, 2, 4),
        "c_col": a["c"].T.reshape(KD, P, NB).transpose(1, 0, 2),
        "wmod": slices(a["wmod"]),
        "ln_wb": everywhere(np.stack([a["ln_w"], a["ln_b"]]), 2, D),
        "W_in": slices(a["W_in"]),
        "W_dt": slices(a["W_in"][:, -H:]),
        "W_out": slices(a["W_out"]).reshape(P, KI * D),
        "glu_w": slices(a["glu_w"]).reshape(P, KD * 2 * D),
        "rms_w": columns(a["rms_w"]),
        "conv_w": a["conv_w"].reshape(MC, P, TAPS).transpose(1, 0, 2),
        "conv_b": columns(a["conv_b"]),
        "dt_bias": everywhere(a["dt_bias"], CH, H),
        "A_log": everywhere(a["A_log"], CH, H),
        "D_skip": everywhere(np.repeat(a["D_skip"], HD), DI),
        "glu_b": columns(a["glu_b"]),
        "gate_w": slices(a["gate_w"].T),
        "gate_b": everywhere(a["gate_b"], MT, NE),
        "experts": np.stack([expert(a["w13"][e], a["w2"][e]) for e in range(NE)] + [expert(a["w13_s"], a["w2_s"])]),
        "ident": np.eye(P, dtype=np.float32),
        "upto": (r[:, None] <= r[None, :]).astype(np.float32),
        "after": (r[:, None] > r[None, :]).astype(np.float32),
        "ones": np.ones((P, P), np.float32),
    }
    return {k: np.ascontiguousarray(v) for k, v in out.items()}


def kernel(**inputs):
    import concourse.bacc as _bacc
    from concourse.bass_utils import run_bass_kernel_spmd as _run

    nc = _bacc.Bacc("TRN2", target_bir_lowering=False, num_devices=1)
    arrays, t = {}, {}
    for name, a in host_layout(inputs).items():
        arrays[f"in_{name}"] = a
        t[name] = nc.dram_tensor(f"in_{name}", a.shape, mybir.dt.from_np(a.dtype), kind="ExternalInput").ap()
    x2_dram = nc.dram_tensor("x2_dram", (NB, STEPS, P, CH, D), F32, kind="Internal").ap()
    out = nc.dram_tensor("out", (NB, SEQ, D), F32, kind="ExternalOutput").ap()
    build(nc, t, x2_dram, out)
    r = _run(nc, [arrays], core_ids=[0])
    return r.results[0]["out"]
```
